# Optimizing a Trainium2 kernel written in Bass

```python
import numpy as np
import jax
import jax.numpy as jnp

def _softmax(x, axis=-1):
    return jax.nn.softmax(x, axis=axis)

def _gelu(x):
    return jax.nn.gelu(x, approximate=True)

def _silu(x):
    return jax.nn.silu(x)

def _sigmoid(x):
    return jax.nn.sigmoid(x)

def _layernorm(x, axis=-1, eps=1e-05):
    m = jnp.mean(x, axis=axis, keepdims=True)
    v = jnp.var(x, axis=axis, keepdims=True)
    return (x - m) / jnp.sqrt(v + eps)

def _scatter_add(tgt, idx, src, axis=0):
    return tgt.at[idx].add(src)

def _segment_sum(src, seg, n):
    return jax.ops.segment_sum(src, seg, n)
kernel_name = 'mk_vit_tower_d1_tok_img256_r4_a4190f'

def setup_inputs(seed: int=0):
    np.random.seed(seed)
    _w = jnp.asarray

    def _rec_inputs():
        import jax
        import jax.numpy as jnp
        _rk = jax.random.key(seed)
        x = -0.000596345 + 1.00056 * jax.random.normal(jax.random.fold_in(_rk, 1), (128, 64, 64, 3), jnp.float32)
        return x
    x = _rec_inputs()

    def _L0_tok_setup():
        import jax, jax.numpy as jnp
        import numpy as np
        B, H, W = (16, 64, 64)
        WIDTH, LAYERS, M1, M2 = (32, 4, 12, 12)
        EPS = 1e-05

        def layer_norm(x, g, b):
            mu = jnp.mean(x, axis=-1, keepdims=True)
            var = jnp.mean((x - mu) ** 2, axis=-1, keepdims=True)
            return (x - mu) * jax.lax.rsqrt(var + EPS) * g + b

        def gelu(x):
            return jax.nn.gelu(x, approximate=False)

        def spectral_conv(x, w1, w2):
            b, c, h, w = x.shape
            x_ft = jnp.fft.rfft2(x)
            out_ft = jnp.zeros((b, w1.shape[1], h, w // 2 + 1), dtype=x_ft.dtype)
            out_ft = out_ft.at[:, :, :M1, :M2].set(jnp.einsum('bixy,ioxy->boxy', x_ft[:, :, :M1, :M2], w1))
            out_ft = out_ft.at[:, :, -M1:, :M2].set(jnp.einsum('bixy,ioxy->boxy', x_ft[:, :, -M1:, :M2], w2))
            return jnp.fft.irfft2(out_ft, s=(h, w))
        key = jax.random.key(seed)
        ks = jax.random.split(key, 16)
        scale = 1.0 / (WIDTH * WIDTH)
        d = {'x': jax.random.normal(ks[0], (B, H, W, 3), jnp.float32), 'fc0_w': jax.random.normal(ks[1], (3, WIDTH), jnp.float32) * 0.5, 'fc0_b': jnp.zeros((WIDTH,), jnp.float32), 'ln0_g': jnp.ones((WIDTH,), jnp.float32), 'ln0_b': jnp.zeros((WIDTH,), jnp.float32), 'w1r': jax.random.uniform(ks[2], (LAYERS, WIDTH, WIDTH, M1, M2), jnp.float32) * scale, 'w1i': jax.random.uniform(ks[3], (LAYERS, WIDTH, WIDTH, M1, M2), jnp.float32) * scale, 'w2r': jax.random.uniform(ks[4], (LAYERS, WIDTH, WIDTH, M1, M2), jnp.float32) * scale, 'w2i': jax.random.uniform(ks[5], (LAYERS, WIDTH, WIDTH, M1, M2), jnp.float32) * scale, 'conv_w': jax.random.normal(ks[6], (LAYERS, WIDTH, WIDTH), jnp.float32) * (1.0 / np.sqrt(WIDTH)), 'conv_b': jnp.zeros((LAYERS, WIDTH), jnp.float32), 'ln_g': jnp.ones((LAYERS, WIDTH), jnp.float32), 'ln_b': jnp.zeros((LAYERS, WIDTH), jnp.float32), 'fc1_w': jax.random.normal(ks[7], (WIDTH, 128), jnp.float32) * (1.0 / np.sqrt(WIDTH)), 'fc1_b': jnp.zeros((128,), jnp.float32), 'fc2_w': jax.random.normal(ks[8], (128, 64), jnp.float32) * (1.0 / np.sqrt(128)), 'fc2_b': jnp.zeros((64,), jnp.float32), 'fc3_w': jax.random.normal(ks[9], (64, 1), jnp.float32) * (1.0 / np.sqrt(64)), 'fc3_b': jnp.zeros((1,), jnp.float32)}
        return d
    _L0_tok_all = _L0_tok_setup()
    _L0_tok_in = {k: v for k, v in _L0_tok_all.items() if k in ('fc0_w', 'fc0_b', 'ln0_g', 'ln0_b', 'w1r', 'w1i', 'w2r', 'w2i', 'conv_w', 'conv_b', 'ln_g', 'ln_b', 'fc1_w', 'fc1_b', 'fc2_w', 'fc2_b', 'fc3_w', 'fc3_b')}
    del _L0_tok_all

    def _L0_attn_setup():
        import math
        import jax, jax.numpy as jnp
        import numpy as np
        D_MODEL = 64
        N_HEADS = 4
        HEAD_DIM = D_MODEL // N_HEADS
        MAX_REL = 30

        def _rel_pos_encodings(t, d_model):
            n = 2 * MAX_REL + 1
            positions = jnp.arange(n, dtype=jnp.float32)[:, None]
            div_term = jnp.exp(jnp.arange(0, d_model, 2, dtype=jnp.float32) * (-math.log(10000.0) / d_model))
            ang = positions * div_term
            enc = jnp.stack([jnp.sin(ang), jnp.cos(ang)], axis=-1).reshape(n, d_model)
            rng = jnp.arange(t)
            final_mat = jnp.clip(rng[None, :] - rng[:, None], -MAX_REL, MAX_REL) + MAX_REL
            return enc[final_mat]
        key = jax.random.key(seed)
        ks = jax.random.split(key, 12)
        d = D_MODEL
        s = 1.0 / math.sqrt(d)
        inp = {'inputs': jax.random.normal(ks[0], (16, 128, d), dtype=jnp.float32), 'ln_gamma': jnp.ones((d,), jnp.float32), 'ln_beta': jnp.zeros((d,), jnp.float32), 'Wq': jax.random.normal(ks[1], (d, d), jnp.float32) * s, 'bq': jnp.zeros((d,), jnp.float32), 'Wk': jax.random.normal(ks[2], (d, d), jnp.float32) * s, 'bk': jnp.zeros((d,), jnp.float32), 'Wv': jax.random.normal(ks[3], (d, d), jnp.float32) * s, 'bv': jnp.zeros((d,), jnp.float32), 'Wpos': jax.random.normal(ks[4], (d, d), jnp.float32) * s, 'bpos': jnp.zeros((d,), jnp.float32), 'Wo': jax.random.normal(ks[5], (d, d), jnp.float32) * s, 'bo': jnp.zeros((d,), jnp.float32), 'u_bias': jax.random.normal(ks[6], (1, N_HEADS, 1, HEAD_DIM), jnp.float32) * 0.02, 'v_bias': jax.random.normal(ks[7], (1, N_HEADS, 1, HEAD_DIM), jnp.float32) * 0.02}
        return inp
    _L0_attn_all = _L0_attn_setup()
    _L0_attn_in = {k: v for k, v in _L0_attn_all.items() if k in ('ln_gamma', 'ln_beta', 'Wq', 'bq', 'Wk', 'bk', 'Wv', 'bv', 'Wpos', 'bpos', 'Wo', 'bo', 'u_bias', 'v_bias')}
    del _L0_attn_all

    def _L0_ffn_setup():
        import jax, jax.numpy as jnp
        import numpy as np
        B, S, D = (8, 1024, 64)
        H = 4 * D
        CAPACITY = 0.5
        key = jax.random.key(seed)
        ks = jax.random.split(key, 6)
        x = jax.random.normal(ks[0], (B, S, D), dtype=jnp.float32)
        attention_mask = jnp.zeros((B, 1, 1, S), dtype=jnp.float32)
        wr = jax.random.normal(ks[1], (D, 1), dtype=jnp.float32) * 0.02
        br = jnp.zeros((1,), dtype=jnp.float32)
        w1 = jax.random.normal(ks[2], (D, H), dtype=jnp.float32) * 0.02
        b1 = jnp.zeros((H,), dtype=jnp.float32)
        w2 = jax.random.normal(ks[3], (H, D), dtype=jnp.float32) * 0.02
        b2 = jnp.zeros((D,), dtype=jnp.float32)
        return {'x': x, 'attention_mask': attention_mask, 'wr': wr, 'br': br, 'w1': w1, 'b1': b1, 'w2': w2, 'b2': b2}
    _L0_ffn_all = _L0_ffn_setup()
    _L0_ffn_in = {k: v for k, v in _L0_ffn_all.items() if k in ('attention_mask', 'wr', 'br', 'w1', 'b1', 'w2', 'b2')}
    del _L0_ffn_all
    return {'x': x, 'L0_tok_fc0_w': _L0_tok_in['fc0_w'], 'L0_tok_fc0_b': _L0_tok_in['fc0_b'], 'L0_tok_ln0_g': _L0_tok_in['ln0_g'], 'L0_tok_ln0_b': _L0_tok_in['ln0_b'], 'L0_tok_w1r': _L0_tok_in['w1r'], 'L0_tok_w1i': _L0_tok_in['w1i'], 'L0_tok_w2r': _L0_tok_in['w2r'], 'L0_tok_w2i': _L0_tok_in['w2i'], 'L0_tok_conv_w': _L0_tok_in['conv_w'], 'L0_tok_conv_b': _L0_tok_in['conv_b'], 'L0_tok_ln_g': _L0_tok_in['ln_g'], 'L0_tok_ln_b': _L0_tok_in['ln_b'], 'L0_tok_fc1_w': _L0_tok_in['fc1_w'], 'L0_tok_fc1_b': _L0_tok_in['fc1_b'], 'L0_tok_fc2_w': _L0_tok_in['fc2_w'], 'L0_tok_fc2_b': _L0_tok_in['fc2_b'], 'L0_tok_fc3_w': _L0_tok_in['fc3_w'], 'L0_tok_fc3_b': _L0_tok_in['fc3_b'], 'L0_attn_ln_gamma': _L0_attn_in['ln_gamma'], 'L0_attn_ln_beta': _L0_attn_in['ln_beta'], 'L0_attn_Wq': _L0_attn_in['Wq'], 'L0_attn_bq': _L0_attn_in['bq'], 'L0_attn_Wk': _L0_attn_in['Wk'], 'L0_attn_bk': _L0_attn_in['bk'], 'L0_attn_Wv': _L0_attn_in['Wv'], 'L0_attn_bv': _L0_attn_in['bv'], 'L0_attn_Wpos': _L0_attn_in['Wpos'], 'L0_attn_bpos': _L0_attn_in['bpos'], 'L0_attn_Wo': _L0_attn_in['Wo'], 'L0_attn_bo': _L0_attn_in['bo'], 'L0_attn_u_bias': _L0_attn_in['u_bias'], 'L0_attn_v_bias': _L0_attn_in['v_bias'], 'L0_ffn_attention_mask': _L0_ffn_in['attention_mask'], 'L0_ffn_wr': _L0_ffn_in['wr'], 'L0_ffn_br': _L0_ffn_in['br'], 'L0_ffn_w1': _L0_ffn_in['w1'], 'L0_ffn_b1': _L0_ffn_in['b1'], 'L0_ffn_w2': _L0_ffn_in['w2'], 'L0_ffn_b2': _L0_ffn_in['b2']}

def reference(x, L0_tok_fc0_w, L0_tok_fc0_b, L0_tok_ln0_g, L0_tok_ln0_b, L0_tok_w1r, L0_tok_w1i, L0_tok_w2r, L0_tok_w2i, L0_tok_conv_w, L0_tok_conv_b, L0_tok_ln_g, L0_tok_ln_b, L0_tok_fc1_w, L0_tok_fc1_b, L0_tok_fc2_w, L0_tok_fc2_b, L0_tok_fc3_w, L0_tok_fc3_b, L0_attn_ln_gamma, L0_attn_ln_beta, L0_attn_Wq, L0_attn_bq, L0_attn_Wk, L0_attn_bk, L0_attn_Wv, L0_attn_bv, L0_attn_Wpos, L0_attn_bpos, L0_attn_Wo, L0_attn_bo, L0_attn_u_bias, L0_attn_v_bias, L0_ffn_attention_mask, L0_ffn_wr, L0_ffn_br, L0_ffn_w1, L0_ffn_b1, L0_ffn_w2, L0_ffn_b2):
    import jax
    import jax.numpy as jnp

    def _L0_tok_ref(x, fc0_w, fc0_b, ln0_g, ln0_b, w1r, w1i, w2r, w2i, conv_w, conv_b, ln_g, ln_b, fc1_w, fc1_b, fc2_w, fc2_b, fc3_w, fc3_b):
        import jax, jax.numpy as jnp
        import numpy as np
        B, H, W = (16, 64, 64)
        WIDTH, LAYERS, M1, M2 = (32, 4, 12, 12)
        EPS = 1e-05

        def layer_norm(x, g, b):
            mu = jnp.mean(x, axis=-1, keepdims=True)
            var = jnp.mean((x - mu) ** 2, axis=-1, keepdims=True)
            return (x - mu) * jax.lax.rsqrt(var + EPS) * g + b

        def gelu(x):
            return jax.nn.gelu(x, approximate=False)

        def spectral_conv(x, w1, w2):
            b, c, h, w = x.shape
            x_ft = jnp.fft.rfft2(x)
            out_ft = jnp.zeros((b, w1.shape[1], h, w // 2 + 1), dtype=x_ft.dtype)
            out_ft = out_ft.at[:, :, :M1, :M2].set(jnp.einsum('bixy,ioxy->boxy', x_ft[:, :, :M1, :M2], w1))
            out_ft = out_ft.at[:, :, -M1:, :M2].set(jnp.einsum('bixy,ioxy->boxy', x_ft[:, :, -M1:, :M2], w2))
            return jnp.fft.irfft2(out_ft, s=(h, w))
        h = layer_norm(x @ fc0_w + fc0_b, ln0_g, ln0_b)
        h = jnp.transpose(h, (0, 3, 1, 2))
        for i in range(LAYERS):
            w1 = w1r[i] + 1j * w1i[i]
            w2 = w2r[i] + 1j * w2i[i]
            x1 = spectral_conv(h, w1, w2)
            x2 = jnp.einsum('bchw,oc->bohw', h, conv_w[i]) + conv_b[i][None, :, None, None]
            h = x1 + x2
            h = jnp.transpose(h, (0, 2, 3, 1))
            h = layer_norm(h, ln_g[i], ln_b[i])
            if i < LAYERS - 1:
                h = gelu(h)
            h = jnp.transpose(h, (0, 3, 1, 2))
        h = jnp.transpose(h, (0, 2, 3, 1))
        h = gelu(h @ fc1_w + fc1_b)
        h = gelu(h @ fc2_w + fc2_b)
        h = h @ fc3_w + fc3_b
        return h[..., 0]

    def _L0_attn_ref(inputs, ln_gamma, ln_beta, Wq, bq, Wk, bk, Wv, bv, Wpos, bpos, Wo, bo, u_bias, v_bias):
        import math
        import jax, jax.numpy as jnp
        import numpy as np
        D_MODEL = 64
        N_HEADS = 4
        HEAD_DIM = D_MODEL // N_HEADS
        MAX_REL = 30

        def _rel_pos_encodings(t, d_model):
            n = 2 * MAX_REL + 1
            positions = jnp.arange(n, dtype=jnp.float32)[:, None]
            div_term = jnp.exp(jnp.arange(0, d_model, 2, dtype=jnp.float32) * (-math.log(10000.0) / d_model))
            ang = positions * div_term
            enc = jnp.stack([jnp.sin(ang), jnp.cos(ang)], axis=-1).reshape(n, d_model)
            rng = jnp.arange(t)
            final_mat = jnp.clip(rng[None, :] - rng[:, None], -MAX_REL, MAX_REL) + MAX_REL
            return enc[final_mat]
        b, t, d = inputs.shape
        h, hd = (N_HEADS, HEAD_DIM)
        mu = jnp.mean(inputs, axis=-1, keepdims=True)
        var = jnp.mean(jnp.square(inputs - mu), axis=-1, keepdims=True)
        x = (inputs - mu) * jax.lax.rsqrt(var + 1e-05) * ln_gamma + ln_beta

        def split_heads(y):
            return y.reshape(b, t, h, hd).transpose(0, 2, 1, 3)
        q = split_heads(x @ Wq.T + bq)
        k = split_heads(x @ Wk.T + bk)
        v = split_heads(x @ Wv.T + bv)
        rel = jax.lax.stop_gradient(_rel_pos_encodings(t, d))
        pos = (rel @ Wpos.T + bpos).reshape(t, t, h, hd)
        qk_score = jnp.einsum('bhtd,bhsd->bhts', q + u_bias, k)
        pos_score = jnp.einsum('bhtd,tshd->bhts', q + v_bias, pos)
        scores = (qk_score + pos_score) / math.sqrt(hd)
        attn = jax.nn.softmax(scores, axis=-1)
        ctx = jnp.einsum('bhts,bhsd->bhtd', attn, v)
        ctx = ctx.transpose(0, 2, 1, 3).reshape(b, t, d)
        return ctx @ Wo.T + bo

    def _L0_ffn_ref(x, attention_mask, wr, br, w1, b1, w2, b2):
        import jax, jax.numpy as jnp
        import numpy as np
        B, S, D = (8, 1024, 64)
        H = 4 * D
        CAPACITY = 0.5
        b, s, d = x.shape
        weights = (jnp.einsum('bsd,do->bso', x, wr) + br)[..., 0]
        k = max(1, int(CAPACITY * s))
        kk = k - 1 if k > 1 else 1
        _, idx = jax.lax.top_k(weights, k)
        sel_idx = idx[:, :kk]
        sel = jnp.take_along_axis(x, sel_idx[:, :, None], axis=1)
        h = jax.nn.gelu(jnp.einsum('bkd,dh->bkh', sel, w1) + b1)
        y = jnp.einsum('bkh,hd->bkd', h, w2) + b2
        w_sel = jnp.take_along_axis(weights, sel_idx, axis=1)
        y = y * w_sel[..., None]
        batch_idx = jnp.arange(b)[:, None]
        processed = jnp.zeros_like(x).at[batch_idx, sel_idx].set(y)
        return processed + x
    h = _L0_tok_ref(x, L0_tok_fc0_w, L0_tok_fc0_b, L0_tok_ln0_g, L0_tok_ln0_b, L0_tok_w1r, L0_tok_w1i, L0_tok_w2r, L0_tok_w2i, L0_tok_conv_w, L0_tok_conv_b, L0_tok_ln_g, L0_tok_ln_b, L0_tok_fc1_w, L0_tok_fc1_b, L0_tok_fc2_w, L0_tok_fc2_b, L0_tok_fc3_w, L0_tok_fc3_b)
    h = h + _L0_attn_ref(_layernorm(h, axis=-1), L0_attn_ln_gamma, L0_attn_ln_beta, L0_attn_Wq, L0_attn_bq, L0_attn_Wk, L0_attn_bk, L0_attn_Wv, L0_attn_bv, L0_attn_Wpos, L0_attn_bpos, L0_attn_Wo, L0_attn_bo, L0_attn_u_bias, L0_attn_v_bias)
    h = h + _L0_ffn_ref(_layernorm(h, axis=-1), L0_ffn_attention_mask, L0_ffn_wr, L0_ffn_br, L0_ffn_w1, L0_ffn_b1, L0_ffn_w2, L0_ffn_b2)
    return h

_drawn_inputs = setup_inputs


def setup_inputs(seed=0):
    import zlib

    import numpy as np

    out = dict(_drawn_inputs(seed))
    spreads = {'L0_tok_fc0_b': (0.0, 0.1),
     'L0_tok_ln0_g': (1.0, 0.2),
     'L0_tok_ln0_b': (0.0, 0.1),
     'L0_tok_conv_b': (0.0, 0.1),
     'L0_tok_ln_g': (1.0, 0.2),
     'L0_tok_ln_b': (0.0, 0.1),
     'L0_tok_fc1_b': (0.0, 0.1),
     'L0_tok_fc2_b': (0.0, 0.1),
     'L0_attn_ln_gamma': (1.0, 0.2),
     'L0_attn_ln_beta': (0.0, 0.1),
     'L0_attn_bq': (0.0, 0.1),
     'L0_attn_bk': (0.0, 2.0),
     'L0_attn_bv': (0.0, 0.1),
     'L0_attn_bpos': (0.0, 2.0),
     'L0_attn_bo': (0.0, 0.1),
     'L0_ffn_b1': (0.0, 0.8),
     'L0_ffn_b2': (0.0, 0.8)}
    factors = {'L0_tok_w1r': 8.0,
     'L0_tok_w1i': 8.0,
     'L0_tok_w2r': 22.274,
     'L0_tok_w2i': 8.0,
     'L0_attn_u_bias': 5.255,
     'L0_attn_v_bias': 8.0,
     'L0_ffn_wr': 8.0,
     'L0_ffn_w1': 8.0,
     'L0_ffn_w2': 8.0}
    for name, (base, spread) in spreads.items():
        noise = np.random.default_rng([zlib.crc32(name.encode()), seed]).standard_normal(out[name].shape)
        drawn = base * np.exp(spread * noise) if base else spread * noise
        out[name] = jnp.asarray(drawn.astype(out[name].dtype))
    for name, factor in factors.items():
        out[name] = (out[name] * factor).astype(out[name].dtype)
    return out
```

```python
from contextlib import ExitStack

import numpy as np

import concourse.bass as bass
from concourse import mybir

F32 = mybir.dt.float32
BF16 = mybir.dt.bfloat16
ALU = mybir.AluOpType
ACT = mybir.ActivationFunctionType
AX_X = mybir.AxisListType.X

P = 128
NIMG = 128
S = 64
PIX = S * S
C = 32
IG = P // C
G = 4
BI = G * IG
LAYERS = 4
M1 = M2 = 12
MODES = M1 * M2
HR = 4
XM = HR * MODES
NORMS = LAYERS + 1
HID1, HID2 = 128, 64
EPS = 1e-5
CH = 512
NCH = PIX // CH
NXP = PIX // P
RO = 8
PARTS = 3


def wait_alone(engine, semaphore, value, passed):
    engine.wait_ge(semaphore, value)
    engine.sem_inc(passed, 1)


def constants():
    f8 = np.float64
    kx = np.concatenate([np.arange(M1), np.arange(-M1, 0)]).reshape(2, M1)
    x = np.arange(S)
    th_x = 2 * np.pi * (kx[:, :, None] * x[None, None, :]) / S
    th_y = 2 * np.pi * np.outer(np.arange(M2), x) / S
    cosx, sinx, cosy, siny = np.cos(th_x), np.sin(th_x), np.cos(th_y), np.sin(th_y)
    two = np.eye(2)
    dft_y = np.zeros((2, S, 2, M2, 2), f8)
    for a in range(2):
        dft_y[a, :, a, :, 0] = cosy.T
        dft_y[a, :, a, :, 1] = -siny.T
    dft_x = np.zeros((S, 2, 2, 2, M1), f8)
    for h in range(2):
        c, s = cosx[h].T, sinx[h].T
        dft_x[:, 0, h, 0], dft_x[:, 1, h, 0] = c, s
        dft_x[:, 0, h, 1], dft_x[:, 1, h, 1] = -s, c
    idft_x = np.zeros((2, 2, M1, 2, S, 2, 2), f8)
    for h in range(2):
        for k in range(2):
            c, s = cosx[h], sinx[h]
            idft_x[h, 0, :, k, :, k, 0], idft_x[h, 1, :, k, :, k, 0] = c, -s
            idft_x[h, 0, :, k, :, k, 1], idft_x[h, 1, :, k, :, k, 1] = s, c
    w = np.where(np.arange(M2) == 0, 1.0, 2.0)[:, None] / PIX
    idft_y = np.zeros((4, M2, 2, 4, S), f8)
    for a in range(4):
        idft_y[a, :, 0, a] = w * cosy
        idft_y[a, :, 1, a] = -w * siny
    blk = np.kron(np.eye(IG), np.ones((C, 1)))
    centre = np.kron(np.eye(IG), np.eye(C) - 1.0 / C)
    ones_v = blk[:, np.arange(32) % IG] / C
    sel = np.zeros((4, 32, 4, IG, C))
    for q in range(4):
        for n in range(PARTS * IG):
            sel[q, n, q, n % IG, :] = 1
    row = np.arange(P) % 32
    minus = np.stack([-(row >= IG).astype(f8) * (row < 3 * IG), -((row >= 2 * IG) & (row < 3 * IG)).astype(f8)], 1)
    fmask = np.zeros((IG, RO, 3, RO, IG))
    for i in range(IG):
        for r in range(RO):
            fmask[i, r, :, r, i] = 1
    mask2 = np.zeros((2, HID2, 32))
    for i in range(2):
        mask2[i, :, i] = 1
    out = dict(k_ident=np.eye(P), k_dft_y=dft_y.reshape(P, 48), k_dft_x=dft_x.reshape(P, 48),
               k_idft_x=idft_x.reshape(96, 256), k_idft_y=idft_y.reshape(96, 256), k_blk=blk, k_centre=centre,
               k_ones_v=ones_v, k_sel=sel.reshape(P, 4 * P), k_minus=minus, k_fmask=fmask.reshape(96, RO * IG),
               k_mask2=mask2.reshape(P, 32))
    return {k: np.ascontiguousarray(v, np.float32) for k, v in out.items()}


def tokenizer(nc, ctx, a, tokens, batches):
    def sb(name, shape, dt=F32):
        return ctx.enter_context(nc.sbuf_tensor(name, shape, dt))

    def sem(name):
        return ctx.enter_context(nc.semaphore(name))

    bank = [ctx.enter_context(nc.psum_tensor(f"bank{i}", [P, 2, CH], F32)) for i in range(4)]

    def bk(n):
        return bank[n // 2][:, n % 2, :]

    h = sb("h", [P, G, PIX])
    mix_w = sb("mix_w", [P, 2, C, MODES])
    xm = sb("xm", [P, BI, MODES])
    ym = sb("ym", [P, BI, MODES])
    th = sb("th", [P, 2, CH])
    ya = sb("ya", [P, M2, S, 2])
    xa = sb("xa", [P, M2, P])
    xg = sb("xg", [P, HR, M1, M2])
    yg = sb("yg", [P, 2, HR * M1, M2])
    yr = sb("yr", [P, M2 // 2, HR * M1, 2])
    yt = sb("yt", [96, M2 // 2, P])
    zx = sb("zx", [P, S, M2 * 2])
    zt = sb("zt", [96, S // 4, P])
    sq = sb("sq", [P, 2, 2 * CH])
    rstd = sb("rstd", [P, 2, CH])
    newt = sb("newt", [P, 2, CH])
    part = sb("part", [P, 2, CH], BF16)
    r3 = sb("r3", [P, 2, CH], BF16)
    xin = sb("xin", [P, G, IG, 32 * 3])
    xr = sb("xr", [P, 4, IG, 3 * RO])
    xt = sb("xt", [96, 4, P])
    g1, g2 = sq, th
    tok = zx[:].rearrange("p a b -> p (a b)")[:, 0:2 * CH].rearrange("p (a b) -> p a b", a=2)
    ident = sb("ident", [P, P])
    dft_y, dft_x = sb("dft_y", [P, 48]), sb("dft_x", [P, 48])
    idft_x, idft_y = sb("idft_x", [96, 256]), sb("idft_y", [96, 256])
    blk, centre = sb("blk", [P, IG]), sb("centre", [P, P])
    ones_v, minus = sb("ones_v", [P, 32]), sb("minus", [P, 2])
    selb = sb("selb", [P, 4, P], BF16)
    f0, f1, f2 = sb("f0", [96, RO, P]), sb("f1", [P, IG, HID1]), sb("f2", [P, HID2])
    f3 = sb("f3", [P, 32])
    conv = sb("conv", [P, LAYERS, P])
    cb = sb("cb", [P, NORMS])
    gam, bet = sb("gam", [P, NORMS]), sb("bet", [P, NORMS])
    b1, b2, b3 = sb("b1", [P, 1]), sb("b2", [P, 1]), sb("b3", [P, 1])
    epst = sb("epst", [P, 1])
    conv_l = sb("conv_l", [P, P])
    cb_l = sb("cb_l", [P, 3])
    zf = zx[:].rearrange("p a b -> p (a b)")
    sel_f, fmask, mask2 = zf[:, 0:512], zf[0:96, 512:544], zf[:, 544:576]
    f0_rep, f1_rep, conv_rep = zf[0:96, 576:608], zf[:, 608:736], zf[:, 736:864]
    cb_raw, f3_rep, f0_sum = zf[:, 864:869], zf[:, 869:870], zf[0:96, 870:871]
    conv_bd = xa[:, 0:LAYERS, :]

    scr_x = a["scr_x"]
    scr_y = a["scr_y"]

    setup_in, setup_v, setup_mm = sem("setup_in"), sem("setup_v"), sem("setup_mm")
    pe_passed = sem("pe_passed")
    setup_g, eps_set, conv_in = sem("setup_g"), sem("eps_set"), sem("conv_in")
    x_in = sem("x_in")
    xr_cp, yr_cp = sem("xr_cp"), sem("yr_cp")
    xt_mm, xt_cp = sem("xt_mm"), sem("xt_cp")
    t_mm, t_cp, a_mm, a_cp = sem("t_mm"), sem("t_cp"), sem("a_mm"), sem("a_cp")
    t2_mm, t2_cp, b_mm, b_cp = sem("t2_mm"), sem("t2_cp"), sem("b_mm"), sem("b_cp")
    xg_out, xm_in, w_in, w_neg = sem("xg_out"), sem("xm_in"), sem("w_in"), sem("w_neg")
    mix_mm, mix_v, mix_a = sem("mix_mm"), sem("mix_v"), sem("mix_a")
    ym_out, yg_in = sem("ym_out"), [sem("yg_in0"), sem("yg_in1")]
    yt_mm, yt_cp, d_mm, d_cp = sem("yt_mm"), sem("yt_cp"), sem("d_mm"), sem("d_cp")
    zt_mm, zt_cp = sem("zt_mm"), sem("zt_cp")
    y_mm, y_cp, sq_done, var_mm = sem("y_mm"), sem("y_cp"), sem("sq_done"), sem("var_mm")
    rs_done, st_done, bc_mm, z_done, h_done = (sem("rs_done"), sem("st_done"), sem("bc_mm"), sem("z_done"),
                                               sem("h_done"))
    m1_mm, m1_done, m2_mm, m2_done = sem("m1_mm"), sem("m1_done"), sem("m2_mm"), sem("m2_done")
    m3_mm, m3_cp, tok_out = sem("m3_mm"), sem("m3_cp"), sem("tok_out")

    NT, NA, NT2, NB = NCH, 4, 3, 2
    NMIX, MC = 6, MODES // 6
    NY, ND, NZ = 2, 3, 4
    NST = 8
    NM = 2 * NCH

    block = ctx.enter_context(nc.Block())

    @block.sync
    def _(sp):
        consts = [(ident, "k_ident"), (dft_y, "k_dft_y"), (dft_x, "k_dft_x"), (idft_x, "k_idft_x"),
                  (idft_y, "k_idft_y"), (blk, "k_blk"), (centre, "k_centre"), (ones_v, "k_ones_v"),
                  (minus, "k_minus")]
        for t, n in consts:
            sp.dma_start(t[:], a[n]).then_inc(setup_in, 16)
        views = [(sel_f, a["k_sel"]), (fmask, a["k_fmask"]), (mask2, a["k_mask2"]), (f2[:], a["L0_tok_fc2_w"])]
        for t, v in views:
            sp.dma_start(t, v).then_inc(setup_in, 16)
        col = lambda v: v.rearrange("(c o) -> c o", o=1)
        with nc.allow_non_contiguous_dma(reason="a few small weights"):
            for i in range(IG):
                rows = slice(C * i, C * (i + 1))
                sp.dma_start(f1_rep[rows, :], a["L0_tok_fc1_w"]).then_inc(setup_in, 16)
                sp.dma_start(conv_rep[rows, :].rearrange("o (l c) -> o l c", l=LAYERS),
                             a["L0_tok_conv_w"].rearrange("l o c -> o l c")).then_inc(setup_in, 16)
                sp.dma_start(cb_raw[rows, 0:1], col(a["L0_tok_fc0_b"])).then_inc(setup_in, 16)
                sp.dma_start(cb_raw[rows, 1:NORMS], a["L0_tok_conv_b"].rearrange("l c -> c l")).then_inc(setup_in, 16)
                sp.dma_start(gam[rows, 0:1], col(a["L0_tok_ln0_g"])).then_inc(setup_in, 16)
                sp.dma_start(bet[rows, 0:1], col(a["L0_tok_ln0_b"])).then_inc(setup_in, 16)
                sp.dma_start(gam[rows, 1:NORMS], a["L0_tok_ln_g"].rearrange("l c -> c l")).then_inc(setup_in, 16)
                sp.dma_start(bet[rows, 1:NORMS], a["L0_tok_ln_b"].rearrange("l c -> c l")).then_inc(setup_in, 16)
            for n in range(IG * RO):
                sp.dma_start(f0_rep[3 * n:3 * n + 3, :], a["L0_tok_fc0_w"]).then_inc(setup_in, 16)
            for i in range(2):
                rows = slice(HID2 * i, HID2 * (i + 1))
                sp.dma_start(f3_rep[rows, :], a["L0_tok_fc3_w"]).then_inc(setup_in, 16)
                sp.dma_start(b2[rows, :], col(a["L0_tok_fc2_b"])).then_inc(setup_in, 16)
            sp.dma_start(b1[:], col(a["L0_tok_fc1_b"])).then_inc(setup_in, 16)
            sp.dma_start(b3[:], a["L0_tok_fc3_b"].rearrange("(a b) -> a b", a=1).broadcast_to([P, 1])
                         ).then_inc(setup_in, 16)

        def load_mix(layer):
            for half, (wr, wi) in enumerate((("L0_tok_w1r", "L0_tok_w1i"), ("L0_tok_w2r", "L0_tok_w2i"))):
                for ri, pair in enumerate(((wr, wi), (wi, wr))):
                    rows = slice(64 * half + 32 * ri, 64 * half + 32 * ri + 32)
                    for ro in range(2):
                        sp.dma_start(mix_w[rows, ro, :, :], a[pair[ro]][layer].rearrange("i o x y -> i o (x y)")
                                     ).then_inc(w_in, 16)

        def layer_dmas(L, it, nxt):
            for g in range(G):
                sp.wait_ge(b_cp, L * (G * NB) + (g + 1) * NB)
                sp.dma_start(scr_x[IG * g:IG * (g + 1)].rearrange("i c m -> (i c) m"),
                             xg[:].rearrange("p a b c -> p (a b c)")).then_inc(xg_out, 16)
                sp.wait_ge(xg_out, L * (G * 16) + (g + 1) * 16)
                for hr in range(HR):
                    sp.dma_start(xm[C * hr:C * (hr + 1), IG * g:IG * (g + 1), :],
                                 scr_x[IG * g:IG * (g + 1), :, MODES * hr:MODES * (hr + 1)]
                                 .rearrange("i c m -> c i m")).then_inc(xm_in, 16)
            sp.wait_ge(mix_v, L * NMIX + NMIX)
            sp.wait_ge(mix_a, L * NMIX + NMIX)
            for hr in range(HR):
                sp.dma_start(scr_y[:, :, MODES * hr:MODES * (hr + 1)].rearrange("i c m -> c i m"),
                             ym[C * hr:C * (hr + 1), :, :]).then_inc(ym_out, 16)
            sp.wait_ge(ym_out, L * (HR * 16) + HR * 16)
            for g in range(G):
                if g >= 2:
                    sp.wait_ge(yr_cp, L * G + g - 1)
                sp.dma_start(yg[:, g % 2, :, :], scr_y[IG * g:IG * (g + 1)].rearrange("i c (n y) -> (i c) n y", y=M2)
                             ).then_inc(yg_in[g % 2], 16)
                if g == 1:
                    load_mix(nxt)

        load_mix(0)
        with sp.Fori(0, batches) as it:
            for g in range(G):
                sp.dma_start(xin[:, g, :, :], a["x"][bass.ds(it * BI + g * IG, IG)]
                             .rearrange("i x y c -> i (x y c)").rearrange("i (q r) -> q i r", q=P)).then_inc(x_in, 16)
            with sp.Fori(0, LAYERS - 1) as l:
                layer_dmas(it * LAYERS + l, it, l + 1)
            layer_dmas(it * LAYERS + LAYERS - 1, it, 0)
            for g in range(G):
                for u in range(2):
                    sp.wait_ge(m3_cp, it * (G * 2) + g * 2 + u + 1)
                    for i in range(2):
                        sp.dma_start(tokens[it * BI + g * IG + 2 * u + i].rearrange("(b q n) -> q b n", b=2, q=4),
                                     tok[i:i + 97:32, :, :]).then_inc(tok_out, 16)
        sp.wait_ge(tok_out, batches * (G * 4) * 16)
        sp.wait_ge(w_in, (batches * LAYERS + 1) * 8 * 16)

    @block.tensor
    def _(pe):
        mm = nc.tensor.matmul
        nset = 13 + 8 * IG + IG * RO + 4 + 2
        pe.wait_ge(setup_in, nset * 16)
        pe.wait_ge(setup_v, 5)
        for layer in range(LAYERS):
            mm(bk(0)[:, P * layer:P * (layer + 1)], conv_bd[:, layer, :], centre[:], start=True, stop=True)
        mm(bk(1)[:, 0:NORMS], centre[:], cb_raw, start=True, stop=True).then_inc(setup_mm, 1)
        pe.wait_ge(setup_v, 7)

        def variance(M, g):
            for k in range(NCH):
                if k % 2 == 0:
                    pe.wait_ge(sq_done, M * (G * 4) + g * 4 + k // 2 + 1)
                q = k % 4
                m = mm(bk(2 + k // 4)[32 * q:32 * q + 32, :], ones_v[:], sq[:, (k // 2) % 2, CH * (k % 2):CH * (k % 2 + 1)],
                       start=True, stop=True)
                if k % 2:
                    m.then_inc(var_mm, 1)

        def spread(M, g):
            pe.wait_ge(st_done, M * (G * NST) + (g + 1) * NST)
            for k in range(NCH):
                if k >= 2:
                    pe.wait_ge(z_done, M * (G * NCH) + g * NCH + k - 1)
                mm(bk(4 + k % 2), selb[:, k % 4, :], r3[:, k // 4, :], start=True, stop=True).then_inc(bc_mm, 1)

        def norm(M, front):
            for g in range(G):
                front(g)
                if g:
                    spread(M, g - 1)
                variance(M, g)
            spread(M, G - 1)

        def layer_body(L, M, layer_conv):
            for g in range(G):
                pe.wait_ge(h_done, M * (G * 2) - G * 2 + (g + 1) * 2)
                for c in range(NT + 1):
                    if c < NT:
                        if c >= 2:
                            pe.wait_ge(t_cp, L * (G * NT) + g * NT + c - 1)
                        for j in range(4):
                            m = pe.transpose(bk(c % 2)[:, P * j:P * (j + 1)], h[:, g, CH * c + P * j:CH * c + P * (j + 1)],
                                             ident[:])
                        m.then_inc(t_mm, 1)
                    if c:
                        b = c - 1
                        pe.wait_ge(t_cp, L * (G * NT) + g * NT + b + 1)
                        if b >= 4 and b % 2 == 0:
                            pe.wait_ge(a_cp, L * (G * NA) + g * NA + b // 2 - 1)
                        for j in range(4):
                            o = 48 * (4 * (b % 2) + j)
                            m = mm(bk(2 + (b // 2) % 2)[:, o:o + 48], th[:, b % 2, P * j:P * (j + 1)], dft_y[:],
                                   start=True, stop=True)
                        if b % 2:
                            m.then_inc(a_mm, 1)
                pe.wait_ge(a_cp, L * (G * NA) + (g + 1) * NA)
                if g == 0:
                    pe.wait_ge(z_done, M * (G * NCH))
                for c in range(NT2):
                    if c >= 2:
                        pe.wait_ge(t2_cp, L * (G * NT2) + g * NT2 + c - 1)
                    for j in range(4):
                        m = pe.transpose(bk(4 + c % 2)[:, P * j:P * (j + 1)],
                                         ya[:, 4 * c + j, :, :].rearrange("p x r -> p (x r)"), ident[:])
                    m.then_inc(t2_mm, 1)
                for c in range(NB):
                    pe.wait_ge(t2_cp, L * (G * NT2) + g * NT2 + 2 + c)
                    if g and c == 0:
                        pe.wait_ge(b_cp, L * (G * NB) + g * NB)
                    for j in range(6):
                        m = mm(bk(6 + c)[:, 48 * j:48 * j + 48], xa[:, 6 * c + j, :], dft_x[:], start=True, stop=True)
                    m.then_inc(b_mm, 1)
            pe.wait_ge(xm_in, L * (G * HR * 16) + G * HR * 16)
            wait_alone(pe, w_neg, L * 2 + 2, pe_passed)
            for c in range(NMIX):
                if c >= 2:
                    pe.wait_ge(mix_v, L * NMIX + c - 1)
                    wait_alone(pe, mix_a, L * NMIX + c - 1, pe_passed)
                for j in range(MC):
                    for half in range(2):
                        rows = slice(64 * half, 64 * half + 64)
                        m = mm(bk(2 * (c % 2) + half)[rows, BI * j:BI * (j + 1)],
                               mix_w[rows, :, :, c * MC + j].rearrange("p a b -> p (a b)"),
                               xm[rows, :, c * MC + j], start=True, stop=True)
                m.then_inc(mix_mm, 1)

            def front(g):
                pe.wait_ge(yr_cp, L * G + g + 1)
                if g >= 2:
                    pe.wait_ge(z_done, M * (G * NCH) + (g - 1) * NCH)
                for c in range(NY):
                    for j in range(3):
                        k = 3 * c + j
                        m = mm(bk(4 + c)[0:96, P * j:P * (j + 1)], yr[:, k, :, :].rearrange("p a b -> p (a b)"), centre[:],
                               start=True, stop=True)
                    m.then_inc(yt_mm, 1)
                for c in range(ND):
                    pe.wait_ge(yt_cp, L * (G * NY) + g * NY + (2 * c + 1) // 3 + 1)
                    if c >= 2:
                        pe.wait_ge(d_cp, L * (G * ND) + g * ND + c - 1)
                    for j in range(2):
                        m = mm(bk(6 + c % 2)[:, 256 * j:256 * j + 256], yt[:, 2 * c + j, :], idft_x[:],
                               start=True, stop=True)
                    m.then_inc(d_mm, 1)
                pe.wait_ge(d_cp, L * (G * ND) + (g + 1) * ND)
                for c in range(NZ):
                    if c >= 2:
                        pe.wait_ge(zt_cp, L * (G * NZ) + g * NZ + c - 1)
                    for j in range(4):
                        k = 4 * c + j
                        m = pe.transpose(bk(4 + c % 2)[0:96, P * j:P * (j + 1)],
                                         zx[:, 4 * k:4 * k + 4, :].rearrange("p x r -> p (x r)"), ident[:])
                    m.then_inc(zt_mm, 1)
                for c in range(NCH):
                    if c >= 2:
                        pe.wait_ge(y_cp, M * (G * NCH) + g * NCH + c - 1)
                    mm(bk(c % 2), layer_conv, h[:, g, CH * c:CH * (c + 1)], start=True, stop=False)
                    pe.wait_ge(zt_cp, L * (G * NZ) + g * NZ + c // 2 + 1)
                    for j in range(2):
                        m = mm(bk(c % 2)[:, 256 * j:256 * j + 256], zt[:, 2 * c + j, :], idft_y[:],
                               start=False, stop=(j == 1))
                    m.then_inc(y_mm, 1)

            norm(M, front)

        with pe.Fori(0, batches) as it:
            M0 = it * NORMS

            def front0(g):
                pe.wait_ge(xr_cp, it * G + g + 1)
                for o in range(4):
                    m = pe.transpose(bk(6)[0:96, P * o:P * (o + 1)],
                                     xr[:, o, :, :].rearrange("p i r -> p (i r)"), ident[:])
                m.then_inc(xt_mm, 1)
                pe.wait_ge(xt_cp, it * G + g + 1)
                for c in range(NCH):
                    if c >= 2:
                        pe.wait_ge(y_cp, M0 * (G * NCH) + g * NCH + c - 1)
                    for j in range(4):
                        r = 4 * c + j
                        m = mm(bk(c % 2)[:, P * j:P * (j + 1)], f0[:, r % RO, :], xt[:, r // RO, :],
                               start=True, stop=True)
                    m.then_inc(y_mm, 1)

            norm(M0, front0)
            with pe.Fori(0, LAYERS - 1) as l:
                pe.wait_ge(conv_in, it * LAYERS + l + 1)
                layer_body(it * LAYERS + l, it * NORMS + l + 1, conv_l[:])
            pe.wait_ge(conv_in, it * LAYERS + LAYERS)
            layer_body(it * LAYERS + LAYERS - 1, it * NORMS + LAYERS, conv_l[:])

            for g in range(G):
                pe.wait_ge(h_done, (it * NORMS + LAYERS) * (G * 2) + (g + 1) * 2)
                for n in range(NM + 2):
                    if n < NM:
                        u, k = divmod(n, NCH)
                        if n >= 2:
                            pe.wait_ge(m1_done, it * (G * NM) + g * NM + n - 1)
                        for i in range(2):
                            m = mm(bk(2 * (n % 2) + i), f1[:, 2 * u + i, :], h[:, g, CH * k:CH * (k + 1)],
                                   start=True, stop=True)
                        m.then_inc(m1_mm, 1)
                    if 1 <= n <= NM:
                        b = n - 1
                        pe.wait_ge(m1_done, it * (G * NM) + g * NM + b + 1)
                        if g or b >= 2:
                            pe.wait_ge(m2_done, it * (G * NM) + g * NM + b - 1)
                        for i in range(2):
                            m = mm(bk(4 + b % 2)[64 * i:64 * i + 64, :], f2[:], g1[:, b % 2, CH * i:CH * (i + 1)],
                                   start=True, stop=True)
                        m.then_inc(m2_mm, 1)
                    if n >= 2:
                        b = n - 2
                        u, k = divmod(b, NCH)
                        pe.wait_ge(m2_done, it * (G * NM) + g * NM + b + 1)
                        if k == 0 and (g or u):
                            pe.wait_ge(m3_cp, it * (G * 2) + g * 2 + u)
                        q = k % 4
                        m = mm(bk(6 + k // 4)[32 * q:32 * q + 32, :], f3[:], g2[:, b % 2, :], start=True, stop=True)
                        if k == NCH - 1:
                            m.then_inc(m3_mm, 1)
            pe.wait_ge(m3_cp, it * (G * 2) + G * 2)

    @block.vector
    def _(dve):
        v = nc.vector
        nset = 13 + 8 * IG + IG * RO + 4 + 2
        dve.wait_ge(setup_in, nset * 16)
        v.tensor_copy(selb[:].rearrange("p a b -> p (a b)"), sel_f).then_inc(setup_v, 1)
        v.tensor_tensor(f1[:], f1_rep.rearrange("p (a n) -> p a n", a=1).broadcast_to([P, IG, HID1]),
                        blk[:].rearrange("p (a n) -> p a n", n=1).broadcast_to([P, IG, HID1]), ALU.mult
                        ).then_inc(setup_v, 1)
        v.tensor_tensor(f3[:], mask2, f3_rep.broadcast_to([P, 32]), ALU.mult).then_inc(setup_v, 1)
        for i in range(IG):
            m = v.tensor_scalar(conv_bd[:, :, C * i:C * (i + 1)], conv_rep.rearrange("p (l c) -> p l c", l=LAYERS),
                                blk[:, i:i + 1], None, ALU.mult)
        m.then_inc(setup_v, 1)
        v.reduce_sum(f0_sum, f0_rep, AX_X).then_inc(setup_v, 1)
        dve.wait_ge(setup_v, 5)
        v.scalar_tensor_tensor(out=f0_rep, in0=f0_sum.broadcast_to([96, C]), scalar=-1.0 / C, in1=f0_rep,
                               op0=ALU.mult, op1=ALU.add).then_inc(setup_g, 1)
        dve.wait_ge(setup_g, 1)
        v.tensor_tensor(f0[:].rearrange("p r (i c) -> p (r i) c", i=IG),
                        f0_rep.rearrange("p (a c) -> p a c", a=1).broadcast_to([96, RO * IG, C]),
                        fmask.rearrange("p (n a) -> p n a", a=1).broadcast_to([96, RO * IG, C]), ALU.mult
                        ).then_inc(setup_g, 1)
        dve.wait_ge(setup_mm, 1)
        v.tensor_copy(conv[:].rearrange("p a b -> p (a b)"), bk(0)).then_inc(setup_v, 1)
        v.tensor_copy(cb[:], bk(1)[:, 0:NORMS]).then_inc(setup_v, 1)
        dve.wait_ge(setup_v, 7)
        dve.wait_ge(setup_g, 2)

        def stat_step(M, g, n):
            var = bank[1][:, :, :]
            if n == 0:
                dve.wait_ge(rs_done, M * G + g + 1)
            else:
                dve.wait_ge(st_done, M * (G * NST) + g * NST + n)
            if n == 0:
                m = v.scalar_tensor_tensor(out=newt[:], in0=var, scalar=EPS, in1=rstd[:], op0=ALU.add, op1=ALU.mult)
            elif n == 1:
                m = v.scalar_tensor_tensor(out=newt[:], in0=newt[:], scalar=-0.5, in1=rstd[:], op0=ALU.mult,
                                           op1=ALU.mult)
            elif n == 2:
                m = v.scalar_tensor_tensor(out=rstd[:], in0=newt[:], scalar=1.5, in1=rstd[:], op0=ALU.add, op1=ALU.mult)
            elif n == 3 or n == 5:
                m = v.tensor_copy(part[:], rstd[:])
            elif n == 4 or n == 6:
                m = v.scalar_tensor_tensor(out=rstd[:], in0=part[:], scalar=minus[:, (n - 4) // 2:(n - 4) // 2 + 1],
                                           in1=rstd[:], op0=ALU.mult, op1=ALU.add)
            else:
                m = v.tensor_copy(r3[:], rstd[:])
            m.then_inc(st_done, 1)

        def scale(M, g):
            for k in range(NCH):
                dve.wait_ge(bc_mm, M * (G * NCH) + g * NCH + k + 1)
                hc = h[:, g, CH * k:CH * (k + 1)]
                v.tensor_tensor(hc, bk(4 + k % 2), hc, ALU.mult).then_inc(z_done, 1)

        def norm(M, front, copy_out):
            for g in range(G):
                front(g)
                for c in range(NCH):
                    dve.wait_ge(y_mm, M * (G * NCH) + g * NCH + c + 1)
                    copy_out(g, c).then_inc(y_cp, 1)
                    if g:
                        stat_step(M, g - 1, c)
                if g:
                    scale(M, g - 1)
            for n in range(NST):
                stat_step(M, G - 1, n)
            scale(M, G - 1)

        def layer_body(L, M, bias):
            for g in range(G):
                for c in range(NT):
                    dve.wait_ge(t_mm, L * (G * NT) + g * NT + c + 1)
                    v.tensor_copy(th[:, c % 2, :], bk(c % 2)).then_inc(t_cp, 1)
                for c in range(NB):
                    dve.wait_ge(b_mm, L * (G * NB) + g * NB + c + 1)
                    if g and c == 0:
                        dve.wait_ge(xg_out, L * (G * 16) + g * 16)
                    v.tensor_copy(xg[:, :, :, 6 * c:6 * c + 6].rearrange("p h x y -> p y h x"),
                                  bk(6 + c)[:, 0:288].rearrange("p (y h x) -> p y h x", y=6, h=HR)
                                  ).then_inc(b_cp, 1)
            dve.wait_ge(w_in, L * (8 * 16) + 8 * 16)
            for half in range(2):
                rows = slice(64 * half + 32, 64 * half + 64)
                v.tensor_scalar(mix_w[rows, 0, :, :], mix_w[rows, 0, :, :], -1.0, None, ALU.mult).then_inc(w_neg, 1)
            for c in range(NMIX):
                dve.wait_ge(mix_mm, L * NMIX + c + 1)
                v.tensor_copy(ym[0:64, :, c * MC:(c + 1) * MC].rearrange("p i m -> p m i"),
                              bk(2 * (c % 2))[0:64, 0:MC * BI].rearrange("p (m i) -> p m i", i=BI)).then_inc(mix_v, 1)

            def front(g):
                dve.wait_ge(yg_in[g % 2], L * 32 + (g // 2 + 1) * 16)
                if g:
                    dve.wait_ge(yt_mm, L * (G * NY) + g * NY)
                v.tensor_copy(yr[:], yg[:, g % 2, :, :].rearrange("p n (k y) -> p k n y", y=2)).then_inc(yr_cp, 1)
                for c in range(ND):
                    dve.wait_ge(d_mm, L * (G * ND) + g * ND + c + 1)
                    v.tensor_copy(zx[:, :, 8 * c:8 * c + 8].rearrange("p x (k f) -> p k x f", k=2),
                                  bk(6 + c % 2).rearrange("p (k x f) -> p k x f", k=2, x=S)).then_inc(d_cp, 1)

            norm(M, front, lambda g, c: v.tensor_scalar(h[:, g, CH * c:CH * (c + 1)], bk(c % 2), bias, None, ALU.add))

        with dve.Fori(0, batches) as it:
            norm(it * NORMS, lambda g: None,
                 lambda g, c: v.tensor_scalar(
                     h[:, g, :].rearrange("p (q r) -> p r q", r=32)[:, 4 * c:4 * c + 4, :],
                     bk(c % 2).rearrange("p (r q) -> p r q", r=4), cb[:, 0:1], None, ALU.add))
            with dve.Fori(0, LAYERS - 1) as l:
                dve.wait_ge(conv_in, it * LAYERS + l + 1)
                layer_body(it * LAYERS + l, it * NORMS + l + 1, cb_l[:, 0:1])
            dve.wait_ge(conv_in, it * LAYERS + LAYERS)
            layer_body(it * LAYERS + LAYERS - 1, it * NORMS + LAYERS, cb_l[:, 0:1])
            for g in range(G):
                for u in range(2):
                    n = g * 2 + u
                    dve.wait_ge(m3_mm, it * (G * 2) + n + 1)
                    if n:
                        dve.wait_ge(tok_out, it * (G * 2 * 32) + n * 32)
                    v.tensor_scalar(tok, bank[3][:, :, :], b3[:, 0:1], None, ALU.add).then_inc(m3_cp, 1)
            dve.wait_ge(tok_out, it * (G * 2 * 32) + G * 2 * 32)

    @block.scalar
    def _(act):
        s = nc.scalar
        nset = 13 + 8 * IG + IG * RO + 4 + 2
        act.wait_ge(setup_in, nset * 16)
        s.activation(epst[:], ident[:, 0:1], ACT.Copy, bias=EPS, scale=0.0).then_inc(eps_set, 1)
        act.wait_ge(eps_set, 1)
        act.wait_ge(setup_v, 7)

        def copy(dst, src):
            return s.activation(dst, src, ACT.Copy)

        def estimate(M, g):
            act.wait_ge(var_mm, M * (G * 4) + (g + 1) * 4)
            s.activation(rstd[:], bank[1][:, :, :], ACT.Abs_reciprocal_sqrt, bias=epst[:, 0:1]).then_inc(rs_done, 1)

        def norm(M, front, rest, func, gamma, beta, square_after):
            def final(g):
                for n in range(2):
                    act.wait_ge(z_done, M * (G * NCH) + g * NCH + 4 * n + 4)
                    hh = h[:, g, 2048 * n:2048 * (n + 1)]
                    s.activation(hh, hh, func, bias=beta, scale=gamma).then_inc(h_done, 1)

            for g in range(G):
                front(g)
                if g:
                    estimate(M, g - 1)
                rest(g)
                for n in range(4):
                    act.wait_ge(y_cp, M * (G * NCH) + g * NCH + (NCH if square_after else 2 * n + 2))
                    if n >= 2:
                        act.wait_ge(var_mm, M * (G * 4) + g * 4 + n - 1)
                    s.activation(sq[:, n % 2, :], h[:, g, 1024 * n:1024 * (n + 1)], ACT.Square).then_inc(sq_done, 1)
                if g:
                    final(g - 1)
            estimate(M, G - 1)
            final(G - 1)

        def layer_weights(L, l, M):
            act.wait_ge(y_cp, M * (G * NCH))
            act.wait_ge(h_done, M * (G * 2))
            copy(conv_l[:], conv[:, l, :]) if isinstance(l, int) else copy(
                conv_l[:], conv[:, bass.ds(l, 1), :].rearrange("p a b -> p (a b)"))
            sl = slice(l + 1, l + 2) if isinstance(l, int) else bass.ds(l + 1, 1)
            copy(cb_l[:, 0:1], cb[:, sl])
            copy(cb_l[:, 1:2], gam[:, sl])
            copy(cb_l[:, 2:3], bet[:, sl]).then_inc(conv_in, 1)
            act.wait_ge(conv_in, L + 1)

        def layer_body(L, M, func):
            for g in range(G):
                for c in range(NA):
                    act.wait_ge(a_mm, L * (G * NA) + g * NA + c + 1)
                    copy(ya[:, :, 16 * c:16 * c + 16, :].rearrange("p k x r -> p x k r"),
                         bk(2 + c % 2)[:, 0:384].rearrange("p (x k r) -> p x k r", x=16, k=M2)).then_inc(a_cp, 1)
                for c in range(NT2):
                    act.wait_ge(t2_mm, L * (G * NT2) + g * NT2 + c + 1)
                    copy(xa[:, 4 * c:4 * c + 4, :].rearrange("p a b -> p (a b)"), bk(4 + c % 2)).then_inc(t2_cp, 1)
            for c in range(NMIX):
                act.wait_ge(mix_mm, L * NMIX + c + 1)
                copy(ym[64:128, :, c * MC:(c + 1) * MC].rearrange("p i m -> p m i"),
                     bk(2 * (c % 2) + 1)[64:128, 0:MC * BI].rearrange("p (m i) -> p m i", i=BI)).then_inc(mix_a, 1)

            def front(g):
                for c in range(NY):
                    act.wait_ge(yt_mm, L * (G * NY) + g * NY + c + 1)
                    copy(yt[:, 3 * c:3 * c + 3, :].rearrange("p a b -> p (a b)"), bk(4 + c)[0:96, 0:384]
                         ).then_inc(yt_cp, 1)

            def rest(g):
                for c in range(NZ):
                    act.wait_ge(zt_mm, L * (G * NZ) + g * NZ + c + 1)
                    copy(zt[:, 4 * c:4 * c + 4, :].rearrange("p a b -> p (a b)"), bk(4 + c % 2)[0:96, :]
                         ).then_inc(zt_cp, 1)

            norm(M, front, rest, func, cb_l[:, 1:2], cb_l[:, 2:3], False)

        with act.Fori(0, batches) as it:
            def front0(g):
                act.wait_ge(x_in, it * (G * 16) + G * 16)
                copy(xr[:], xin[:, g, :, :].rearrange("p i (o r) -> p o i r", o=4)).then_inc(xr_cp, 1)
                act.wait_ge(xt_mm, it * G + g + 1)
                copy(xt[:].rearrange("p a b -> p (a b)"), bk(6)[0:96, :]).then_inc(xt_cp, 1)

            norm(it * NORMS, front0, lambda g: None, ACT.Identity, gam[:, 0:1], bet[:, 0:1], True)
            with act.Fori(0, LAYERS - 1) as l:
                layer_weights(it * LAYERS + l, l, it * NORMS + l + 1)
                layer_body(it * LAYERS + l, it * NORMS + l + 1, ACT.Gelu)
            layer_weights(it * LAYERS + LAYERS - 1, LAYERS - 1, it * NORMS + LAYERS)
            layer_body(it * LAYERS + LAYERS - 1, it * NORMS + LAYERS, ACT.Identity)
            for g in range(G):
                for n in range(NM + 1):
                    if n < NM:
                        act.wait_ge(m1_mm, it * (G * NM) + g * NM + n + 1)
                        s.activation(g1[:, n % 2, :], bank[n % 2][:, :, :], ACT.Gelu, bias=b1[:, 0:1]
                                     ).then_inc(m1_done, 1)
                    if n:
                        act.wait_ge(m2_mm, it * (G * NM) + g * NM + n)
                        s.activation(g2[:, (n - 1) % 2, :], bk(4 + (n - 1) % 2), ACT.Gelu, bias=b2[:, 0:1]
                                     ).then_inc(m2_done, 1)


D = 64
HEADS, HD, HP = 4, 16, 32
MAX_REL = 30
TL = 8
ROUNDS = NIMG // (2 * TL)
RT = TL * P
FH = 4 * D
KEPT = S // 2 - 1


def attention_constants():
    f4 = np.float32
    pos = np.arange(2 * MAX_REL + 1, dtype=f4)[:, None]
    div = np.exp(np.arange(0, D, 2, dtype=f4) * f4(-np.log(10000.0) / D)).astype(f4)
    ang = (pos * div).astype(f4)
    enc = np.stack([np.sin(ang), np.cos(ang)], -1).reshape(-1, D)
    near = np.clip(np.arange(2 * S - 1) - (S - 1), -MAX_REL, MAX_REL) + MAX_REL
    enc_t = np.concatenate([enc[near].T, np.ones((1, 2 * S - 1))])
    t = np.arange(P) % S
    before = (np.arange(S)[None, :] < t[:, None])
    out = dict(k_enc=enc_t, k_before=before)
    return {k: np.ascontiguousarray(v, np.float32) for k, v in out.items()}


def attention_and_ffn(nc, ctx, a, tokens, out):
    def sb(name, shape, dt=F32):
        return ctx.enter_context(nc.sbuf_tensor(name, shape, dt))

    def sem(name):
        return ctx.enter_context(nc.semaphore(name))

    bank = [ctx.enter_context(nc.psum_tensor(f"pbank{i}", [P, 2, CH], F32)) for i in range(4)]

    def bk(n):
        return bank[n // 2][:, n % 2, :]

    ident, blk, before = sb("ident2", [P, P]), sb("blk2", [P, IG]), sb("before", [P, S])
    enc_t = sb("enc_t", [D + 1, 2 * S - 1])
    w_p, bias_uv = sb("w_p", [P, 5, D + 1]), sb("bias_uv", [P, 2])
    w_t = sb("w_t", [D + 1, 5, P])
    wo_p, wo_t = sb("wo_p", [D, HEADS, HP]), sb("wo_t", [P, D])
    pos_t, pos_bd = sb("pos_t", [P, 2 * S - 1]), sb("pos_bd", [P, HEADS, 2 * S - 1])
    rows = sb("rows", [P, 5, D])
    br = sb("br", [P, 1])
    w1, w2, fb1 = sb("w1s", [D, FH]), sb("w2s", [P, 2, D]), sb("fb1", [P, 2])

    ht, xa, tmp = sb("ht", [P, TL, D]), sb("xa2", [P, TL, D]), sb("tmp", [P, TL, D])
    ln_s = sb("ln_s", [P, 4, TL])
    x_t = sb("x_t", [D + 1, RT])
    qv = sb("qv", [P, NIMG, S])
    pos_s = sb("pos_s", [P, 2, TL, HEADS * S])
    pos_in = sb("pos_in", [P, TL, HEADS * S])
    q, k = sb("q", [P, RT]), sb("kk", [P, RT])
    val = sb("val", [S, 2 * TL, P])
    att = sb("att", [P, HEADS, TL, S])
    stat = sb("stat", [P, 2, HEADS, TL])
    att_t = sb("att_t", [S, TL, HEADS, P])
    ctx_t = sb("ctx_t", [P, RT])
    h4, x5 = sb("h4", [P, TL, D]), sb("x5", [P, TL, D])
    w, coef = sb("wgt", [P, TL]), sb("coef", [P, TL])
    above, same = sb("above", [P, TL, S]), sb("same", [P, TL, S])
    hid = sb("hid", [P, 2, 2, CH])

    scr_p = a["scr_p"]
    tok_v = tokens.rearrange("i (t d) -> (i t) d", d=D).rearrange("(n p) d -> p n d", p=P)
    out_v = out.rearrange("i t d -> (i t) d").rearrange("(n p) d -> p n d", p=P)
    pos_v = scr_p.rearrange("i t m -> (i t) m").rearrange("(n p) m -> p n m", p=P)

    s2_in, s2_zero, s2_v, s2_mm = sem("s2_in"), sem("s2_zero"), sem("s2_v"), sem("s2_mm")
    a_in, a_x, a_xt, a_xtc, a_q, a_qc, a_var, a_rs = (sem("a_in"), sem("a_x"), sem("a_xt"), sem("a_xtc"), sem("a_q"),
                                                      sem("a_qc"), sem("a_var"), sem("a_rs"))
    pe_passed, sp_passed = sem("pe_passed"), sem("sp_passed")
    p_mm, p_v, p_a, p_out = sem("p_mm"), sem("p_v"), sem("p_a"), [sem("p_out0"), sem("p_out1")]
    names = ("tok_in pos_ld x_ready xt_mm2 xt_c qk_mm q_c k_c val_mm val_c score_mm shifted exp_c att_n at_mm0 at_mm1 "
             "at_c0 at_c1 ctx_mm ctx_c wo_mm x5_ready x5t_mm x5t_c w_ready wt_mm hid_mm hid_c y2_mm res "
             "out_st seq_a seq_b b_var b_rs h4_ready wt_read y2_read").split()
    s = {n: sem("b_" + n) for n in names}
    block = ctx.enter_context(nc.Block())
    NSET = 4 + 5 * HEADS + 5 * HEADS + 2 * HEADS + 1 + 5 + 1 + 3

    @block.sync
    def _(sp):
        col = lambda v: v.rearrange("(c o) -> c o", o=1)
        for t, n in ((ident, "k_ident"), (blk, "k_blk"), (before, "k_before"), (enc_t, "k_enc")):
            sp.dma_start(t[:], a[n]).then_inc(s2_in, 16)
        sp.wait_ge(s2_zero, 4)
        with nc.allow_non_contiguous_dma(reason="a few small weights"):
            for n, (wn, bn) in enumerate((("Wq", "bq"), ("Wq", "bq"), ("Wk", "bk"), ("Wv", "bv"), ("Wpos", "bpos"))):
                for hd in range(HEADS):
                    dst = slice(HP * hd, HP * hd + HD)
                    src = slice(HD * hd, HD * hd + HD)
                    sp.dma_start(w_p[dst, n, 0:D], a["L0_attn_" + wn][src, :]).then_inc(s2_in, 16)
                    sp.dma_start(w_p[dst, n, D:D + 1], col(a["L0_attn_" + bn])[src, :]).then_inc(s2_in, 16)
            for n, un in enumerate(("u_bias", "v_bias")):
                for hd in range(HEADS):
                    sp.dma_start(bias_uv[HP * hd:HP * hd + HD, n:n + 1],
                                 a["L0_attn_" + un].rearrange("a h b d -> (a h b) d")[hd:hd + 1, :]
                                 .rearrange("a d -> d a")).then_inc(s2_in, 16)
            sp.dma_start(wo_p[:, :, 0:HD], a["L0_attn_Wo"].rearrange("o (h d) -> o h d", h=HEADS)).then_inc(s2_in, 16)
            for n, v in enumerate((a["L0_attn_ln_gamma"], a["L0_attn_ln_beta"], a["L0_attn_bo"],
                                   a["L0_ffn_wr"].rearrange("d o -> (d o)"), a["L0_ffn_b2"])):
                sp.dma_start(rows[:, n, :], v.rearrange("(a d) -> a d", a=1).broadcast_to([P, D])).then_inc(s2_in, 16)
            sp.dma_start(br[:], a["L0_ffn_br"].rearrange("(a b) -> a b", a=1).broadcast_to([P, 1])).then_inc(s2_in, 16)
            sp.dma_start(w1[:], a["L0_ffn_w1"]).then_inc(s2_in, 16)
            sp.dma_start(w2[:], a["L0_ffn_w2"].rearrange("(n p) d -> p n d", p=P)).then_inc(s2_in, 16)
            sp.dma_start(fb1[:], a["L0_ffn_b1"].rearrange("(n p) -> p n", p=P)).then_inc(s2_in, 16)
        with sp.Fori(0, ROUNDS) as o:
            sp.dma_start(ht[:], tok_v[:, bass.ds(o * TL, TL), :]).then_inc(a_in, 16)
            wait_alone(sp, a_x, o + 1, sp_passed)
        for n in range(S // TL):
            sp.wait_ge(p_v, 2 * (n + 1))
            sp.wait_ge(p_a, 2 * (n + 1))
            sp.dma_start(scr_p[:, TL * n:TL * (n + 1), :], pos_s[:, n % 2, :, :]).then_inc(p_out[n % 2], 16)
        for n in range(2):
            sp.wait_ge(p_out[n], 16 * (S // TL // 2))
        with sp.Fori(0, ROUNDS) as o:
            sp.dma_start(ht[:], tok_v[:, bass.ds(o * TL, TL), :]).then_inc(s["tok_in"], 16)
            sp.dma_start(pos_in[:], pos_v[:, bass.ds(o * TL, TL), :]).then_inc(s["pos_ld"], 16)
            sp.wait_ge(s["res"], o + 1)
            sp.dma_start(out_v[:, bass.ds(o * TL, TL), :], xa[:]).then_inc(s["out_st"], 16)
            wait_alone(sp, s["out_st"], o * 16 + 16, sp_passed)

    @block.tensor
    def _(pe):
        mm = nc.tensor.matmul
        pe.wait_ge(s2_in, NSET * 16)
        pe.wait_ge(s2_v, 1)
        for n in range(5):
            pe.transpose(bk(n // 4)[0:D + 1, P * (n % 4):P * (n % 4 + 1)], w_p[:, n, :], ident[:])
        pe.transpose(bk(2)[:, 0:D], wo_p[:].rearrange("p a b -> p (a b)"), ident[0:D, 0:D]).then_inc(s2_mm, 1)
        pe.wait_ge(s2_v, 3)
        mm(bk(3)[:, 0:2 * S - 1], w_t[:, 4, :], enc_t[:], start=True, stop=True).then_inc(s2_mm, 1)
        pe.wait_ge(s2_v, 5)

        def transposes(src, done):
            for n in range(TL):
                m = pe.transpose(bk(n // 4)[0:D, P * (n % 4):P * (n % 4 + 1)], src[:, n, :], ident[:])
            m.then_inc(done, 1)

        with pe.Fori(0, ROUNDS) as o:
            wait_alone(pe, a_x, o + 1, pe_passed)
            transposes(xa, a_xt)
            pe.wait_ge(a_xtc, o + 1)
            for n in range(2):
                m = mm(bk(2 + n), w_t[:, 1, :], x_t[:, CH * n:CH * (n + 1)], start=True, stop=True)
            m.then_inc(a_q, 1)
        pe.wait_ge(a_qc, ROUNDS)
        for t in range(S):
            c = t // 2
            if c >= 8 and t % 2 == 0:
                pe.wait_ge(p_v if c % 2 == 0 else p_a, (c - 8) // 2 + 1)
            m = mm(bk(c % 8)[:, 256 * (t % 2):256 * (t % 2) + 256], qv[:, :, t], pos_bd[:, :, S - 1 - t:2 * S - 1 - t],
                   start=True, stop=True)
            if t % 2:
                m.then_inc(p_mm, 1)
        pe.wait_ge(p_v, S // 4)
        pe.wait_ge(p_a, S // 4)
        with pe.Fori(0, ROUNDS) as o:
            wait_alone(pe, s["x_ready"], o + 1, pe_passed)
            transposes(xa, s["xt_mm2"])
            pe.wait_ge(s["xt_c"], o + 1)
            for n in range(2):
                mm(bk(2 + n), w_t[:, 0, :], x_t[:, CH * n:CH * (n + 1)], start=True, stop=True)
                m = mm(bk(4 + n), w_t[:, 2, :], x_t[:, CH * n:CH * (n + 1)], start=True, stop=True)
            m.then_inc(s["qk_mm"], 1)
            for n in range(2 * TL):
                b = (6, 7, 0, 1)[n // 4]
                m = mm(bk(b)[0:S, P * (n % 4):P * (n % 4 + 1)], x_t[:, S * n:S * (n + 1)], w_t[:, 3, :],
                       start=True, stop=True)
            m.then_inc(s["val_mm"], 1)
            pe.wait_ge(s["q_c"], o + 1)
            pe.wait_ge(s["k_c"], o + 1)
            for n in range(2 * TL):
                for hd in range(HEADS):
                    r = slice(HP * hd, HP * (hd + 1))
                    m = mm(bk(2 + hd)[S * (n % 2):S * (n % 2) + S, S * (n // 2):S * (n // 2) + S],
                           q[r, S * n:S * (n + 1)], k[r, S * n:S * (n + 1)], start=True, stop=True)
            m.then_inc(s["score_mm"], 1)
            pe.wait_ge(s["att_n"], o + 1)
            wait_alone(pe, s["val_c"], o + 1, pe_passed)
            for n in range(TL):
                for hd in range(HEADS):
                    b = (6, 7, 0, 1, 2, 3, 4, 5)[n]
                    m = pe.transpose(bk(b)[0:S, P * hd:P * (hd + 1)], att[:, hd, n, :], ident[:])
                if n == 3:
                    m.then_inc(s["at_mm0"], 1)
            m.then_inc(s["at_mm1"], 1)
            pe.wait_ge(s["at_c0"], o + 1)
            wait_alone(pe, s["at_c1"], o + 1, pe_passed)
            for n in range(2 * TL):
                for hd in range(HEADS):
                    m = mm(bk(n // 8)[HP * hd:HP * (hd + 1), S * (n % 8):S * (n % 8) + S], val[:, n, HP * hd:HP * (hd + 1)],
                           att_t[:, n // 2, hd, S * (n % 2):S * (n % 2) + S], start=True, stop=True)
            m.then_inc(s["ctx_mm"], 1)
            pe.wait_ge(s["ctx_c"], o + 1)
            for n in range(TL):
                m = mm(bk(6)[:, D * n:D * (n + 1)], ctx_t[:, P * n:P * (n + 1)], wo_t[:], start=True, stop=True)
            m.then_inc(s["wo_mm"], 1)
            wait_alone(pe, s["x5_ready"], o + 1, pe_passed)
            transposes(x5, s["x5t_mm"])
            pe.wait_ge(s["w_ready"], o + 1)
            for n in range(TL):
                m = pe.transpose(bk(4 + n // 4)[:, P * (n % 4):P * (n % 4 + 1)], w[:, n:n + 1].broadcast_to([P, P]),
                                 ident[:])
            m.then_inc(s["wt_mm"], 1)
            pe.wait_ge(s["x5t_c"], o + 1)
            for c in range(2):
                for n in range(2):
                    m = mm(bk(2 - 2 * c + n), w1[:, P * n:P * (n + 1)], x_t[0:D, CH * c:CH * (c + 1)],
                           start=True, stop=True)
                m.then_inc(s["hid_mm"], 1)
            pe.wait_ge(s["hid_c"], o * 2 + 2)
            for n in range(TL):
                for c in range(2):
                    m = mm(bk(7)[:, D * n:D * (n + 1)], hid[:, n // 4, c, P * (n % 4):P * (n % 4 + 1)], w2[:, c, :],
                           start=(c == 0), stop=(c == 1))
            m.then_inc(s["y2_mm"], 1)

    def per_token(v, width=D):
        return v.rearrange("p (n a) -> p n a", a=1).broadcast_to([P, TL, width])

    def per_feature(v):
        return v.rearrange("p (a d) -> p a d", a=1).broadcast_to([P, TL, v.shape[-1]])

    @block.vector
    def _(dve):
        v = nc.vector
        for t in (w_p, wo_p, bias_uv):
            v.memset(t[:], 0.0).then_inc(s2_zero, 1)
        v.memset(x_t[D:D + 1, :], 1.0).then_inc(s2_zero, 1)
        dve.wait_ge(s2_in, NSET * 16)
        v.tensor_tensor(w_p[:, 0:2, D], w_p[:, 0:2, D], bias_uv[:], ALU.add).then_inc(s2_v, 1)
        dve.wait_ge(s2_mm, 1)
        v.tensor_copy(w_t[:, 0:4, :].rearrange("p a b -> p (a b)"), bk(0)[0:D + 1, :])
        v.tensor_copy(w_t[:, 4, :], bk(1)[0:D + 1, 0:P]).then_inc(s2_v, 1)
        v.tensor_copy(wo_t[:], bk(2)[:, 0:D]).then_inc(s2_v, 1)
        dve.wait_ge(s2_mm, 2)
        v.tensor_copy(pos_t[:], bk(3)[:, 0:2 * S - 1]).then_inc(s2_v, 1)
        dve.wait_ge(s2_v, 4)
        v.tensor_tensor(pos_bd[:], pos_t[:].rearrange("p (a d) -> p a d", a=1).broadcast_to([P, HEADS, 2 * S - 1]),
                        blk[:].rearrange("p (a d) -> p a d", d=1).broadcast_to([P, HEADS, 2 * S - 1]), ALU.mult
                        ).then_inc(s2_v, 1)
        dve.wait_ge(s2_v, 5)

        class Chain:
            def __init__(self, semaphore, base, steps):
                self.semaphore, self.base, self.n = semaphore, base * steps, 0

            def __call__(self, ins):
                self.n += 1
                ins.then_inc(self.semaphore, 1)
                dve.wait_ge(self.semaphore, self.base + self.n)

        def normalise(link, dst, src, var_ready, rs_ready, nth):
            total, var, est, u = (ln_s[:, n, :] for n in range(4))
            link(v.reduce_sum(total, src, AX_X))
            link(v.scalar_tensor_tensor(out=dst, in0=per_token(total), scalar=-1.0 / D, in1=src, op0=ALU.mult,
                                        op1=ALU.add))
            link(v.tensor_tensor(tmp[:], dst, dst, ALU.mult))
            link(v.reduce_sum(total, tmp[:], AX_X))
            v.tensor_scalar(var, total, 1.0 / D, EPS, ALU.mult, ALU.add).then_inc(var_ready, 1)
            dve.wait_ge(rs_ready, nth)
            link(v.tensor_tensor(u, var, est, ALU.mult))
            link(v.scalar_tensor_tensor(out=u, in0=u, scalar=-0.5, in1=est, op0=ALU.mult, op1=ALU.mult))
            link(v.scalar_tensor_tensor(out=est, in0=u, scalar=1.5, in1=est, op0=ALU.add, op1=ALU.mult))
            return v.tensor_tensor(dst, dst, per_token(est), ALU.mult)

        def inputs(link, var_ready, rs_ready, base, ready):
            link(normalise(link, xa[:], ht[:], var_ready, rs_ready, base + 1))
            link(normalise(link, xa[:], xa[:], var_ready, rs_ready, base + 2))
            link(v.tensor_tensor(xa[:], xa[:], per_feature(rows[:, 0, :]), ALU.mult))
            v.tensor_tensor(xa[:], xa[:], per_feature(rows[:, 1, :]), ALU.add).then_inc(ready, 1)

        STEPS_A = 17
        with dve.Fori(0, ROUNDS) as o:
            link = Chain(s["seq_a"], o, STEPS_A)
            dve.wait_ge(a_in, o * 16 + 16)
            inputs(link, a_var, a_rs, o * 2, a_x)
            dve.wait_ge(a_xt, o + 1)
            assert link.n == STEPS_A
        for c in range(0, S // 2, 2):
            n = c // 4
            if n >= 2 and c % 4 == 0:
                dve.wait_ge(p_out[n % 2], 16 * (n // 2))
            dve.wait_ge(p_mm, c + 1)
            v.tensor_copy(pos_s[:, n % 2, 2 * (c % 4):2 * (c % 4) + 2, :].rearrange("p a b -> p (a b)"), bk(c % 8)
                          ).then_inc(p_v, 1)
        STEPS_B = 46
        with dve.Fori(0, ROUNDS) as o:
            link = Chain(s["seq_b"], o, STEPS_B)
            dve.wait_ge(s["tok_in"], o * 16 + 16)
            inputs(link, s["b_var"], s["b_rs"], o * 3, s["x_ready"])
            link(v.tensor_tensor(h4[:], ht[:], per_feature(rows[:, 2, :]), ALU.add))
            dve.wait_ge(s["qk_mm"], o + 1)
            v.tensor_copy(k[:].rearrange("p (a b) -> p a b", a=2), bank[2][:, :, :]).then_inc(s["k_c"], 1)
            dve.wait_ge(s["score_mm"], o + 1)
            dve.wait_ge(s["pos_ld"], o * 16 + 16)
            for hd in range(HEADS):
                link(v.tensor_tensor(att[:, hd, :, :], bk(2 + hd).rearrange("p (n t) -> p n t", t=S),
                                     pos_in[:, :, S * hd:S * (hd + 1)], ALU.add))
            att_v = att[:].rearrange("p h n t -> p (h n) t")
            top = stat[:, 0, :, :].rearrange("p h n -> p (h n)")
            total = stat[:, 1, :, :].rearrange("p h n -> p (h n)")

            def per_row(x):
                return x.rearrange("p (n a) -> p n a", a=1).broadcast_to([P, HEADS * TL, S])

            link(v.tensor_reduce(top, att_v, AX_X, ALU.max))
            v.tensor_tensor(att_v, att_v, per_row(top), ALU.subtract).then_inc(s["shifted"], 1)
            dve.wait_ge(s["exp_c"], o + 1)
            link(v.reduce_sum(total, att_v, AX_X))
            link(v.reciprocal(top, total))
            v.tensor_tensor(att_v, att_v, per_row(top), ALU.mult).then_inc(s["att_n"], 1)
            dve.wait_ge(s["at_mm1"], o + 1)
            v.tensor_copy(att_t[:, 4:6, :, :].rearrange("p a h t -> p (a h t)").rearrange("p (a b) -> p a b", a=2),
                          bank[1][0:S, :, :])
            v.tensor_copy(att_t[:, 6:8, :, :].rearrange("p a h t -> p (a h t)").rearrange("p (a b) -> p a b", a=2),
                          bank[2][0:S, :, :]).then_inc(s["at_c1"], 1)
            dve.wait_ge(s["wo_mm"], o + 1)
            link(v.tensor_tensor(h4[:].rearrange("p n d -> p (n d)"), bk(6), h4[:].rearrange("p n d -> p (n d)"), ALU.add))
            normalise(link, x5[:], h4[:], s["b_var"], s["b_rs"], o * 3 + 3).then_inc(s["x5_ready"], 1)
            dve.wait_ge(s["x5_ready"], o + 1)
            link(v.tensor_tensor(tmp[:], x5[:], per_feature(rows[:, 3, :]), ALU.mult))
            link(v.reduce_sum(w[:], tmp[:], AX_X))
            v.tensor_scalar(w[:], w[:], br[:, 0:1], None, ALU.add).then_inc(s["w_ready"], 1)
            link(v.tensor_tensor(h4[:], h4[:], x5[:], ALU.add))
            dve.wait_ge(s["w_ready"], o + 1)
            dve.wait_ge(s["wt_mm"], o + 1)
            for i in range(2):
                r = slice(S * i, S * (i + 1))
                others = bank[2][r, :, :].rearrange("p a b -> p (a b)").rearrange("p (n c j) -> p n c j", c=2, j=S)[:, :, i, :]
                own = w[r, :].rearrange("p (n a) -> p n a", a=1).broadcast_to([S, TL, S])
                link(v.tensor_tensor(above[r, :, :], others, own, ALU.is_gt))
                link(v.tensor_tensor(same[r, :, :], others, own, ALU.is_equal))
            link(v.tensor_tensor(same[:], same[:], per_feature(before[:]), ALU.mult))
            link(v.tensor_tensor(above[:], above[:], same[:], ALU.add))
            link(v.reduce_sum(coef[:], above[:], AX_X))
            link(v.scalar_tensor_tensor(out=coef[:], in0=coef[:], scalar=KEPT - 0.5, in1=w[:], op0=ALU.is_lt,
                                        op1=ALU.mult))
            dve.wait_ge(s["y2_mm"], o + 1)
            link(v.tensor_tensor(tmp[:], bk(7).rearrange("p (n d) -> p n d", d=D), per_feature(rows[:, 4, :]), ALU.add))
            link(v.tensor_tensor(tmp[:], tmp[:], per_token(coef[:]), ALU.mult))
            v.tensor_tensor(xa[:], tmp[:], h4[:], ALU.add).then_inc(s["res"], 1)
            dve.wait_ge(s["out_st"], o * 16 + 16)
            assert link.n == STEPS_B

    @block.scalar
    def _(act):
        f = nc.scalar
        act.wait_ge(s2_v, 5)

        def copy(dst, src):
            return f.activation(dst, src, ACT.Copy)

        def estimate(var_ready, rs_ready, nth):
            act.wait_ge(var_ready, nth)
            f.activation(ln_s[:, 2, :], ln_s[:, 1, :], ACT.Abs_reciprocal_sqrt).then_inc(rs_ready, 1)

        with act.Fori(0, ROUNDS) as o:
            estimate(a_var, a_rs, o * 2 + 1)
            estimate(a_var, a_rs, o * 2 + 2)
            act.wait_ge(a_xt, o + 1)
            copy(x_t[0:D, :].rearrange("p (a b) -> p a b", a=2), bank[0][0:D, :, :]).then_inc(a_xtc, 1)
            act.wait_ge(a_q, o + 1)
            copy(qv[:, bass.ds(o * 2 * TL, 2 * TL), :].rearrange("p i t -> p (i t)").rearrange("p (a b) -> p a b", a=2),
                 bank[1][:, :, :]).then_inc(a_qc, 1)
        for c in range(1, S // 2, 2):
            n = c // 4
            if n >= 2 and c % 4 == 1:
                act.wait_ge(p_out[n % 2], 16 * (n // 2))
            act.wait_ge(p_mm, c + 1)
            copy(pos_s[:, n % 2, 2 * (c % 4):2 * (c % 4) + 2, :].rearrange("p a b -> p (a b)"), bk(c % 8)
                 ).then_inc(p_a, 1)
        with act.Fori(0, ROUNDS) as o:
            estimate(s["b_var"], s["b_rs"], o * 3 + 1)
            estimate(s["b_var"], s["b_rs"], o * 3 + 2)
            act.wait_ge(s["xt_mm2"], o + 1)
            copy(x_t[0:D, :].rearrange("p (a b) -> p a b", a=2), bank[0][0:D, :, :]).then_inc(s["xt_c"], 1)
            act.wait_ge(s["qk_mm"], o + 1)
            copy(q[:].rearrange("p (a b) -> p a b", a=2), bank[1][:, :, :]).then_inc(s["q_c"], 1)
            act.wait_ge(s["val_mm"], o + 1)
            copy(val[:, 0:8, :].rearrange("p a b -> p (a b)").rearrange("p (a b) -> p a b", a=2), bank[3][0:S, :, :])
            copy(val[:, 8:16, :].rearrange("p a b -> p (a b)").rearrange("p (a b) -> p a b", a=2), bank[0][0:S, :, :]
                 ).then_inc(s["val_c"], 1)
            act.wait_ge(s["shifted"], o + 1)
            av = att[:].rearrange("p h n t -> p (h n t)")
            f.activation(av, av, ACT.Exp, scale=float(HD) ** -0.5).then_inc(s["exp_c"], 1)
            act.wait_ge(s["at_mm0"], o + 1)
            copy(att_t[:, 0:2, :, :].rearrange("p a h t -> p (a h t)").rearrange("p (a b) -> p a b", a=2),
                 bank[3][0:S, :, :])
            copy(att_t[:, 2:4, :, :].rearrange("p a h t -> p (a h t)").rearrange("p (a b) -> p a b", a=2),
                 bank[0][0:S, :, :]).then_inc(s["at_c0"], 1)
            act.wait_ge(s["ctx_mm"], o + 1)
            copy(ctx_t[:].rearrange("p (a b) -> p a b", a=2), bank[0][:, :, :]).then_inc(s["ctx_c"], 1)
            estimate(s["b_var"], s["b_rs"], o * 3 + 3)
            act.wait_ge(s["x5t_mm"], o + 1)
            copy(x_t[0:D, :].rearrange("p (a b) -> p a b", a=2), bank[0][0:D, :, :]).then_inc(s["x5t_c"], 1)
            for c in range(2):
                act.wait_ge(s["hid_mm"], o * 2 + c + 1)
                for n in range(2):
                    m = f.activation(hid[:, c, n, :], bk(2 - 2 * c + n), ACT.Gelu_apprx_tanh, bias=fb1[:, n:n + 1])
                m.then_inc(s["hid_c"], 1)


def vision_tower(nc, a, out):
    tokens = nc.dram_tensor("tokens", (NIMG, PIX), F32, kind="Internal").ap()
    a["scr_x"] = nc.dram_tensor("scr_x", (BI, C, XM), F32, kind="Internal").ap()
    a["scr_y"] = nc.dram_tensor("scr_y", (BI, C, XM), F32, kind="Internal").ap()
    a["scr_p"] = nc.dram_tensor("scr_p", (NIMG, S, HEADS * S), F32, kind="Internal").ap()
    with ExitStack() as ctx:
        tokenizer(nc, ctx, a, tokens, NIMG // BI)
    with ExitStack() as ctx:
        attention_and_ffn(nc, ctx, a, tokens, out)


def kernel(**inputs):
    import concourse.bacc as bacc
    from concourse.bass_utils import run_bass_kernel_spmd

    nc = bacc.Bacc("TRN2", target_bir_lowering=False, num_devices=1)
    arrays, aps = {}, {}
    given = {n: np.ascontiguousarray(v) for n, v in inputs.items()}
    for name, array in {**given, **constants(), **attention_constants()}.items():
        arrays[f"in_{name}"] = array
        aps[name] = nc.dram_tensor(f"in_{name}", array.shape, mybir.dt.from_np(array.dtype), kind="ExternalInput").ap()
    out = nc.dram_tensor("out_0", (NIMG, S, S), F32, kind="ExternalOutput").ap()
    vision_tower(nc, aps, out)
    r = run_bass_kernel_spmd(nc, [arrays], core_ids=[0])
    return r.results[0]["out_0"]
```

```python
from contextlib import ExitStack

import numpy as np

import concourse.bass as bass
from concourse import mybir

F32 = mybir.dt.float32
BF16 = mybir.dt.bfloat16
ALU = mybir.AluOpType
ACT = mybir.ActivationFunctionType
AX_X = mybir.AxisListType.X

P = 128
NIMG = 128
S = 64
PIX = S * S
C = 32
IG = P // C
G = 4
BI = G * IG
LAYERS = 4
M1 = M2 = 12
MODES = M1 * M2
HR = 4
XM = HR * MODES
NORMS = LAYERS + 1
HID1, HID2 = 128, 64
EPS = 1e-5
CH = 512
NCH = PIX // CH
NXP = PIX // P
RO = 8
PARTS = 3


def wait_alone(engine, semaphore, value, passed):
    engine.wait_ge(semaphore, value)
    engine.sem_inc(passed, 1)


def constants():
    f8 = np.float64
    kx = np.concatenate([np.arange(M1), np.arange(-M1, 0)]).reshape(2, M1)
    x = np.arange(S)
    th_x = 2 * np.pi * (kx[:, :, None] * x[None, None, :]) / S
    th_y = 2 * np.pi * np.outer(np.arange(M2), x) / S
    cosx, sinx, cosy, siny = np.cos(th_x), np.sin(th_x), np.cos(th_y), np.sin(th_y)
    two = np.eye(2)
    dft_y = np.zeros((2, S, 2, M2, 2), f8)
    for a in range(2):
        dft_y[a, :, a, :, 0] = cosy.T
        dft_y[a, :, a, :, 1] = -siny.T
    dft_x = np.zeros((S, 2, 2, 2, M1), f8)
    for h in range(2):
        c, s = cosx[h].T, sinx[h].T
        dft_x[:, 0, h, 0], dft_x[:, 1, h, 0] = c, s
        dft_x[:, 0, h, 1], dft_x[:, 1, h, 1] = -s, c
    idft_x = np.zeros((2, 2, M1, 2, S, 2, 2), f8)
    for h in range(2):
        for k in range(2):
            c, s = cosx[h], sinx[h]
            idft_x[h, 0, :, k, :, k, 0], idft_x[h, 1, :, k, :, k, 0] = c, -s
            idft_x[h, 0, :, k, :, k, 1], idft_x[h, 1, :, k, :, k, 1] = s, c
    w = np.where(np.arange(M2) == 0, 1.0, 2.0)[:, None] / PIX
    idft_y = np.zeros((4, M2, 2, 4, S), f8)
    for a in range(4):
        idft_y[a, :, 0, a] = w * cosy
        idft_y[a, :, 1, a] = -w * siny
    blk = np.kron(np.eye(IG), np.ones((C, 1)))
    centre = np.kron(np.eye(IG), np.eye(C) - 1.0 / C)
    ones_v = blk[:, np.arange(32) % IG] / C
    sel = np.zeros((4, 32, 4, IG, C))
    for q in range(4):
        for n in range(PARTS * IG):
            sel[q, n, q, n % IG, :] = 1
    row = np.arange(P) % 32
    minus = np.stack([-(row >= IG).astype(f8) * (row < 3 * IG), -((row >= 2 * IG) & (row < 3 * IG)).astype(f8)], 1)
    fmask = np.zeros((IG, RO, 3, RO, IG))
    for i in range(IG):
        for r in range(RO):
            fmask[i, r, :, r, i] = 1
    mask2 = np.zeros((2, HID2, 32))
    for i in range(2):
        mask2[i, :, i] = 1
    out = dict(k_ident=np.eye(P), k_dft_y=dft_y.reshape(P, 48), k_dft_x=dft_x.reshape(P, 48),
               k_idft_x=idft_x.reshape(96, 256), k_idft_y=idft_y.reshape(96, 256), k_blk=blk, k_centre=centre,
               k_ones_v=ones_v, k_sel=sel.reshape(P, 4 * P), k_minus=minus, k_fmask=fmask.reshape(96, RO * IG),
               k_mask2=mask2.reshape(P, 32))
    return {k: np.ascontiguousarray(v, np.float32) for k, v in out.items()}


def tokenizer(nc, ctx, a, tokens, batches):
    def sb(name, shape, dt=F32):
        return ctx.enter_context(nc.sbuf_tensor(name, shape, dt))

    def sem(name):
        return ctx.enter_context(nc.semaphore(name))

    bank = [ctx.enter_context(nc.psum_tensor(f"bank{i}", [P, 2, CH], F32)) for i in range(4)]

    def bk(n):
        return bank[n // 2][:, n % 2, :]

    h = sb("h", [P, G, PIX])
    mix_w = sb("mix_w", [P, 2, C, MODES])
    xm = sb("xm", [P, 2, BI, MODES])
    ym = sb("ym", [2 * C, 2, BI, MODES])
    th = sb("th", [P, 4, CH])
    ya = sb("ya", [P, M2, S, 2])
    xa = sb("xa", [P, M2, P])
    xg = sb("xg", [P, HR, M1, M2])
    yg = sb("yg", [P, 2, HR * M1, M2])
    yr = sb("yr", [P, M2 // 2, HR * M1, 2])
    yt = sb("yt", [96, M2 // 2, P])
    zx = sb("zx", [P, S, M2 * 2])
    zt = sb("zt", [96, S // 4, P])
    sq = sb("sq", [P, 2, 2 * CH])
    rstd = sb("rstd", [P, 2, CH])
    newt = sb("newt", [P, 2, CH])
    newt_high = newt[:].bitcast(BF16).rearrange("p a (n e) -> p a n e", e=2)[:, :, :, 1]
    high = rstd[:].bitcast(BF16).rearrange("p a (n e) -> p a n e", e=2)[:, :, :, 1]
    xin = sb("xin", [P, G, IG, 32 * 3])
    xr = sb("xr", [P, 4, IG, 3 * RO])
    xt = sb("xt", [96, 4, P])
    g1, g2 = sq, th
    tok = zx[:].rearrange("p a b -> p (a b)")[:, 0:2 * CH].rearrange("p (a b) -> p a b", a=2)
    ident = sb("ident", [P, P])
    dft_y, dft_x = sb("dft_y", [P, 48]), sb("dft_x", [P, 48])
    idft_x, idft_y = sb("idft_x", [96, 256]), sb("idft_y", [96, 256])
    blk, centre = sb("blk", [P, IG]), sb("centre", [P, P])
    ones_v, minus = sb("ones_v", [P, 32]), sb("minus", [P, 2])
    selb = sb("selb", [P, 4, P], BF16)
    f0, f1, f2 = sb("f0", [96, RO, P]), sb("f1", [P, IG, HID1]), sb("f2", [P, HID2])
    f3 = sb("f3", [P, 32])
    conv = sb("conv", [P, LAYERS, P])
    cb = sb("cb", [P, NORMS])
    gam, bet = sb("gam", [P, NORMS]), sb("bet", [P, NORMS])
    b1, b2, b3 = sb("b1", [P, 1]), sb("b2", [P, 1]), sb("b3", [P, 1])
    epst = sb("epst", [P, 1])
    conv_l = sb("conv_l", [P, P])
    cb_l, gb_l = sb("cb_l", [P, 1]), sb("gb_l", [P, 2])
    zf = zx[:].rearrange("p a b -> p (a b)")
    sel_f, fmask, mask2 = zf[:, 0:512], zf[0:96, 512:544], zf[:, 544:576]
    f0_rep, f1_rep, conv_rep = zf[0:96, 576:608], zf[:, 608:736], zf[:, 736:864]
    cb_raw, f3_rep, f0_sum = zf[:, 864:869], zf[:, 869:870], zf[0:96, 870:871]
    conv_bd = xa[:, 0:LAYERS, :]

    scr_x = a["scr_x"]
    scr_y = a["scr_y"]

    setup_in, setup_v, setup_mm = sem("setup_in"), sem("setup_v"), sem("setup_mm")
    pe_passed = sem("pe_passed")
    setup_g, eps_set, conv_in = sem("setup_g"), sem("eps_set"), sem("conv_in")
    x_in = sem("x_in")
    xr_cp, yr_cp = sem("xr_cp"), sem("yr_cp")
    xt_mm, xt_cp = sem("xt_mm"), sem("xt_cp")
    t_mm, t_cp, a_mm, a_cp = sem("t_mm"), sem("t_cp"), sem("a_mm"), sem("a_cp")
    t2_mm, t2_cp, b_mm, b_cp = sem("t2_mm"), sem("t2_cp"), sem("b_mm"), sem("b_cp")
    xg_out, xm_in, w_in, w_neg = sem("xg_out"), sem("xm_in"), sem("w_in"), sem("w_neg")
    xm_zero = sem("xm_zero")
    mix_mm, mix_v, mix_a = sem("mix_mm"), sem("mix_v"), sem("mix_a")
    ym_out, yg_in = sem("ym_out"), [sem("yg_in0"), sem("yg_in1")]
    yt_mm, yt_cp, d_mm, d_cp = sem("yt_mm"), sem("yt_cp"), sem("d_mm"), sem("d_cp")
    zt_mm, zt_cp = sem("zt_mm"), sem("zt_cp")
    y_mm, y_cp, sq_done, var_mm = sem("y_mm"), sem("y_cp"), sem("sq_done"), sem("var_mm")
    rs_done, st_done, bc_mm, z_done, h_done = (sem("rs_done"), sem("st_done"), sem("bc_mm"), sem("z_done"),
                                               sem("h_done"))
    gb_in = sem("gb_in")
    m1_mm, m1_done, m2_mm, m2_done = sem("m1_mm"), sem("m1_done"), sem("m2_mm"), sem("m2_done")
    m3_mm, m3_cp, tok_out = sem("m3_mm"), sem("m3_cp"), sem("tok_out")

    NT, NA, NT2, NB = NCH, 4, 3, 2
    MC = CH // (2 * BI)
    NMIX = MODES // MC
    NMV, NMA = (NMIX + 1) // 2, NMIX // 2
    NY, ND, NZ = 2, 3, 4
    NST = 5
    NM = 2 * NCH

    block = ctx.enter_context(nc.Block())

    @block.sync
    def _(sp):
        consts = [(ident, "k_ident"), (dft_y, "k_dft_y"), (dft_x, "k_dft_x"), (idft_x, "k_idft_x"),
                  (idft_y, "k_idft_y"), (blk, "k_blk"), (centre, "k_centre"), (ones_v, "k_ones_v"),
                  (minus, "k_minus")]
        for t, n in consts:
            sp.dma_start(t[:], a[n]).then_inc(setup_in, 16)
        views = [(sel_f, a["k_sel"]), (fmask, a["k_fmask"]), (mask2, a["k_mask2"]), (f2[:], a["L0_tok_fc2_w"])]
        for t, v in views:
            sp.dma_start(t, v).then_inc(setup_in, 16)
        col = lambda v: v.rearrange("(c o) -> c o", o=1)
        with nc.allow_non_contiguous_dma(reason="a few small weights"):
            for i in range(IG):
                rows = slice(C * i, C * (i + 1))
                sp.dma_start(f1_rep[rows, :], a["L0_tok_fc1_w"]).then_inc(setup_in, 16)
                sp.dma_start(conv_rep[rows, :].rearrange("o (l c) -> o l c", l=LAYERS),
                             a["L0_tok_conv_w"].rearrange("l o c -> o l c")).then_inc(setup_in, 16)
                sp.dma_start(cb_raw[rows, 0:1], col(a["L0_tok_fc0_b"])).then_inc(setup_in, 16)
                sp.dma_start(cb_raw[rows, 1:NORMS], a["L0_tok_conv_b"].rearrange("l c -> c l")).then_inc(setup_in, 16)
                sp.dma_start(gam[rows, 0:1], col(a["L0_tok_ln0_g"])).then_inc(setup_in, 16)
                sp.dma_start(bet[rows, 0:1], col(a["L0_tok_ln0_b"])).then_inc(setup_in, 16)
                sp.dma_start(gam[rows, 1:NORMS], a["L0_tok_ln_g"].rearrange("l c -> c l")).then_inc(setup_in, 16)
                sp.dma_start(bet[rows, 1:NORMS], a["L0_tok_ln_b"].rearrange("l c -> c l")).then_inc(setup_in, 16)
            for n in range(IG * RO):
                sp.dma_start(f0_rep[3 * n:3 * n + 3, :], a["L0_tok_fc0_w"]).then_inc(setup_in, 16)
            for i in range(2):
                rows = slice(HID2 * i, HID2 * (i + 1))
                sp.dma_start(f3_rep[rows, :], a["L0_tok_fc3_w"]).then_inc(setup_in, 16)
                sp.dma_start(b2[rows, :], col(a["L0_tok_fc2_b"])).then_inc(setup_in, 16)
            sp.dma_start(b1[:], col(a["L0_tok_fc1_b"])).then_inc(setup_in, 16)
            sp.dma_start(b3[:], a["L0_tok_fc3_b"].rearrange("(a b) -> a b", a=1).broadcast_to([P, 1])
                         ).then_inc(setup_in, 16)

        def load_mix(layer):
            for half, (wr, wi) in enumerate((("L0_tok_w1r", "L0_tok_w1i"), ("L0_tok_w2r", "L0_tok_w2i"))):
                for ri, pair in enumerate(((wr, wi), (wi, wr))):
                    rows = slice(64 * half + 32 * ri, 64 * half + 32 * ri + 32)
                    for ro in range(2):
                        sp.dma_start(mix_w[rows, ro, :, :], a[pair[ro]][layer].rearrange("i o x y -> i o (x y)")
                                     ).then_inc(w_in, 16)

        def layer_dmas(L, it, nxt):
            for g in range(G):
                sp.wait_ge(b_cp, L * (G * NB) + (g + 1) * NB)
                sp.dma_start(scr_x[IG * g:IG * (g + 1)].rearrange("i c m -> (i c) m"),
                             xg[:].rearrange("p a b c -> p (a b c)")).then_inc(xg_out, 16)
                sp.wait_ge(xg_out, L * (G * 16) + (g + 1) * 16)
                for hr in range(HR):
                    sp.dma_start(xm[C * hr:C * (hr + 1), hr // 2, IG * g:IG * (g + 1), :],
                                 scr_x[IG * g:IG * (g + 1), :, MODES * hr:MODES * (hr + 1)]
                                 .rearrange("i c m -> c i m")).then_inc(xm_in, 16)
            sp.wait_ge(mix_v, L * NMV + NMV)
            sp.wait_ge(mix_a, L * NMA + NMA)
            for hr in range(HR):
                sp.dma_start(scr_y[:, :, MODES * hr:MODES * (hr + 1)].rearrange("i c m -> c i m"),
                             ym[C * (hr % 2):C * (hr % 2 + 1), hr // 2, :, :]).then_inc(ym_out, 16)
            sp.wait_ge(ym_out, L * (HR * 16) + HR * 16)
            for g in range(G):
                if g >= 2:
                    sp.wait_ge(yr_cp, L * G + g - 1)
                sp.dma_start(yg[:, g % 2, :, :], scr_y[IG * g:IG * (g + 1)].rearrange("i c (n y) -> (i c) n y", y=M2)
                             ).then_inc(yg_in[g % 2], 16)
                if g == 1:
                    load_mix(nxt)

        load_mix(0)
        sp.wait_ge(xm_zero, 1)
        with sp.Fori(0, batches) as it:
            for g in range(G):
                sp.dma_start(xin[:, g, :, :], a["x"][bass.ds(it * BI + g * IG, IG)]
                             .rearrange("i x y c -> i (x y c)").rearrange("i (q r) -> q i r", q=P)).then_inc(x_in, 16)
            with sp.Fori(0, LAYERS - 1) as l:
                layer_dmas(it * LAYERS + l, it, l + 1)
            layer_dmas(it * LAYERS + LAYERS - 1, it, 0)
            for g in range(G):
                for u in range(2):
                    sp.wait_ge(m3_cp, it * (G * 2) + g * 2 + u + 1)
                    for i in range(2):
                        sp.dma_start(tokens[it * BI + g * IG + 2 * u + i].rearrange("(b q n) -> q b n", b=2, q=4),
                                     tok[i:i + 97:32, :, :]).then_inc(tok_out, 16)
        sp.wait_ge(tok_out, batches * (G * 4) * 16)
        sp.wait_ge(w_in, (batches * LAYERS + 1) * 8 * 16)

    @block.tensor
    def _(pe):
        mm = nc.tensor.matmul
        nset = 13 + 8 * IG + IG * RO + 4 + 2
        pe.wait_ge(setup_in, nset * 16)
        pe.wait_ge(setup_v, 5)
        for layer in range(LAYERS):
            mm(bk(0)[:, P * layer:P * (layer + 1)], conv_bd[:, layer, :], centre[:], start=True, stop=True)
        mm(bk(1)[:, 0:NORMS], centre[:], cb_raw, start=True, stop=True).then_inc(setup_mm, 1)
        pe.wait_ge(setup_v, 7)

        def variance(M, g, n):
            pe.wait_ge(sq_done, M * (G * 4) + g * 4 + n + 1)
            for k in (2 * n, 2 * n + 1):
                q = k % 4
                m = mm(bk(2 + k // 4)[32 * q:32 * q + 32, :], ones_v[:], sq[:, n % 2, CH * (k % 2):CH * (k % 2 + 1)],
                       start=True, stop=True)
            m.then_inc(var_mm, 1)

        def spread(M, g, k):
            if k == 0:
                pe.wait_ge(st_done, M * (G * NST) + (g + 1) * NST)
            if g or k >= 2:
                pe.wait_ge(z_done, M * (G * NCH) + g * NCH + k - 1)
            mm(bk(4 + k % 2), selb[:, k % 4, :], high[:, k // 4, :], start=True, stop=True).then_inc(bc_mm, 1)

        def norm(M, first, front, product, squares_last):
            first(0)
            for g in range(G):
                front(g)
                for c in range(NCH):
                    if c >= 2:
                        pe.wait_ge(y_cp, M * (G * NCH) + g * NCH + c - 1)
                    product(g, c)
                    if not squares_last and c % 2 and c >= 3:
                        variance(M, g, (c - 3) // 2)
                    if g and c >= 4:
                        spread(M, g - 1, 2 * c - 8)
                        spread(M, g - 1, 2 * c - 7)
                if squares_last:
                    for n in range(3):
                        variance(M, g, n)
                if g < G - 1:
                    first(g + 1)
                variance(M, g, 3)

        def layer_body(L, M, layer_conv):
            def turn(g, c):
                if c == 0:
                    pe.wait_ge(h_done, M * (G * 2) - G * 2 + (g + 1) * 2)
                if g or c >= 2:
                    pe.wait_ge(t_cp, L * (G * NT) + g * NT + c - 1)
                for j in range(4):
                    m = pe.transpose(bk(c % 2)[:, P * j:P * (j + 1)], h[:, g, CH * c + P * j:CH * c + P * (j + 1)],
                                     ident[:])
                m.then_inc(t_mm, 1)

            def along_y(g, c):
                pe.wait_ge(t_cp, L * (G * NT) + g * NT + c + 1)
                if (g or c >= 4) and c % 2 == 0:
                    pe.wait_ge(a_cp, L * (G * NA) + g * NA + c // 2 - 1)
                for j in range(4):
                    o = 48 * (4 * (c % 2) + j)
                    m = mm(bk(6 + (c // 2) % 2)[:, o:o + 48], th[:, c % 4, P * j:P * (j + 1)], dft_y[:],
                           start=True, stop=True)
                if c % 2:
                    m.then_inc(a_mm, 1)

            def along_x(g):
                pe.wait_ge(a_cp, L * (G * NA) + (g + 1) * NA)
                if g == 1:
                    pe.wait_ge(z_done, M * (G * NCH))
                for c in range(NT2):
                    if c >= 2:
                        pe.wait_ge(t2_cp, L * (G * NT2) + g * NT2 + c - 1)
                    for j in range(4):
                        m = pe.transpose(bk(4 + c % 2)[:, P * j:P * (j + 1)],
                                         ya[:, 4 * c + j, :, :].rearrange("p x r -> p (x r)"), ident[:])
                    m.then_inc(t2_mm, 1)
                if g == 0:
                    pe.wait_ge(st_done, M * (G * NST) - NST + 1)
                else:
                    pe.wait_ge(b_cp, L * (G * NB) + g * NB)
                for c in range(NB):
                    pe.wait_ge(t2_cp, L * (G * NT2) + g * NT2 + 2 + c)
                    for j in range(6):
                        m = mm(bk(2 + c)[:, 48 * j:48 * j + 48], xa[:, 6 * c + j, :], dft_x[:], start=True, stop=True)
                    m.then_inc(b_mm, 1)

            turn(0, 0)
            turn(0, 1)
            for g in range(G):
                for c in range(NT):
                    if c < NT - 2:
                        turn(g, c + 2)
                    along_y(g, c)
                    if g == 1:
                        spread(M - 1, G - 1, c)
                if g < G - 1:
                    turn(g + 1, 0)
                    turn(g + 1, 1)
                along_x(g)
            pe.wait_ge(xm_in, L * (G * HR * 16) + G * HR * 16)
            wait_alone(pe, w_neg, L * 2 + 2, pe_passed)
            for c in range(NMIX):
                if c >= 4:
                    n = c - 4
                    if n % 2:
                        pe.wait_ge(mix_a, L * NMA + n // 2 + 1)
                    else:
                        pe.wait_ge(mix_v, L * NMV + n // 2 + 1)
                for j in range(MC):
                    m = mm(bk(c % 4)[0:2 * C, 2 * BI * j:2 * BI * (j + 1)],
                           mix_w[:, :, :, c * MC + j].rearrange("p a b -> p (a b)"),
                           xm[:, :, :, c * MC + j].rearrange("p a b -> p (a b)"), start=True, stop=True)
                m.then_inc(mix_mm, 1)

            def first(g):
                pe.wait_ge(yr_cp, L * G + g + 1)
                for c in range(NY):
                    for j in range(3):
                        m = mm(bk(6 + c)[0:96, P * j:P * (j + 1)],
                               yr[:, 3 * c + j, :, :].rearrange("p a b -> p (a b)"), centre[:], start=True, stop=True)
                    m.then_inc(yt_mm, 1)

            def front(g):
                for c in range(ND):
                    pe.wait_ge(yt_cp, L * (G * NY) + g * NY + (2 * c + 1) // 3 + 1)
                    if c >= 2:
                        pe.wait_ge(d_cp, L * (G * ND) + g * ND + c - 1)
                    elif g and c == 0:
                        pe.wait_ge(y_cp, M * (G * NCH) + g * NCH)
                    for j in range(2):
                        m = mm(bk(c % 2)[:, 256 * j:256 * j + 256], yt[:, 2 * c + j, :], idft_x[:],
                               start=True, stop=True)
                    m.then_inc(d_mm, 1)
                pe.wait_ge(d_cp, L * (G * ND) + (g + 1) * ND)
                for c in range(NZ):
                    if c >= 2:
                        pe.wait_ge(zt_cp, L * (G * NZ) + g * NZ + c - 1)
                    for j in range(4):
                        k = 4 * c + j
                        m = pe.transpose(bk(6 + c % 2)[0:96, P * j:P * (j + 1)],
                                         zx[:, 4 * k:4 * k + 4, :].rearrange("p x r -> p (x r)"), ident[:])
                    m.then_inc(zt_mm, 1)

            def product(g, c):
                mm(bk(c % 2), layer_conv, h[:, g, CH * c:CH * (c + 1)], start=True, stop=False)
                pe.wait_ge(zt_cp, L * (G * NZ) + g * NZ + c // 2 + 1)
                for j in range(2):
                    m = mm(bk(c % 2)[:, 256 * j:256 * j + 256], zt[:, 2 * c + j, :], idft_y[:],
                           start=False, stop=(j == 1))
                m.then_inc(y_mm, 1)

            norm(M, first, front, product, False)

        with pe.Fori(0, batches) as it:
            M0 = it * NORMS

            def first0(g):
                pe.wait_ge(xr_cp, it * G + g + 1)
                for o in range(4):
                    m = pe.transpose(bk(6)[0:96, P * o:P * (o + 1)], xr[:, o, :, :].rearrange("p i r -> p (i r)"),
                                     ident[:])
                m.then_inc(xt_mm, 1)

            def product0(g, c):
                if c == 0:
                    pe.wait_ge(xt_cp, it * G + g + 1)
                for j in range(4):
                    r = 4 * c + j
                    m = mm(bk(c % 2)[:, P * j:P * (j + 1)], f0[:, r % RO, :], xt[:, r // RO, :],
                           start=True, stop=True)
                m.then_inc(y_mm, 1)

            norm(M0, first0, lambda g: None, product0, True)
            with pe.Fori(0, LAYERS) as l:
                pe.wait_ge(conv_in, it * LAYERS + l + 1)
                layer_body(it * LAYERS + l, it * NORMS + l + 1, conv_l[:])

            for g in range(G):
                if g == 1:
                    for k in range(NCH):
                        spread(it * NORMS + LAYERS, G - 1, k)
                    pe.wait_ge(z_done, (it * NORMS + NORMS) * (G * NCH))
                pe.wait_ge(h_done, (it * NORMS + LAYERS) * (G * 2) + (g + 1) * 2)
                for n in range(NM + 2):
                    if n < NM:
                        u, k = divmod(n, NCH)
                        if n >= 2:
                            pe.wait_ge(m1_done, it * (G * NM) + g * NM + n - 1)
                        if g == 0 and n == 1:
                            pe.wait_ge(st_done, (it * NORMS + NORMS) * (G * NST) - NST + 1)
                        for i in range(2):
                            m = mm(bk(2 * (n % 2) + i), f1[:, 2 * u + i, :], h[:, g, CH * k:CH * (k + 1)],
                                   start=True, stop=True)
                        m.then_inc(m1_mm, 1)
                    if 1 <= n <= NM:
                        b = n - 1
                        pe.wait_ge(m1_done, it * (G * NM) + g * NM + b + 1)
                        if g or b >= 2:
                            pe.wait_ge(m2_done, it * (G * NM) + g * NM + b - 1)
                        for i in range(2):
                            m = mm(bk(4 + b % 2)[64 * i:64 * i + 64, :], f2[:], g1[:, b % 2, CH * i:CH * (i + 1)],
                                   start=True, stop=True)
                        m.then_inc(m2_mm, 1)
                    if n >= 2:
                        b = n - 2
                        u, k = divmod(b, NCH)
                        pe.wait_ge(m2_done, it * (G * NM) + g * NM + b + 1)
                        if k == 0 and (g or u):
                            pe.wait_ge(m3_cp, it * (G * 2) + g * 2 + u)
                        q = k % 4
                        m = mm(bk(6 + k // 4)[32 * q:32 * q + 32, :], f3[:], g2[:, b % 2, :], start=True, stop=True)
                        if k == NCH - 1:
                            m.then_inc(m3_mm, 1)
            pe.wait_ge(m3_cp, it * (G * 2) + G * 2)

    @block.vector
    def _(dve):
        v = nc.vector
        nset = 13 + 8 * IG + IG * RO + 4 + 2
        dve.wait_ge(setup_in, nset * 16)
        v.tensor_copy(selb[:].rearrange("p a b -> p (a b)"), sel_f).then_inc(setup_v, 1)
        v.tensor_tensor(f1[:], f1_rep.rearrange("p (a n) -> p a n", a=1).broadcast_to([P, IG, HID1]),
                        blk[:].rearrange("p (a n) -> p a n", n=1).broadcast_to([P, IG, HID1]), ALU.mult
                        ).then_inc(setup_v, 1)
        v.tensor_tensor(f3[:], mask2, f3_rep.broadcast_to([P, 32]), ALU.mult).then_inc(setup_v, 1)
        for i in range(IG):
            m = v.tensor_scalar(conv_bd[:, :, C * i:C * (i + 1)], conv_rep.rearrange("p (l c) -> p l c", l=LAYERS),
                                blk[:, i:i + 1], None, ALU.mult)
        m.then_inc(setup_v, 1)
        v.reduce_sum(f0_sum, f0_rep, AX_X).then_inc(setup_v, 1)
        dve.wait_ge(setup_v, 5)
        v.scalar_tensor_tensor(out=f0_rep, in0=f0_sum.broadcast_to([96, C]), scalar=-1.0 / C, in1=f0_rep,
                               op0=ALU.mult, op1=ALU.add).then_inc(setup_g, 1)
        dve.wait_ge(setup_g, 1)
        v.tensor_tensor(f0[:].rearrange("p r (i c) -> p (r i) c", i=IG),
                        f0_rep.rearrange("p (a c) -> p a c", a=1).broadcast_to([96, RO * IG, C]),
                        fmask.rearrange("p (n a) -> p n a", a=1).broadcast_to([96, RO * IG, C]), ALU.mult
                        ).then_inc(setup_g, 1)
        v.memset(xm[:].rearrange("p a b c -> p (a b c)"), 0.0).then_inc(xm_zero, 1)
        dve.wait_ge(setup_mm, 1)
        v.tensor_copy(conv[:].rearrange("p a b -> p (a b)"), bk(0)).then_inc(setup_v, 1)
        v.tensor_copy(cb[:], bk(1)[:, 0:NORMS]).then_inc(setup_v, 1)
        dve.wait_ge(setup_v, 7)
        dve.wait_ge(setup_g, 2)

        def stat_step(M, g, n):
            if n == 0:
                dve.wait_ge(rs_done, M * G + g + 1)
                m = v.scalar_tensor_tensor(out=newt[:], in0=bank[1][:, :, :], scalar=EPS, in1=rstd[:], op0=ALU.add,
                                           op1=ALU.mult)
            else:
                dve.wait_ge(st_done, M * (G * NST) + g * NST + n)
            if n == 1:
                m = v.scalar_tensor_tensor(out=newt[:], in0=newt[:], scalar=-0.5, in1=rstd[:], op0=ALU.mult,
                                           op1=ALU.mult)
            elif n == 2:
                m = v.scalar_tensor_tensor(out=rstd[:], in0=newt[:], scalar=1.5, in1=rstd[:], op0=ALU.add, op1=ALU.mult)
            elif n == 3:
                m = v.scalar_tensor_tensor(out=newt[:], in0=high, scalar=minus[:, 0:1], in1=rstd[:], op0=ALU.mult,
                                           op1=ALU.add)
            elif n == 4:
                m = v.scalar_tensor_tensor(out=rstd[:], in0=newt_high, scalar=minus[:, 1:2], in1=newt[:], op0=ALU.mult,
                                           op1=ALU.add)
            m.then_inc(st_done, 1)

        def scale(M, g, k):
            dve.wait_ge(bc_mm, M * (G * NCH) + g * NCH + k + 1)
            hc = h[:, g, CH * k:CH * (k + 1)]
            v.tensor_tensor(hc, bk(4 + k % 2), hc, ALU.mult).then_inc(z_done, 1)

        def norm(M, front, copy_out):
            for g in range(G):
                front(g)
                if g:
                    stat_step(M, g - 1, 0)
                    stat_step(M, g - 1, 1)
                for c in range(NCH):
                    dve.wait_ge(y_mm, M * (G * NCH) + g * NCH + c + 1)
                    copy_out(g, c).then_inc(y_cp, 1)
                    if g and c + 2 < NST:
                        stat_step(M, g - 1, c + 2)
                    if g and c >= 4:
                        scale(M, g - 1, 2 * c - 8)
                        scale(M, g - 1, 2 * c - 7)

        def layer_body(L, M, bias):
            for g in range(G):
                for c in range(NT):
                    dve.wait_ge(t_mm, L * (G * NT) + g * NT + c + 1)
                    v.tensor_copy(th[:, c % 4, :], bk(c % 2)).then_inc(t_cp, 1)
                    if g == 0 and 0 <= c - 2 < NST:
                        stat_step(M - 1, G - 1, c - 2)
                    if g == 1 and c >= 2:
                        scale(M - 1, G - 1, c - 2)
                if g == 1:
                    scale(M - 1, G - 1, NCH - 2)
                    scale(M - 1, G - 1, NCH - 1)
                if g < G - 1:
                    pass
                for c in range(NB):
                    dve.wait_ge(b_mm, L * (G * NB) + g * NB + c + 1)
                    if g and c == 0:
                        dve.wait_ge(xg_out, L * (G * 16) + g * 16)
                    v.tensor_copy(xg[:, :, :, 6 * c:6 * c + 6].rearrange("p h x y -> p y h x"),
                                  bk(2 + c)[:, 0:288].rearrange("p (y h x) -> p y h x", y=6, h=HR)
                                  ).then_inc(b_cp, 1)
                if g == 1:
                    dve.wait_ge(w_in, L * (8 * 16) + 8 * 16)
                    for half in range(2):
                        rows = slice(64 * half + 32, 64 * half + 64)
                        v.tensor_scalar(mix_w[rows, 0, :, :], mix_w[rows, 0, :, :], -1.0, None, ALU.mult
                                        ).then_inc(w_neg, 1)
            for c in range(0, NMIX, 2):
                dve.wait_ge(mix_mm, L * NMIX + c + 1)
                v.tensor_copy(ym[:, :, :, c * MC:(c + 1) * MC].rearrange("p h i m -> p m (h i)"),
                              bk(c % 4)[0:2 * C, :].rearrange("p (m i) -> p m i", m=MC)).then_inc(mix_v, 1)

            def front(g):
                dve.wait_ge(yg_in[g % 2], L * 32 + (g // 2 + 1) * 16)
                if g:
                    dve.wait_ge(yt_mm, L * (G * NY) + g * NY)
                v.tensor_copy(yr[:], yg[:, g % 2, :, :].rearrange("p n (k y) -> p k n y", y=2)).then_inc(yr_cp, 1)
                for c in range(ND):
                    dve.wait_ge(d_mm, L * (G * ND) + g * ND + c + 1)
                    v.tensor_copy(zx[:, :, 8 * c:8 * c + 8].rearrange("p x (k f) -> p k x f", k=2),
                                  bk(c % 2).rearrange("p (k x f) -> p k x f", k=2, x=S)).then_inc(d_cp, 1)

            norm(M, front, lambda g, c: v.tensor_scalar(h[:, g, CH * c:CH * (c + 1)], bk(c % 2), bias, None, ALU.add))

        with dve.Fori(0, batches) as it:
            norm(it * NORMS, lambda g: None,
                 lambda g, c: v.tensor_scalar(
                     h[:, g, :].rearrange("p (q r) -> p r q", r=32)[:, 4 * c:4 * c + 4, :],
                     bk(c % 2).rearrange("p (r q) -> p r q", r=4), cb[:, 0:1], None, ALU.add))
            with dve.Fori(0, LAYERS) as l:
                dve.wait_ge(conv_in, it * LAYERS + l + 1)
                layer_body(it * LAYERS + l, it * NORMS + l + 1, cb_l[:, 0:1])
            for n in range(NST):
                stat_step(it * NORMS + LAYERS, G - 1, n)
            for g in range(G):
                if g == 1:
                    for k in range(NCH):
                        scale(it * NORMS + LAYERS, G - 1, k)
                for u in range(2):
                    n = g * 2 + u
                    dve.wait_ge(m3_mm, it * (G * 2) + n + 1)
                    if n:
                        dve.wait_ge(tok_out, it * (G * 2 * 32) + n * 32)
                    v.tensor_scalar(tok, bank[3][:, :, :], b3[:, 0:1], None, ALU.add).then_inc(m3_cp, 1)
            dve.wait_ge(tok_out, it * (G * 2 * 32) + G * 2 * 32)

    @block.scalar
    def _(act):
        s = nc.scalar
        nset = 13 + 8 * IG + IG * RO + 4 + 2
        act.wait_ge(setup_in, nset * 16)
        s.activation(epst[:], ident[:, 0:1], ACT.Copy, bias=EPS, scale=0.0).then_inc(eps_set, 1)
        act.wait_ge(eps_set, 1)
        act.wait_ge(setup_v, 7)

        def copy(dst, src):
            return s.activation(dst, src, ACT.Copy)

        def estimate(M, g):
            act.wait_ge(var_mm, M * (G * 4) + (g + 1) * 4)
            s.activation(rstd[:], bank[1][:, :, :], ACT.Abs_reciprocal_sqrt, bias=epst[:, 0:1]).then_inc(rs_done, 1)

        def final(M, g, n, func, gamma, beta):
            act.wait_ge(z_done, M * (G * NCH) + g * NCH + 4 * n + 4)
            hh = h[:, g, 2048 * n:2048 * (n + 1)]
            s.activation(hh, hh, func, bias=beta, scale=gamma).then_inc(h_done, 1)

        def norm(M, front, rest, func, gamma, beta, squares_last):
            for g in range(G):
                front(g)
                if g:
                    estimate(M, g - 1)
                rest(g)
                for n in range(4):
                    act.wait_ge(y_cp, M * (G * NCH) + g * NCH + (NCH if squares_last else 2 * n + 2))
                    if n >= 2:
                        act.wait_ge(var_mm, M * (G * 4) + g * 4 + n - 1)
                    s.activation(sq[:, n % 2, :], h[:, g, 1024 * n:1024 * (n + 1)], ACT.Square).then_inc(sq_done, 1)
                    if g and n >= 2:
                        final(M, g - 1, n - 2, func, gamma, beta)

        def layer_weights(L, l, M):
            act.wait_ge(y_cp, M * (G * NCH))
            copy(conv_l[:], conv[:, l, :] if isinstance(l, int) else
                 conv[:, bass.ds(l, 1), :].rearrange("p a b -> p (a b)"))
            copy(cb_l[:], cb[:, l + 1:l + 2] if isinstance(l, int) else cb[:, bass.ds(l + 1, 1)]).then_inc(conv_in, 1)

        def layer_body(L, l, M, pending, func):
            layer_weights(L, l, M)
            estimate(M - 1, G - 1)
            for g in range(G):
                for c in range(NA):
                    act.wait_ge(a_mm, L * (G * NA) + g * NA + c + 1)
                    copy(ya[:, :, 16 * c:16 * c + 16, :].rearrange("p k x r -> p x k r"),
                         bk(6 + c % 2)[:, 0:384].rearrange("p (x k r) -> p x k r", x=16, k=M2)).then_inc(a_cp, 1)
                for c in range(NT2):
                    act.wait_ge(t2_mm, L * (G * NT2) + g * NT2 + c + 1)
                    copy(xa[:, 4 * c:4 * c + 4, :].rearrange("p a b -> p (a b)"), bk(4 + c % 2)).then_inc(t2_cp, 1)
                if g == 1:
                    final(M - 1, G - 1, 0, *pending)
                    final(M - 1, G - 1, 1, *pending)
                    act.wait_ge(h_done, M * (G * 2))
                    for n, t in enumerate((gam, bet)):
                        m = copy(gb_l[:, n:n + 1], t[:, l + 1:l + 2] if isinstance(l, int) else t[:, bass.ds(l + 1, 1)])
                        m.then_inc(gb_in, 1)
                    act.wait_ge(gb_in, L * 2 + 2)
            for c in range(1, NMIX, 2):
                act.wait_ge(mix_mm, L * NMIX + c + 1)
                copy(ym[:, :, :, c * MC:(c + 1) * MC].rearrange("p h i m -> p m (h i)"),
                     bk(c % 4)[0:2 * C, :].rearrange("p (m i) -> p m i", m=MC)).then_inc(mix_a, 1)

            def front(g):
                for c in range(NY):
                    act.wait_ge(yt_mm, L * (G * NY) + g * NY + c + 1)
                    copy(yt[:, 3 * c:3 * c + 3, :].rearrange("p a b -> p (a b)"), bk(6 + c)[0:96, 0:384]
                         ).then_inc(yt_cp, 1)

            def rest(g):
                for c in range(NZ):
                    act.wait_ge(zt_mm, L * (G * NZ) + g * NZ + c + 1)
                    copy(zt[:, 4 * c:4 * c + 4, :].rearrange("p a b -> p (a b)"), bk(6 + c % 2)[0:96, :]
                         ).then_inc(zt_cp, 1)

            norm(M, front, rest, func, gb_l[:, 0:1], gb_l[:, 1:2], False)

        with act.Fori(0, batches) as it:
            def front0(g):
                act.wait_ge(x_in, it * (G * 16) + G * 16)
                copy(xr[:], xin[:, g, :, :].rearrange("p i (o r) -> p o i r", o=4)).then_inc(xr_cp, 1)
                act.wait_ge(xt_mm, it * G + g + 1)
                copy(xt[:].rearrange("p a b -> p (a b)"), bk(6)[0:96, :]).then_inc(xt_cp, 1)

            affine = (ACT.Identity, gam[:, 0:1], bet[:, 0:1])
            gelu = (ACT.Gelu, gb_l[:, 0:1], gb_l[:, 1:2])
            norm(it * NORMS, front0, lambda g: None, *affine, True)
            layer_body(it * LAYERS, 0, it * NORMS + 1, affine, ACT.Gelu)
            with act.Fori(1, LAYERS - 1) as l:
                layer_body(it * LAYERS + l, l, it * NORMS + l + 1, gelu, ACT.Gelu)
            layer_body(it * LAYERS + LAYERS - 1, LAYERS - 1, it * NORMS + LAYERS, gelu, ACT.Identity)
            estimate(it * NORMS + LAYERS, G - 1)
            for g in range(G):
                if g == 1:
                    for n in range(2):
                        final(it * NORMS + LAYERS, G - 1, n, ACT.Identity, gb_l[:, 0:1], gb_l[:, 1:2])
                for n in range(NM + 1):
                    if n < NM:
                        act.wait_ge(m1_mm, it * (G * NM) + g * NM + n + 1)
                        s.activation(g1[:, n % 2, :], bank[n % 2][:, :, :], ACT.Gelu, bias=b1[:, 0:1]
                                     ).then_inc(m1_done, 1)
                    if n:
                        act.wait_ge(m2_mm, it * (G * NM) + g * NM + n)
                        s.activation(g2[:, (n - 1) % 2, :], bk(4 + (n - 1) % 2), ACT.Gelu, bias=b2[:, 0:1]
                                     ).then_inc(m2_done, 1)


D = 64
HEADS, HD, HP = 4, 16, 32
MAX_REL = 30
TL = 8
ROUNDS = NIMG // (2 * TL)
RT = TL * P
FH = 4 * D
KEPT = S // 2 - 1


def attention_constants():
    f4 = np.float32
    pos = np.arange(2 * MAX_REL + 1, dtype=f4)[:, None]
    div = np.exp(np.arange(0, D, 2, dtype=f4) * f4(-np.log(10000.0) / D)).astype(f4)
    ang = (pos * div).astype(f4)
    enc = np.stack([np.sin(ang), np.cos(ang)], -1).reshape(-1, D)
    near = np.clip(np.arange(2 * S - 1) - (S - 1), -MAX_REL, MAX_REL) + MAX_REL
    enc_t = np.concatenate([enc[near].T, np.ones((1, 2 * S - 1))])
    t = np.arange(P) % S
    before = (np.arange(S)[None, :] < t[:, None])
    out = dict(k_enc=enc_t, k_before=before)
    return {k: np.ascontiguousarray(v, np.float32) for k, v in out.items()}


def attention_and_ffn(nc, ctx, a, tokens, out):
    def sb(name, shape, dt=F32):
        return ctx.enter_context(nc.sbuf_tensor(name, shape, dt))

    def sem(name):
        return ctx.enter_context(nc.semaphore(name))

    bank = [ctx.enter_context(nc.psum_tensor(f"pbank{i}", [P, 2, CH], F32)) for i in range(4)]

    def bk(n):
        return bank[n // 2][:, n % 2, :]

    ident, blk, before = sb("ident2", [P, P]), sb("blk2", [P, IG]), sb("before", [P, S])
    enc_t = sb("enc_t", [D + 1, 2 * S - 1])
    w_p, bias_uv = sb("w_p", [P, 5, D + 1]), sb("bias_uv", [P, 2])
    w_t = sb("w_t", [D + 1, 5, P])
    wo_p, wo_t = sb("wo_p", [D, HEADS, HP]), sb("wo_t", [P, D])
    pos_t, pos_bd = sb("pos_t", [P, 2 * S - 1]), sb("pos_bd", [P, HEADS, 2 * S - 1])
    rows = sb("rows", [P, 5, D])
    br = sb("br", [P, 1])
    w1, w2, fb1 = sb("w1s", [D, FH]), sb("w2s", [P, 2, D]), sb("fb1", [P, 2])

    ht, xa, tmp = sb("ht", [P, TL, D]), sb("xa2", [P, TL, D]), sb("tmp", [P, TL, D])
    ln_s = sb("ln_s", [P, 4, TL])
    x_t = sb("x_t", [D + 1, RT])
    qv = sb("qv", [P, NIMG, S])
    pos_s = sb("pos_s", [P, 2, TL, HEADS * S])
    pos_in = sb("pos_in", [P, TL, HEADS * S])
    q, k = sb("q", [P, RT]), sb("kk", [P, RT])
    val = sb("val", [S, 2 * TL, P])
    att = sb("att", [P, HEADS, TL, S])
    stat = sb("stat", [P, 2, HEADS, TL])
    att_t = sb("att_t", [S, TL, HEADS, P])
    ctx_t = sb("ctx_t", [P, RT])
    h4, x5 = sb("h4", [P, TL, D]), sb("x5", [P, TL, D])
    w, coef = sb("wgt", [P, TL]), sb("coef", [P, TL])
    above, same = sb("above", [P, TL, S]), sb("same", [P, TL, S])
    hid = sb("hid", [P, 2, 2, CH])

    scr_p = a["scr_p"]
    tok_v = tokens.rearrange("i (t d) -> (i t) d", d=D).rearrange("(n p) d -> p n d", p=P)
    out_v = out.rearrange("i t d -> (i t) d").rearrange("(n p) d -> p n d", p=P)
    pos_v = scr_p.rearrange("i t m -> (i t) m").rearrange("(n p) m -> p n m", p=P)

    s2_in, s2_zero, s2_v, s2_mm = sem("s2_in"), sem("s2_zero"), sem("s2_v"), sem("s2_mm")
    a_in, a_x, a_xt, a_xtc, a_q, a_qc, a_var, a_rs = (sem("a_in"), sem("a_x"), sem("a_xt"), sem("a_xtc"), sem("a_q"),
                                                      sem("a_qc"), sem("a_var"), sem("a_rs"))
    pe_passed, sp_passed = sem("pe_passed"), sem("sp_passed")
    p_mm, p_v, p_a, p_out = sem("p_mm"), sem("p_v"), sem("p_a"), [sem("p_out0"), sem("p_out1")]
    names = ("tok_in pos_ld x_ready xt_mm2 xt_c qk_mm q_c k_c val_mm val_c score_mm shifted exp_c att_n at_mm0 at_mm1 "
             "at_c0 at_c1 ctx_mm ctx_c wo_mm x5_ready x5t_mm x5t_c w_ready wt_mm hid_mm hid_c y2_mm res "
             "out_st seq_a seq_b b_var b_rs h4_ready wt_read y2_read").split()
    s = {n: sem("b_" + n) for n in names}
    block = ctx.enter_context(nc.Block())
    NSET = 4 + 5 * HEADS + 5 * HEADS + 2 * HEADS + 1 + 5 + 1 + 3

    @block.sync
    def _(sp):
        col = lambda v: v.rearrange("(c o) -> c o", o=1)
        for t, n in ((ident, "k_ident"), (blk, "k_blk"), (before, "k_before"), (enc_t, "k_enc")):
            sp.dma_start(t[:], a[n]).then_inc(s2_in, 16)
        sp.wait_ge(s2_zero, 4)
        with nc.allow_non_contiguous_dma(reason="a few small weights"):
            for n, (wn, bn) in enumerate((("Wq", "bq"), ("Wq", "bq"), ("Wk", "bk"), ("Wv", "bv"), ("Wpos", "bpos"))):
                for hd in range(HEADS):
                    dst = slice(HP * hd, HP * hd + HD)
                    src = slice(HD * hd, HD * hd + HD)
                    sp.dma_start(w_p[dst, n, 0:D], a["L0_attn_" + wn][src, :]).then_inc(s2_in, 16)
                    sp.dma_start(w_p[dst, n, D:D + 1], col(a["L0_attn_" + bn])[src, :]).then_inc(s2_in, 16)
            for n, un in enumerate(("u_bias", "v_bias")):
                for hd in range(HEADS):
                    sp.dma_start(bias_uv[HP * hd:HP * hd + HD, n:n + 1],
                                 a["L0_attn_" + un].rearrange("a h b d -> (a h b) d")[hd:hd + 1, :]
                                 .rearrange("a d -> d a")).then_inc(s2_in, 16)
            sp.dma_start(wo_p[:, :, 0:HD], a["L0_attn_Wo"].rearrange("o (h d) -> o h d", h=HEADS)).then_inc(s2_in, 16)
            for n, v in enumerate((a["L0_attn_ln_gamma"], a["L0_attn_ln_beta"], a["L0_attn_bo"],
                                   a["L0_ffn_wr"].rearrange("d o -> (d o)"), a["L0_ffn_b2"])):
                sp.dma_start(rows[:, n, :], v.rearrange("(a d) -> a d", a=1).broadcast_to([P, D])).then_inc(s2_in, 16)
            sp.dma_start(br[:], a["L0_ffn_br"].rearrange("(a b) -> a b", a=1).broadcast_to([P, 1])).then_inc(s2_in, 16)
            sp.dma_start(w1[:], a["L0_ffn_w1"]).then_inc(s2_in, 16)
            sp.dma_start(w2[:], a["L0_ffn_w2"].rearrange("(n p) d -> p n d", p=P)).then_inc(s2_in, 16)
            sp.dma_start(fb1[:], a["L0_ffn_b1"].rearrange("(n p) -> p n", p=P)).then_inc(s2_in, 16)
        with sp.Fori(0, ROUNDS) as o:
            sp.dma_start(ht[:], tok_v[:, bass.ds(o * TL, TL), :]).then_inc(a_in, 16)
            wait_alone(sp, a_x, o + 1, sp_passed)
        for n in range(S // TL):
            sp.wait_ge(p_v, 2 * (n + 1))
            sp.wait_ge(p_a, 2 * (n + 1))
            sp.dma_start(scr_p[:, TL * n:TL * (n + 1), :], pos_s[:, n % 2, :, :]).then_inc(p_out[n % 2], 16)
        for n in range(2):
            sp.wait_ge(p_out[n], 16 * (S // TL // 2))
        with sp.Fori(0, ROUNDS) as o:
            sp.dma_start(ht[:], tok_v[:, bass.ds(o * TL, TL), :]).then_inc(s["tok_in"], 16)
            sp.dma_start(pos_in[:], pos_v[:, bass.ds(o * TL, TL), :]).then_inc(s["pos_ld"], 16)
            sp.wait_ge(s["res"], o + 1)
            sp.dma_start(out_v[:, bass.ds(o * TL, TL), :], xa[:]).then_inc(s["out_st"], 16)
            wait_alone(sp, s["out_st"], o * 16 + 16, sp_passed)

    @block.tensor
    def _(pe):
        mm = nc.tensor.matmul
        pe.wait_ge(s2_in, NSET * 16)
        pe.wait_ge(s2_v, 1)
        for n in range(5):
            pe.transpose(bk(n // 4)[0:D + 1, P * (n % 4):P * (n % 4 + 1)], w_p[:, n, :], ident[:])
        pe.transpose(bk(2)[:, 0:D], wo_p[:].rearrange("p a b -> p (a b)"), ident[0:D, 0:D]).then_inc(s2_mm, 1)
        pe.wait_ge(s2_v, 3)
        mm(bk(3)[:, 0:2 * S - 1], w_t[:, 4, :], enc_t[:], start=True, stop=True).then_inc(s2_mm, 1)
        pe.wait_ge(s2_v, 5)

        def transposes(src, done):
            for n in range(TL):
                m = pe.transpose(bk(n // 4)[0:D, P * (n % 4):P * (n % 4 + 1)], src[:, n, :], ident[:])
            m.then_inc(done, 1)

        with pe.Fori(0, ROUNDS) as o:
            wait_alone(pe, a_x, o + 1, pe_passed)
            transposes(xa, a_xt)
            pe.wait_ge(a_xtc, o + 1)
            for n in range(2):
                m = mm(bk(2 + n), w_t[:, 1, :], x_t[:, CH * n:CH * (n + 1)], start=True, stop=True)
            m.then_inc(a_q, 1)
        pe.wait_ge(a_qc, ROUNDS)
        for t in range(S):
            c = t // 2
            if c >= 8 and t % 2 == 0:
                pe.wait_ge(p_v if c % 2 == 0 else p_a, (c - 8) // 2 + 1)
            m = mm(bk(c % 8)[:, 256 * (t % 2):256 * (t % 2) + 256], qv[:, :, t], pos_bd[:, :, S - 1 - t:2 * S - 1 - t],
                   start=True, stop=True)
            if t % 2:
                m.then_inc(p_mm, 1)
        pe.wait_ge(p_v, S // 4)
        pe.wait_ge(p_a, S // 4)
        with pe.Fori(0, ROUNDS) as o:
            wait_alone(pe, s["x_ready"], o + 1, pe_passed)
            transposes(xa, s["xt_mm2"])
            pe.wait_ge(s["xt_c"], o + 1)
            for n in range(2):
                mm(bk(2 + n), w_t[:, 0, :], x_t[:, CH * n:CH * (n + 1)], start=True, stop=True)
                m = mm(bk(4 + n), w_t[:, 2, :], x_t[:, CH * n:CH * (n + 1)], start=True, stop=True)
            m.then_inc(s["qk_mm"], 1)
            for n in range(2 * TL):
                b = (6, 7, 0, 1)[n // 4]
                m = mm(bk(b)[0:S, P * (n % 4):P * (n % 4 + 1)], x_t[:, S * n:S * (n + 1)], w_t[:, 3, :],
                       start=True, stop=True)
            m.then_inc(s["val_mm"], 1)
            pe.wait_ge(s["q_c"], o + 1)
            pe.wait_ge(s["k_c"], o + 1)
            for n in range(2 * TL):
                for hd in range(HEADS):
                    r = slice(HP * hd, HP * (hd + 1))
                    m = mm(bk(2 + hd)[S * (n % 2):S * (n % 2) + S, S * (n // 2):S * (n // 2) + S],
                           q[r, S * n:S * (n + 1)], k[r, S * n:S * (n + 1)], start=True, stop=True)
            m.then_inc(s["score_mm"], 1)
            pe.wait_ge(s["att_n"], o + 1)
            wait_alone(pe, s["val_c"], o + 1, pe_passed)
            for n in range(TL):
                for hd in range(HEADS):
                    b = (6, 7, 0, 1, 2, 3, 4, 5)[n]
                    m = pe.transpose(bk(b)[0:S, P * hd:P * (hd + 1)], att[:, hd, n, :], ident[:])
                if n == 3:
                    m.then_inc(s["at_mm0"], 1)
            m.then_inc(s["at_mm1"], 1)
            pe.wait_ge(s["at_c0"], o + 1)
            wait_alone(pe, s["at_c1"], o + 1, pe_passed)
            for n in range(2 * TL):
                for hd in range(HEADS):
                    m = mm(bk(n // 8)[HP * hd:HP * (hd + 1), S * (n % 8):S * (n % 8) + S], val[:, n, HP * hd:HP * (hd + 1)],
                           att_t[:, n // 2, hd, S * (n % 2):S * (n % 2) + S], start=True, stop=True)
            m.then_inc(s["ctx_mm"], 1)
            pe.wait_ge(s["ctx_c"], o + 1)
            for n in range(TL):
                m = mm(bk(6)[:, D * n:D * (n + 1)], ctx_t[:, P * n:P * (n + 1)], wo_t[:], start=True, stop=True)
            m.then_inc(s["wo_mm"], 1)
            wait_alone(pe, s["x5_ready"], o + 1, pe_passed)
            transposes(x5, s["x5t_mm"])
            pe.wait_ge(s["w_ready"], o + 1)
            for n in range(TL):
                m = pe.transpose(bk(4 + n // 4)[:, P * (n % 4):P * (n % 4 + 1)], w[:, n:n + 1].broadcast_to([P, P]),
                                 ident[:])
            m.then_inc(s["wt_mm"], 1)
            pe.wait_ge(s["x5t_c"], o + 1)
            for c in range(2):
                for n in range(2):
                    m = mm(bk(2 - 2 * c + n), w1[:, P * n:P * (n + 1)], x_t[0:D, CH * c:CH * (c + 1)],
                           start=True, stop=True)
                m.then_inc(s["hid_mm"], 1)
            pe.wait_ge(s["hid_c"], o * 2 + 2)
            for n in range(TL):
                for c in range(2):
                    m = mm(bk(7)[:, D * n:D * (n + 1)], hid[:, n // 4, c, P * (n % 4):P * (n % 4 + 1)], w2[:, c, :],
                           start=(c == 0), stop=(c == 1))
            m.then_inc(s["y2_mm"], 1)

    def per_token(v, width=D):
        return v.rearrange("p (n a) -> p n a", a=1).broadcast_to([P, TL, width])

    def per_feature(v):
        return v.rearrange("p (a d) -> p a d", a=1).broadcast_to([P, TL, v.shape[-1]])

    @block.vector
    def _(dve):
        v = nc.vector
        for t in (w_p, wo_p, bias_uv):
            v.memset(t[:], 0.0).then_inc(s2_zero, 1)
        v.memset(x_t[D:D + 1, :], 1.0).then_inc(s2_zero, 1)
        dve.wait_ge(s2_in, NSET * 16)
        v.tensor_tensor(w_p[:, 0:2, D], w_p[:, 0:2, D], bias_uv[:], ALU.add).then_inc(s2_v, 1)
        dve.wait_ge(s2_mm, 1)
        v.tensor_copy(w_t[:, 0:4, :].rearrange("p a b -> p (a b)"), bk(0)[0:D + 1, :])
        v.tensor_copy(w_t[:, 4, :], bk(1)[0:D + 1, 0:P]).then_inc(s2_v, 1)
        v.tensor_copy(wo_t[:], bk(2)[:, 0:D]).then_inc(s2_v, 1)
        dve.wait_ge(s2_mm, 2)
        v.tensor_copy(pos_t[:], bk(3)[:, 0:2 * S - 1]).then_inc(s2_v, 1)
        dve.wait_ge(s2_v, 4)
        v.tensor_tensor(pos_bd[:], pos_t[:].rearrange("p (a d) -> p a d", a=1).broadcast_to([P, HEADS, 2 * S - 1]),
                        blk[:].rearrange("p (a d) -> p a d", d=1).broadcast_to([P, HEADS, 2 * S - 1]), ALU.mult
                        ).then_inc(s2_v, 1)
        dve.wait_ge(s2_v, 5)

        class Chain:
            def __init__(self, semaphore, base, steps):
                self.semaphore, self.base, self.n = semaphore, base * steps, 0

            def __call__(self, ins):
                self.n += 1
                ins.then_inc(self.semaphore, 1)
                dve.wait_ge(self.semaphore, self.base + self.n)

        def normalise(link, dst, src, var_ready, rs_ready, nth):
            total, var, est, u = (ln_s[:, n, :] for n in range(4))
            link(v.reduce_sum(total, src, AX_X))
            link(v.scalar_tensor_tensor(out=dst, in0=per_token(total), scalar=-1.0 / D, in1=src, op0=ALU.mult,
                                        op1=ALU.add))
            link(v.tensor_tensor(tmp[:], dst, dst, ALU.mult))
            link(v.reduce_sum(total, tmp[:], AX_X))
            v.tensor_scalar(var, total, 1.0 / D, EPS, ALU.mult, ALU.add).then_inc(var_ready, 1)
            dve.wait_ge(rs_ready, nth)
            link(v.tensor_tensor(u, var, est, ALU.mult))
            link(v.scalar_tensor_tensor(out=u, in0=u, scalar=-0.5, in1=est, op0=ALU.mult, op1=ALU.mult))
            link(v.scalar_tensor_tensor(out=est, in0=u, scalar=1.5, in1=est, op0=ALU.add, op1=ALU.mult))
            return v.tensor_tensor(dst, dst, per_token(est), ALU.mult)

        def inputs(link, var_ready, rs_ready, base, ready):
            link(normalise(link, xa[:], ht[:], var_ready, rs_ready, base + 1))
            link(normalise(link, xa[:], xa[:], var_ready, rs_ready, base + 2))
            link(v.tensor_tensor(xa[:], xa[:], per_feature(rows[:, 0, :]), ALU.mult))
            v.tensor_tensor(xa[:], xa[:], per_feature(rows[:, 1, :]), ALU.add).then_inc(ready, 1)

        STEPS_A = 17
        with dve.Fori(0, ROUNDS) as o:
            link = Chain(s["seq_a"], o, STEPS_A)
            dve.wait_ge(a_in, o * 16 + 16)
            inputs(link, a_var, a_rs, o * 2, a_x)
            dve.wait_ge(a_xt, o + 1)
            assert link.n == STEPS_A
        for c in range(0, S // 2, 2):
            n = c // 4
            if n >= 2 and c % 4 == 0:
                dve.wait_ge(p_out[n % 2], 16 * (n // 2))
            dve.wait_ge(p_mm, c + 1)
            v.tensor_copy(pos_s[:, n % 2, 2 * (c % 4):2 * (c % 4) + 2, :].rearrange("p a b -> p (a b)"), bk(c % 8)
                          ).then_inc(p_v, 1)
        STEPS_B = 46
        with dve.Fori(0, ROUNDS) as o:
            link = Chain(s["seq_b"], o, STEPS_B)
            dve.wait_ge(s["tok_in"], o * 16 + 16)
            inputs(link, s["b_var"], s["b_rs"], o * 3, s["x_ready"])
            link(v.tensor_tensor(h4[:], ht[:], per_feature(rows[:, 2, :]), ALU.add))
            dve.wait_ge(s["qk_mm"], o + 1)
            v.tensor_copy(k[:].rearrange("p (a b) -> p a b", a=2), bank[2][:, :, :]).then_inc(s["k_c"], 1)
            dve.wait_ge(s["score_mm"], o + 1)
            dve.wait_ge(s["pos_ld"], o * 16 + 16)
            for hd in range(HEADS):
                link(v.tensor_tensor(att[:, hd, :, :], bk(2 + hd).rearrange("p (n t) -> p n t", t=S),
                                     pos_in[:, :, S * hd:S * (hd + 1)], ALU.add))
            att_v = att[:].rearrange("p h n t -> p (h n) t")
            top = stat[:, 0, :, :].rearrange("p h n -> p (h n)")
            total = stat[:, 1, :, :].rearrange("p h n -> p (h n)")

            def per_row(x):
                return x.rearrange("p (n a) -> p n a", a=1).broadcast_to([P, HEADS * TL, S])

            link(v.tensor_reduce(top, att_v, AX_X, ALU.max))
            v.tensor_tensor(att_v, att_v, per_row(top), ALU.subtract).then_inc(s["shifted"], 1)
            dve.wait_ge(s["exp_c"], o + 1)
            link(v.reduce_sum(total, att_v, AX_X))
            link(v.reciprocal(top, total))
            v.tensor_tensor(att_v, att_v, per_row(top), ALU.mult).then_inc(s["att_n"], 1)
            dve.wait_ge(s["at_mm1"], o + 1)
            v.tensor_copy(att_t[:, 4:6, :, :].rearrange("p a h t -> p (a h t)").rearrange("p (a b) -> p a b", a=2),
                          bank[1][0:S, :, :])
            v.tensor_copy(att_t[:, 6:8, :, :].rearrange("p a h t -> p (a h t)").rearrange("p (a b) -> p a b", a=2),
                          bank[2][0:S, :, :]).then_inc(s["at_c1"], 1)
            dve.wait_ge(s["wo_mm"], o + 1)
            link(v.tensor_tensor(h4[:].rearrange("p n d -> p (n d)"), bk(6), h4[:].rearrange("p n d -> p (n d)"), ALU.add))
            normalise(link, x5[:], h4[:], s["b_var"], s["b_rs"], o * 3 + 3).then_inc(s["x5_ready"], 1)
            dve.wait_ge(s["x5_ready"], o + 1)
            link(v.tensor_tensor(tmp[:], x5[:], per_feature(rows[:, 3, :]), ALU.mult))
            link(v.reduce_sum(w[:], tmp[:], AX_X))
            v.tensor_scalar(w[:], w[:], br[:, 0:1], None, ALU.add).then_inc(s["w_ready"], 1)
            link(v.tensor_tensor(h4[:], h4[:], x5[:], ALU.add))
            dve.wait_ge(s["w_ready"], o + 1)
            dve.wait_ge(s["wt_mm"], o + 1)
            for i in range(2):
                r = slice(S * i, S * (i + 1))
                others = bank[2][r, :, :].rearrange("p a b -> p (a b)").rearrange("p (n c j) -> p n c j", c=2, j=S)[:, :, i, :]
                own = w[r, :].rearrange("p (n a) -> p n a", a=1).broadcast_to([S, TL, S])
                link(v.tensor_tensor(above[r, :, :], others, own, ALU.is_gt))
                link(v.tensor_tensor(same[r, :, :], others, own, ALU.is_equal))
            link(v.tensor_tensor(same[:], same[:], per_feature(before[:]), ALU.mult))
            link(v.tensor_tensor(above[:], above[:], same[:], ALU.add))
            link(v.reduce_sum(coef[:], above[:], AX_X))
            link(v.scalar_tensor_tensor(out=coef[:], in0=coef[:], scalar=KEPT - 0.5, in1=w[:], op0=ALU.is_lt,
                                        op1=ALU.mult))
            dve.wait_ge(s["y2_mm"], o + 1)
            link(v.tensor_tensor(tmp[:], bk(7).rearrange("p (n d) -> p n d", d=D), per_feature(rows[:, 4, :]), ALU.add))
            link(v.tensor_tensor(tmp[:], tmp[:], per_token(coef[:]), ALU.mult))
            v.tensor_tensor(xa[:], tmp[:], h4[:], ALU.add).then_inc(s["res"], 1)
            dve.wait_ge(s["out_st"], o * 16 + 16)
            assert link.n == STEPS_B

    @block.scalar
    def _(act):
        f = nc.scalar
        act.wait_ge(s2_v, 5)

        def copy(dst, src):
            return f.activation(dst, src, ACT.Copy)

        def estimate(var_ready, rs_ready, nth):
            act.wait_ge(var_ready, nth)
            f.activation(ln_s[:, 2, :], ln_s[:, 1, :], ACT.Abs_reciprocal_sqrt).then_inc(rs_ready, 1)

        with act.Fori(0, ROUNDS) as o:
            estimate(a_var, a_rs, o * 2 + 1)
            estimate(a_var, a_rs, o * 2 + 2)
            act.wait_ge(a_xt, o + 1)
            copy(x_t[0:D, :].rearrange("p (a b) -> p a b", a=2), bank[0][0:D, :, :]).then_inc(a_xtc, 1)
            act.wait_ge(a_q, o + 1)
            copy(qv[:, bass.ds(o * 2 * TL, 2 * TL), :].rearrange("p i t -> p (i t)").rearrange("p (a b) -> p a b", a=2),
                 bank[1][:, :, :]).then_inc(a_qc, 1)
        for c in range(1, S // 2, 2):
            n = c // 4
            if n >= 2 and c % 4 == 1:
                act.wait_ge(p_out[n % 2], 16 * (n // 2))
            act.wait_ge(p_mm, c + 1)
            copy(pos_s[:, n % 2, 2 * (c % 4):2 * (c % 4) + 2, :].rearrange("p a b -> p (a b)"), bk(c % 8)
                 ).then_inc(p_a, 1)
        with act.Fori(0, ROUNDS) as o:
            estimate(s["b_var"], s["b_rs"], o * 3 + 1)
            estimate(s["b_var"], s["b_rs"], o * 3 + 2)
            act.wait_ge(s["xt_mm2"], o + 1)
            copy(x_t[0:D, :].rearrange("p (a b) -> p a b", a=2), bank[0][0:D, :, :]).then_inc(s["xt_c"], 1)
            act.wait_ge(s["qk_mm"], o + 1)
            copy(q[:].rearrange("p (a b) -> p a b", a=2), bank[1][:, :, :]).then_inc(s["q_c"], 1)
            act.wait_ge(s["val_mm"], o + 1)
            copy(val[:, 0:8, :].rearrange("p a b -> p (a b)").rearrange("p (a b) -> p a b", a=2), bank[3][0:S, :, :])
            copy(val[:, 8:16, :].rearrange("p a b -> p (a b)").rearrange("p (a b) -> p a b", a=2), bank[0][0:S, :, :]
                 ).then_inc(s["val_c"], 1)
            act.wait_ge(s["shifted"], o + 1)
            av = att[:].rearrange("p h n t -> p (h n t)")
            f.activation(av, av, ACT.Exp, scale=float(HD) ** -0.5).then_inc(s["exp_c"], 1)
            act.wait_ge(s["at_mm0"], o + 1)
            copy(att_t[:, 0:2, :, :].rearrange("p a h t -> p (a h t)").rearrange("p (a b) -> p a b", a=2),
                 bank[3][0:S, :, :])
            copy(att_t[:, 2:4, :, :].rearrange("p a h t -> p (a h t)").rearrange("p (a b) -> p a b", a=2),
                 bank[0][0:S, :, :]).then_inc(s["at_c0"], 1)
            act.wait_ge(s["ctx_mm"], o + 1)
            copy(ctx_t[:].rearrange("p (a b) -> p a b", a=2), bank[0][:, :, :]).then_inc(s["ctx_c"], 1)
            estimate(s["b_var"], s["b_rs"], o * 3 + 3)
            act.wait_ge(s["x5t_mm"], o + 1)
            copy(x_t[0:D, :].rearrange("p (a b) -> p a b", a=2), bank[0][0:D, :, :]).then_inc(s["x5t_c"], 1)
            for c in range(2):
                act.wait_ge(s["hid_mm"], o * 2 + c + 1)
                for n in range(2):
                    m = f.activation(hid[:, c, n, :], bk(2 - 2 * c + n), ACT.Gelu_apprx_tanh, bias=fb1[:, n:n + 1])
                m.then_inc(s["hid_c"], 1)


def vision_tower(nc, a, out):
    tokens = nc.dram_tensor("tokens", (NIMG, PIX), F32, kind="Internal").ap()
    a["scr_x"] = nc.dram_tensor("scr_x", (BI, C, XM), F32, kind="Internal").ap()
    a["scr_y"] = nc.dram_tensor("scr_y", (BI, C, XM), F32, kind="Internal").ap()
    a["scr_p"] = nc.dram_tensor("scr_p", (NIMG, S, HEADS * S), F32, kind="Internal").ap()
    with ExitStack() as ctx:
        tokenizer(nc, ctx, a, tokens, NIMG // BI)
    with ExitStack() as ctx:
        attention_and_ffn(nc, ctx, a, tokens, out)


def kernel(**inputs):
    import concourse.bacc as bacc
    from concourse.bass_utils import run_bass_kernel_spmd

    nc = bacc.Bacc("TRN2", target_bir_lowering=False, num_devices=1, dynamic_dma_scratch_size=256)
    arrays, aps = {}, {}
    given = {n: np.ascontiguousarray(v) for n, v in inputs.items()}
    for name, array in {**given, **constants(), **attention_constants()}.items():
        arrays[f"in_{name}"] = array
        aps[name] = nc.dram_tensor(f"in_{name}", array.shape, mybir.dt.from_np(array.dtype), kind="ExternalInput").ap()
    out = nc.dram_tensor("out_0", (NIMG, S, S), F32, kind="ExternalOutput").ap()
    vision_tower(nc, aps, out)
    r = run_bass_kernel_spmd(nc, [arrays], core_ids=[0])
    return r.results[0]["out_0"]
```

```python
from contextlib import ExitStack

import numpy as np

import concourse.bass as bass
from concourse import mybir

F32 = mybir.dt.float32
BF16 = mybir.dt.bfloat16
ALU = mybir.AluOpType
ACT = mybir.ActivationFunctionType
AX_X = mybir.AxisListType.X

P = 128
NIMG = 128
S = 64
PIX = S * S
C = 32
IG = P // C
G = 4
BI = G * IG
LAYERS = 4
M1 = M2 = 12
MODES = M1 * M2
HR = 4
Q = 4
NF = 2 * 2 * M2
XM = HR * MODES
NORMS = LAYERS + 1
HID1, HID2 = 128, 64
EPS = 1e-5
CH = 512
NCH = PIX // CH
NXP = PIX // P
RO = 8
PARTS = 3


def wait_alone(engine, semaphore, value, passed):
    engine.wait_ge(semaphore, value)
    engine.sem_inc(passed, 1)


def wide(psum, j):
    return psum[:, NF * j:NF * j + 2 * NF]


def constants():
    f8 = np.float64
    kx = np.concatenate([np.arange(M1), np.arange(-M1, 0)]).reshape(2, M1)
    x = np.arange(S)
    th_x = 2 * np.pi * (kx[:, :, None] * x[None, None, :]) / S
    th_y = 2 * np.pi * np.outer(np.arange(M2), x) / S
    cosx, sinx, cosy, siny = np.cos(th_x), np.sin(th_x), np.cos(th_y), np.sin(th_y)
    two = np.eye(2)
    dft_y = np.zeros((2, S, 2, M2, 2), f8)
    for a in range(2):
        dft_y[a, :, a, :, 0] = cosy.T
        dft_y[a, :, a, :, 1] = -siny.T
    dft_x = np.zeros((S, 2, 2, 2, M1), f8)
    for h in range(2):
        c, s = cosx[h].T, sinx[h].T
        dft_x[:, 0, h, 0], dft_x[:, 1, h, 0] = c, s
        dft_x[:, 0, h, 1], dft_x[:, 1, h, 1] = -s, c
    idft_x = np.zeros((2, 2, M1, 2, S, 2, 2), f8)
    for h in range(2):
        for k in range(2):
            c, s = cosx[h], sinx[h]
            idft_x[h, 0, :, k, :, k, 0], idft_x[h, 1, :, k, :, k, 0] = c, -s
            idft_x[h, 0, :, k, :, k, 1], idft_x[h, 1, :, k, :, k, 1] = s, c
    idft_x = idft_x.reshape(HR, Q, M1 // Q, 2, 256).transpose(1, 0, 2, 3, 4)
    w = np.where(np.arange(M2) == 0, 1.0, 2.0)[:, None] / PIX
    idft_y = np.zeros((4, M2, 2, 4, S), f8)
    for a in range(4):
        idft_y[a, :, 0, a] = w * cosy
        idft_y[a, :, 1, a] = -w * siny
    blk = np.kron(np.eye(IG), np.ones((C, 1)))
    centre = np.kron(np.eye(IG), np.eye(C) - 1.0 / C)
    ones_v = blk[:, np.arange(32) % IG] / C
    sel = np.zeros((4, 32, 4, IG, C))
    for q in range(4):
        for n in range(PARTS * IG):
            sel[q, n, q, n % IG, :] = 1
    row = np.arange(P) % 32
    minus = np.stack([-(row >= IG).astype(f8) * (row < 3 * IG), -((row >= 2 * IG) & (row < 3 * IG)).astype(f8)], 1)
    fmask = np.zeros((IG, RO, 3, RO, IG))
    for i in range(IG):
        for r in range(RO):
            fmask[i, r, :, r, i] = 1
    mask2 = np.zeros((2, HID2, 32))
    for i in range(2):
        mask2[i, :, i] = 1
    out = dict(k_ident=np.eye(P), k_dft_y=np.tile(dft_y.reshape(P, NF), (1, 2)), k_dft_x=np.tile(dft_x.reshape(P, NF), (1, 2)),
               k_idft_x=idft_x.reshape(96, 256), k_idft_y=idft_y.reshape(96, 256), k_blk=blk, k_centre=centre,
               k_ones_v=ones_v, k_sel=sel.reshape(P, 4 * P), k_minus=minus, k_fmask=fmask.reshape(96, RO * IG),
               k_mask2=mask2.reshape(P, 32))
    return {k: np.ascontiguousarray(v, np.float32) for k, v in out.items()}


def layouts(a):
    def per_image(v, n=IG):
        return np.tile(v, (n, 1))

    out = dict(l_fc0=per_image(a["L0_tok_fc0_w"], IG * RO), l_fc1=per_image(a["L0_tok_fc1_w"]),
               l_conv=per_image(a["L0_tok_conv_w"].transpose(1, 0, 2).reshape(C, LAYERS * C)),
               l_cb=per_image(np.concatenate([a["L0_tok_fc0_b"][None], a["L0_tok_conv_b"]]).T),
               l_gam=per_image(np.concatenate([a["L0_tok_ln0_g"][None], a["L0_tok_ln_g"]]).T),
               l_bet=per_image(np.concatenate([a["L0_tok_ln0_b"][None], a["L0_tok_ln_b"]]).T),
               l_fc3=per_image(a["L0_tok_fc3_w"], 2), l_b2=per_image(a["L0_tok_fc2_b"][:, None], 2),
               l_b1=a["L0_tok_fc1_b"][:, None], l_b3=per_image(a["L0_tok_fc3_b"][:, None], P))
    return {k: np.ascontiguousarray(v) for k, v in out.items()}


def tokenizer(nc, ctx, a, tokens, batches):
    def sb(name, shape, dt=F32):
        return ctx.enter_context(nc.sbuf_tensor(name, shape, dt))

    def sem(name):
        return ctx.enter_context(nc.semaphore(name))

    bank = [ctx.enter_context(nc.psum_tensor(f"bank{i}", [P, 2, CH], F32)) for i in range(4)]

    def bk(n):
        return bank[n // 2][:, n % 2, :]

    h = sb("h", [P, G, PIX])
    mix_w = sb("mix_w", [P, 2, C, MODES])
    xm = sb("xm", [P, 2, BI, MODES])
    ym = sb("ym", [P, 2, C, MODES // Q])
    th = sb("th", [P, 4, CH])
    ya = sb("ya", [P, M2, S, 2])
    xa = sb("xa", [P, M2, P])
    xg = sb("xg", [P, HR, M1, M2])
    yg = sb("yg", [P, 2, Q * HR * M1 // Q, M2])
    yr = sb("yr", [P, M2 // 2, HR * M1, 2])
    yt = sb("yt", [96, M2 // 2, P])
    zx = sb("zx", [P, S, M2 * 2])
    zt = sb("zt", [96, S // 4, P])
    sq = sb("sq", [P, 2, 2 * CH])
    rstd = sb("rstd", [P, 2, CH])
    newt = sb("newt", [P, 2, CH])
    newt_high = newt[:].bitcast(BF16).rearrange("p a (n e) -> p a n e", e=2)[:, :, :, 1]
    high = rstd[:].bitcast(BF16).rearrange("p a (n e) -> p a n e", e=2)[:, :, :, 1]
    xin = sb("xin", [P, G, IG, 32 * 3])
    xr = sb("xr", [P, 4, IG, 3 * RO])
    xt = sb("xt", [96, 4, P])
    g1, g2 = sq, th
    tok = zx[:].rearrange("p a b -> p (a b)")[:, 0:2 * CH].rearrange("p (a b) -> p a b", a=2)
    ident = sb("ident", [P, P])
    dft_y, dft_x = sb("dft_y", [P, 2 * NF]), sb("dft_x", [P, 2 * NF])
    idft_x, idft_y = sb("idft_x", [96, 256]), sb("idft_y", [96, 256])
    blk, centre = sb("blk", [P, IG]), sb("centre", [P, P])
    ones_v, minus = sb("ones_v", [P, 32]), sb("minus", [P, 2])
    selb = sb("selb", [P, 4, P], BF16)
    f0, f1, f2 = sb("f0", [96, RO, P]), sb("f1", [P, IG, HID1]), sb("f2", [P, HID2])
    f3 = sb("f3", [P, 32])
    conv = sb("conv", [P, LAYERS, P])
    cb = sb("cb", [P, NORMS])
    gam, bet = sb("gam", [P, NORMS]), sb("bet", [P, NORMS])
    b1, b2, b3 = sb("b1", [P, 1]), sb("b2", [P, 1]), sb("b3", [P, 1])
    epst = sb("epst", [P, 1])
    conv_l = sb("conv_l", [P, P])
    cb_l, gb_l = sb("cb_l", [P, 1]), sb("gb_l", [P, 2])
    zf = zx[:].rearrange("p a b -> p (a b)")
    sel_f, fmask, mask2 = zf[:, 0:512], zf[0:96, 512:544], zf[:, 544:576]
    f0_rep, f1_rep, conv_rep = zf[0:96, 576:608], zf[:, 608:736], zf[:, 736:864]
    cb_raw, f3_rep, f0_sum = zf[:, 864:869], zf[:, 869:870], zf[0:96, 870:871]
    conv_bd = xa[:, 0:LAYERS, :]

    wi_raw = h[:].rearrange("p g n -> p (g n)")[:, 0:2 * C * MODES].rearrange("p (f n) -> p f n", f=2)

    scr_x = a["scr_x"]
    scr_y = a["scr_y"]
    scr_w = a["scr_w"]

    setup_in, setup_v, setup_mm = sem("setup_in"), sem("setup_v"), sem("setup_mm")
    pe_passed = sem("pe_passed")
    setup_g, eps_set, conv_in = sem("setup_g"), sem("eps_set"), sem("conv_in")
    x_in = sem("x_in")
    xr_cp, yr_cp = sem("xr_cp"), sem("yr_cp")
    xt_mm, xt_cp = sem("xt_mm"), sem("xt_cp")
    t_mm, t_cp, a_mm, a_cp = sem("t_mm"), sem("t_cp"), sem("a_mm"), sem("a_cp")
    t2_mm, t2_cp, b_mm, b_cp = sem("t2_mm"), sem("t2_cp"), sem("b_mm"), sem("b_cp")
    xg_out, xm_in, w_in = sem("xg_out"), sem("xm_in"), sem("w_in")
    wi_in, w_neg, neg_out = sem("wi_in"), sem("w_neg"), sem("neg_out")
    xm_zero = sem("xm_zero")
    mix_mm, mix_v, mix_a = sem("mix_mm"), sem("mix_v"), sem("mix_a")
    ym_out, yg_in = sem("ym_out"), [sem("yg_in0"), sem("yg_in1")]
    yt_mm, yt_cp, d_mm, d_cp = sem("yt_mm"), sem("yt_cp"), sem("d_mm"), sem("d_cp")
    zt_mm, zt_cp = sem("zt_mm"), sem("zt_cp")
    y_mm, y_cp, sq_done, var_mm = sem("y_mm"), sem("y_cp"), sem("sq_done"), sem("var_mm")
    rs_done, st_done, bc_mm, z_done, h_done = (sem("rs_done"), sem("st_done"), sem("bc_mm"), sem("z_done"),
                                               sem("h_done"))
    gb_in = sem("gb_in")
    m1_mm, m1_done, m2_mm, m2_done = sem("m1_mm"), sem("m1_done"), sem("m2_mm"), sem("m2_done")
    m3_mm, m3_cp, tok_out = sem("m3_mm"), sem("m3_cp"), sem("tok_out")

    NT, NA, NT2, NB = NCH, 4, 3, 2
    MQ = MODES // Q
    MC = CH // (2 * C)
    NMIX = -(-MQ // MC)
    NMV, NMA = (NMIX + 1) // 2, NMIX // 2
    NY, ND, NZ = 2, 3, 4
    NST = 5
    NSET = 13 + 10
    NM = 2 * NCH

    def by_row(g, r, n):
        return h[:, g, :].rearrange("p (q r) -> p r q", r=32)[:, r:r + n, :]

    def product_bank(g, c):
        return 2 + c if g == 0 and c < 6 else c % 2

    def back_bank(g, c):
        return c % 2 if g == 0 else 6 + c % 2

    def mixed(c):
        n = min(MC, MQ - c * MC)
        return (ym[:, :, :, c * MC:c * MC + n].rearrange("p r c m -> p m (r c)"),
                bk(c % 2)[:, 0:2 * C * n].rearrange("p (m n) -> p m n", m=n))

    block = ctx.enter_context(nc.Block())

    @block.sync
    def _(sp):
        def load_images(it):
            for g in range(G):
                n = it * BI + g * IG
                sp.dma_start(xin[:, g, :, :], a["x"][slice(n, n + IG) if isinstance(n, int) else bass.ds(n, IG)]
                             .rearrange("i x y c -> i (x y c)").rearrange("i (q r) -> q i r", q=P)).then_inc(x_in, 16)

        load_images(0)
        for half, n in enumerate(("L0_tok_w1i", "L0_tok_w2i")):
            sp.dma_start(wi_raw[:, half, :], a[n].rearrange("l i o x y -> (l i) (o x y)")).then_inc(wi_in, 16)
        consts = [(ident, "k_ident"), (dft_y, "k_dft_y"), (dft_x, "k_dft_x"), (idft_x, "k_idft_x"),
                  (idft_y, "k_idft_y"), (blk, "k_blk"), (centre, "k_centre"), (ones_v, "k_ones_v"),
                  (minus, "k_minus")]
        for t, n in consts:
            sp.dma_start(t[:], a[n]).then_inc(setup_in, 16)
        views = [(sel_f, a["k_sel"]), (fmask, a["k_fmask"]), (mask2, a["k_mask2"]), (f2[:], a["L0_tok_fc2_w"])]
        for t, v in views:
            sp.dma_start(t, v).then_inc(setup_in, 16)
        weights = [(f1_rep, "l_fc1"), (conv_rep, "l_conv"), (cb_raw, "l_cb"), (gam[:], "l_gam"), (bet[:], "l_bet"),
                   (f0_rep, "l_fc0"), (f3_rep, "l_fc3"), (b2[:], "l_b2"), (b1[:], "l_b1"), (b3[:], "l_b3")]
        for t, n in weights:
            sp.dma_start(t, a[n]).then_inc(setup_in, 16)

        def load_mix(layer):
            for half, (wr, wi) in enumerate((("L0_tok_w1r", "L0_tok_w1i"), ("L0_tok_w2r", "L0_tok_w2i"))):
                for ri, pair in enumerate(((wr, wi), (wi, wr))):
                    rows = slice(64 * half + 32 * ri, 64 * half + 32 * ri + 32)
                    for ro in range(2):
                        if ri == 1 and ro == 0:
                            w = scr_w[half, layer] if isinstance(layer, int) else (
                                scr_w[half, bass.ds(layer, 1)].rearrange("l i o m -> (l i) o m"))
                        else:
                            w = a[pair[ro]][layer].rearrange("i o x y -> i o (x y)")
                        sp.dma_start(mix_w[rows, ro, :, :], w).then_inc(w_in, 16)

        def layer_dmas(L, it, nxt):
            for g in range(G):
                sp.wait_ge(b_cp, L * (G * NB) + (g + 1) * NB)
                sp.dma_start(scr_x[IG * g:IG * (g + 1)].rearrange("i c m -> (i c) m"),
                             xg[:].rearrange("p a b c -> p (a b c)")).then_inc(xg_out, 16)
                sp.wait_ge(xg_out, L * (G * 16) + (g + 1) * 16)
                for hr in range(HR):
                    sp.dma_start(xm[C * hr:C * (hr + 1), hr // 2, IG * g:IG * (g + 1), :],
                                 scr_x[IG * g:IG * (g + 1), :, MODES * hr:MODES * (hr + 1)]
                                 .rearrange("i c m -> c i m")).then_inc(xm_in, 16)
            sp.wait_ge(mix_v, L * NMV + NMV)
            sp.wait_ge(mix_a, L * NMA + NMA)
            for ri in range(2):
                sp.dma_start(scr_y[:, ri].rearrange("n i c m -> n i (c m)"),
                             ym[:, ri, :, :].rearrange("p c m -> p (c m)")).then_inc(ym_out, 16)
            sp.wait_ge(ym_out, L * (2 * 16) + 2 * 16)
            for g in range(G):
                if g >= 2:
                    sp.wait_ge(yr_cp, L * G + g - 1)
                sp.dma_start(yg[:, g % 2, :, :].rearrange("p (n x) y -> p n (x y)", x=M1 // Q),
                             scr_y[:, :, IG * g:IG * (g + 1)].rearrange("n r i c m -> (i c) (n r) m")
                             ).then_inc(yg_in[g % 2], 16)
                if g == 1:
                    load_mix(nxt)

        for half in range(2):
            sp.wait_ge(w_neg, half + 1)
            sp.dma_start(scr_w[half].rearrange("l i o m -> (l i) (o m)"), wi_raw[:, half, :]).then_inc(neg_out, 16)
        sp.wait_ge(neg_out, 2 * 16)
        load_mix(0)
        sp.wait_ge(xm_zero, 1)

        def batch(it, last):
            layer_dmas(it * LAYERS, it, 1)
            if not last:
                load_images(it + 1)
            with sp.Fori(1, LAYERS - 1) as l:
                layer_dmas(it * LAYERS + l, it, l + 1)
            layer_dmas(it * LAYERS + LAYERS - 1, it, 0)
            for g in range(G):
                for u in range(2):
                    sp.wait_ge(m3_cp, it * (G * 2) + g * 2 + u + 1)
                    for i in range(2):
                        sp.dma_start(tokens[it * BI + g * IG + 2 * u + i].rearrange("(b q n) -> q b n", b=2, q=4),
                                     tok[i:i + 97:32, :, :]).then_inc(tok_out, 16)

        if batches > 1:
            with sp.Fori(0, batches - 1) as it:
                batch(it, False)
        batch(batches - 1, True)
        sp.wait_ge(tok_out, batches * (G * 4) * 16)
        sp.wait_ge(w_in, (batches * LAYERS + 1) * 8 * 16)

    @block.tensor
    def _(pe):
        mm = nc.tensor.matmul
        pe.wait_ge(setup_in, NSET * 16)
        pe.wait_ge(setup_v, 5)
        for layer in range(LAYERS):
            mm(bk(0)[:, P * layer:P * (layer + 1)], conv_bd[:, layer, :], centre[:], start=True, stop=True)
        mm(bk(1)[:, 0:NORMS], centre[:], cb_raw, start=True, stop=True).then_inc(setup_mm, 1)
        pe.wait_ge(setup_v, 7)

        def variance(M, g, n):
            pe.wait_ge(sq_done, M * (G * 4) + g * 4 + n + 1)
            for k in (2 * n, 2 * n + 1):
                q = k % 4
                m = mm(bk(2 + k // 4)[32 * q:32 * q + 32, :], ones_v[:], sq[:, n % 2, CH * (k % 2):CH * (k % 2 + 1)],
                       start=True, stop=True)
            m.then_inc(var_mm, 1)

        def spread(M, g, k):
            if k == 0:
                pe.wait_ge(st_done, M * (G * NST) + (g + 1) * NST)
            if g or k >= 2:
                pe.wait_ge(z_done, M * (G * NCH) + g * NCH + k - 1)
            mm(bk(4 + k % 2), selb[:, k % 4, :], high[:, k // 4, :], start=True, stop=True).then_inc(bc_mm, 1)

        def norm(M, first, front, product, images):
            first(0)
            for g in range(G):
                front(g)
                for c in range(NCH):
                    if c >= 2:
                        pe.wait_ge(y_cp, M * (G * NCH) + g * NCH + c - 1)
                    product(g, c)
                    if not (images and g == G - 1) and c % 2 and c >= 3:
                        variance(M, g, (c - 3) // 2)
                    if g and c >= 4:
                        spread(M, g - 1, 2 * c - 8)
                        spread(M, g - 1, 2 * c - 7)
                if images and g == G - 1:
                    for n in range(3):
                        variance(M, g, n)
                if g < G - 1:
                    first(g + 1)
                variance(M, g, 3)

        def layer_body(L, M, layer_conv):
            def pointwise(g, c):
                mm(bk(product_bank(g, c)), layer_conv, h[:, g, CH * c:CH * (c + 1)], start=True, stop=False)

            def turn(g, c):
                if c == 0:
                    pe.wait_ge(h_done, M * (G * 2) - G * 2 + (g + 1) * 2)
                if g or c >= 2:
                    pe.wait_ge(t_cp, L * (G * NT) + g * NT + c - 1)
                for j in range(4):
                    m = pe.transpose(bk(c % 2)[:, P * j:P * (j + 1)], h[:, g, CH * c + P * j:CH * c + P * (j + 1)],
                                     ident[:])
                m.then_inc(t_mm, 1)

            def along_y(g, c):
                pe.wait_ge(t_cp, L * (G * NT) + g * NT + c + 1)
                if (g or c >= 4) and c % 2 == 0:
                    pe.wait_ge(a_cp, L * (G * NA) + g * NA + c // 2 - 1)
                for j in range(4):
                    m = mm(wide(bk(6 + (c // 2) % 2), 4 * (c % 2) + j), th[:, c % 4, P * j:P * (j + 1)], dft_y[:],
                           start=True, stop=True)
                if c % 2:
                    m.then_inc(a_mm, 1)

            def along_x(g):
                pe.wait_ge(a_cp, L * (G * NA) + (g + 1) * NA)
                if g == 1:
                    pe.wait_ge(z_done, M * (G * NCH))
                for c in range(NT2):
                    if c >= 2:
                        pe.wait_ge(t2_cp, L * (G * NT2) + g * NT2 + c - 1)
                    for j in range(4):
                        m = pe.transpose(bk(4 + c % 2)[:, P * j:P * (j + 1)],
                                         ya[:, 4 * c + j, :, :].rearrange("p x r -> p (x r)"), ident[:])
                    m.then_inc(t2_mm, 1)
                if g == 0:
                    pe.wait_ge(st_done, M * (G * NST) - NST + 1)
                else:
                    pe.wait_ge(b_cp, L * (G * NB) + g * NB)
                for c in range(NB):
                    pe.wait_ge(t2_cp, L * (G * NT2) + g * NT2 + 2 + c)
                    for j in range(6):
                        m = mm(wide(bk(2 + c), j), xa[:, 6 * c + j, :], dft_x[:], start=True, stop=True)
                    m.then_inc(b_mm, 1)

            turn(0, 0)
            turn(0, 1)
            for g in range(G):
                for c in range(NT):
                    if c < NT - 2:
                        turn(g, c + 2)
                    along_y(g, c)
                    if g == 1:
                        spread(M - 1, G - 1, c)
                if g < G - 1:
                    turn(g + 1, 0)
                    turn(g + 1, 1)
                along_x(g)
            pe.wait_ge(conv_in, L + 1)
            pe.wait_ge(b_cp, L * (G * NB) + G * NB)
            for c in range(4):
                pointwise(0, c)
            pe.wait_ge(xm_in, L * (G * HR * 16) + G * HR * 16)
            wait_alone(pe, w_in, L * (8 * 16) + 8 * 16, pe_passed)
            for c in range(NMIX):
                if c >= 2:
                    n = c - 2
                    if n % 2:
                        pe.wait_ge(mix_a, L * NMA + n // 2 + 1)
                    else:
                        pe.wait_ge(mix_v, L * NMV + n // 2 + 1)
                for j in range(min(MC, MQ - c * MC)):
                    for q in range(Q):
                        k = q * MQ + c * MC + j
                        m = mm(bk(c % 2)[32 * q:32 * (q + 1), 2 * C * j:2 * C * (j + 1)],
                               xm[:, :, :, k].rearrange("p a b -> p (a b)"),
                               mix_w[:, :, :, k].rearrange("p a b -> p (a b)"), start=True, stop=True)
                m.then_inc(mix_mm, 1)
            for c in (4, 5):
                pointwise(0, c)

            def first(g):
                pe.wait_ge(yr_cp, L * G + g + 1)
                for c in range(NY):
                    for j in range(3):
                        m = mm(bk(back_bank(g, c))[0:96, P * j:P * (j + 1)],
                               yr[:, 3 * c + j, :, :].rearrange("p a b -> p (a b)"), centre[:], start=True, stop=True)
                    m.then_inc(yt_mm, 1)

            def front(g):
                for c in range(ND):
                    pe.wait_ge(yt_cp, L * (G * NY) + g * NY + (2 * c + 1) // 3 + 1)
                    if c >= 2:
                        pe.wait_ge(d_cp, L * (G * ND) + g * ND + c - 1)
                    elif g and c == 0:
                        pe.wait_ge(y_cp, M * (G * NCH) + g * NCH)
                    for j in range(2):
                        m = mm(bk(c % 2)[:, 256 * j:256 * j + 256], yt[:, 2 * c + j, :], idft_x[:],
                               start=True, stop=True)
                    m.then_inc(d_mm, 1)
                if g:
                    pe.wait_ge(d_cp, L * (G * ND) + g * ND + 2)
                    pointwise(g, 1)
                pe.wait_ge(d_cp, L * (G * ND) + (g + 1) * ND)
                for c in range(NZ):
                    if c >= 2:
                        pe.wait_ge(zt_cp, L * (G * NZ) + g * NZ + c - 1)
                    for j in range(4):
                        k = 4 * c + j
                        m = pe.transpose(bk(back_bank(g, c))[0:96, P * j:P * (j + 1)],
                                         zx[:, 4 * k:4 * k + 4, :].rearrange("p x r -> p (x r)"), ident[:])
                    m.then_inc(zt_mm, 1)

            def product(g, c):
                if c != 1 and (g or c >= 6):
                    pointwise(g, c)
                pe.wait_ge(zt_cp, L * (G * NZ) + g * NZ + c // 2 + 1)
                for j in range(2):
                    m = mm(bk(product_bank(g, c))[:, 256 * j:256 * j + 256], zt[:, 2 * c + j, :], idft_y[:],
                           start=False, stop=(j == 1))
                m.then_inc(y_mm, 1)

            norm(M, first, front, product, False)

        with pe.Fori(0, batches) as it:
            M0 = it * NORMS

            def first0(g):
                pe.wait_ge(xr_cp, it * G + g + 1)
                for o in range(4):
                    m = pe.transpose(bk(6)[0:96, P * o:P * (o + 1)], xr[:, o, :, :].rearrange("p i r -> p (i r)"),
                                     ident[:])
                m.then_inc(xt_mm, 1)

            def product0(g, c):
                if c == 0:
                    pe.wait_ge(xt_cp, it * G + g + 1)
                for j in range(4):
                    r = 4 * c + j
                    m = mm(bk(c % 2)[:, P * j:P * (j + 1)], f0[:, r % RO, :], xt[:, r // RO, :],
                           start=True, stop=True)
                m.then_inc(y_mm, 1)

            norm(M0, first0, lambda g: None, product0, True)
            with pe.Fori(0, LAYERS) as l:
                layer_body(it * LAYERS + l, it * NORMS + l + 1, conv_l[:])

            for g in range(G):
                if g == 1:
                    for k in range(NCH):
                        spread(it * NORMS + LAYERS, G - 1, k)
                    pe.wait_ge(z_done, (it * NORMS + NORMS) * (G * NCH))
                pe.wait_ge(h_done, (it * NORMS + LAYERS) * (G * 2) + (g + 1) * 2)
                for n in range(NM + 2):
                    if n < NM:
                        u, k = divmod(n, NCH)
                        if n >= 2:
                            pe.wait_ge(m1_done, it * (G * NM) + g * NM + n - 1)
                        if g == 0 and n == 1:
                            pe.wait_ge(st_done, (it * NORMS + NORMS) * (G * NST) - NST + 1)
                        for i in range(2):
                            m = mm(bk(2 * (n % 2) + i), f1[:, 2 * u + i, :], h[:, g, CH * k:CH * (k + 1)],
                                   start=True, stop=True)
                        m.then_inc(m1_mm, 1)
                    if 1 <= n <= NM:
                        b = n - 1
                        pe.wait_ge(m1_done, it * (G * NM) + g * NM + b + 1)
                        if g or b >= 2:
                            pe.wait_ge(m2_done, it * (G * NM) + g * NM + b - 1)
                        for i in range(2):
                            m = mm(bk(4 + b % 2)[64 * i:64 * i + 64, :], f2[:], g1[:, b % 2, CH * i:CH * (i + 1)],
                                   start=True, stop=True)
                        m.then_inc(m2_mm, 1)
                    if n >= 2:
                        b = n - 2
                        u, k = divmod(b, NCH)
                        pe.wait_ge(m2_done, it * (G * NM) + g * NM + b + 1)
                        if k == 0 and (g or u):
                            pe.wait_ge(m3_cp, it * (G * 2) + g * 2 + u)
                        q = k % 4
                        m = mm(bk(6 + k // 4)[32 * q:32 * q + 32, :], f3[:], g2[:, b % 2, :], start=True, stop=True)
                        if k == NCH - 1:
                            m.then_inc(m3_mm, 1)
            pe.wait_ge(m3_cp, it * (G * 2) + G * 2)

    @block.vector
    def _(dve):
        v = nc.vector
        dve.wait_ge(setup_in, NSET * 16)
        v.tensor_copy(selb[:].rearrange("p a b -> p (a b)"), sel_f).then_inc(setup_v, 1)
        v.tensor_tensor(f1[:], f1_rep.rearrange("p (a n) -> p a n", a=1).broadcast_to([P, IG, HID1]),
                        blk[:].rearrange("p (a n) -> p a n", n=1).broadcast_to([P, IG, HID1]), ALU.mult
                        ).then_inc(setup_v, 1)
        v.tensor_tensor(f3[:], mask2, f3_rep.broadcast_to([P, 32]), ALU.mult).then_inc(setup_v, 1)
        for i in range(IG):
            m = v.tensor_scalar(conv_bd[:, :, C * i:C * (i + 1)], conv_rep.rearrange("p (l c) -> p l c", l=LAYERS),
                                blk[:, i:i + 1], None, ALU.mult)
        m.then_inc(setup_v, 1)
        v.reduce_sum(f0_sum, f0_rep, AX_X).then_inc(setup_v, 1)
        dve.wait_ge(setup_v, 5)
        v.scalar_tensor_tensor(out=f0_rep, in0=f0_sum.broadcast_to([96, C]), scalar=-1.0 / C, in1=f0_rep,
                               op0=ALU.mult, op1=ALU.add).then_inc(setup_g, 1)
        dve.wait_ge(setup_g, 1)
        v.tensor_tensor(f0[:].rearrange("p r (i c) -> p (r i) c", i=IG),
                        f0_rep.rearrange("p (a c) -> p a c", a=1).broadcast_to([96, RO * IG, C]),
                        fmask.rearrange("p (n a) -> p n a", a=1).broadcast_to([96, RO * IG, C]), ALU.mult
                        ).then_inc(setup_g, 1)
        v.memset(xm[:].rearrange("p a b c -> p (a b c)"), 0.0).then_inc(xm_zero, 1)
        dve.wait_ge(wi_in, 2 * 16)
        for half in range(2):
            v.tensor_scalar(wi_raw[:, half, :], wi_raw[:, half, :], -1.0, None, ALU.mult).then_inc(w_neg, 1)
        dve.wait_ge(setup_mm, 1)
        v.tensor_copy(conv[:].rearrange("p a b -> p (a b)"), bk(0)).then_inc(setup_v, 1)
        v.tensor_copy(cb[:], bk(1)[:, 0:NORMS]).then_inc(setup_v, 1)
        dve.wait_ge(setup_v, 7)
        dve.wait_ge(setup_g, 2)
        dve.wait_ge(neg_out, 2 * 16)

        def stat_step(M, g, n):
            if n == 0:
                dve.wait_ge(rs_done, M * G + g + 1)
                m = v.scalar_tensor_tensor(out=newt[:], in0=bank[1][:, :, :], scalar=EPS, in1=rstd[:], op0=ALU.add,
                                           op1=ALU.mult)
            else:
                dve.wait_ge(st_done, M * (G * NST) + g * NST + n)
            if n == 1:
                m = v.scalar_tensor_tensor(out=newt[:], in0=newt[:], scalar=-0.5, in1=rstd[:], op0=ALU.mult,
                                           op1=ALU.mult)
            elif n == 2:
                m = v.scalar_tensor_tensor(out=rstd[:], in0=newt[:], scalar=1.5, in1=rstd[:], op0=ALU.add, op1=ALU.mult)
            elif n == 3:
                m = v.scalar_tensor_tensor(out=newt[:], in0=high, scalar=minus[:, 0:1], in1=rstd[:], op0=ALU.mult,
                                           op1=ALU.add)
            elif n == 4:
                m = v.scalar_tensor_tensor(out=rstd[:], in0=newt_high, scalar=minus[:, 1:2], in1=newt[:], op0=ALU.mult,
                                           op1=ALU.add)
            m.then_inc(st_done, 1)

        def scale(M, g, k, images=False):
            dve.wait_ge(bc_mm, M * (G * NCH) + g * NCH + k + 1)
            hc, by = h[:, g, CH * k:CH * (k + 1)], bk(4 + k % 2)
            if images:
                hc, by = by_row(g, 4 * k, 4), by.rearrange("p (r q) -> p r q", r=4)
            v.tensor_tensor(hc, by, hc, ALU.mult).then_inc(z_done, 1)

        def norm(M, before, front, copy_out, images=False):
            before(0)
            for g in range(G):
                front(g)
                if g:
                    stat_step(M, g - 1, 0)
                    stat_step(M, g - 1, 1)
                for c in range(NCH):
                    dve.wait_ge(y_mm, M * (G * NCH) + g * NCH + c + 1)
                    copy_out(g, c).then_inc(y_cp, 1)
                    if g and c + 2 < NST:
                        stat_step(M, g - 1, c + 2)
                    if c == 3 and g < G - 1:
                        before(g + 1)
                    if g and c >= 4:
                        scale(M, g - 1, 2 * c - 8, images)
                        scale(M, g - 1, 2 * c - 7, images)

        def layer_body(L, M, bias):
            def turned(g, c):
                dve.wait_ge(t_mm, L * (G * NT) + g * NT + c + 1)
                v.tensor_copy(th[:, c % 4, :], bk(c % 2)).then_inc(t_cp, 1)

            for g in range(G):
                for c in range(NT):
                    if g == 0 or c >= 2:
                        turned(g, c)
                    if g == 0 and 0 <= c - 2 < NST:
                        stat_step(M - 1, G - 1, c - 2)
                    if g == 1 and c >= 2:
                        scale(M - 1, G - 1, c - 2)
                if g == 1:
                    scale(M - 1, G - 1, NCH - 2)
                    scale(M - 1, G - 1, NCH - 1)
                if g < G - 1:
                    turned(g + 1, 0)
                    turned(g + 1, 1)
                for c in range(NB):
                    dve.wait_ge(b_mm, L * (G * NB) + g * NB + c + 1)
                    if g and c == 0:
                        dve.wait_ge(xg_out, L * (G * 16) + g * 16)
                    v.tensor_copy(xg[:, :, :, 6 * c:6 * c + 6].rearrange("p h x y -> p y h x"),
                                  bk(2 + c)[:, 0:288].rearrange("p (y h x) -> p y h x", y=6, h=HR)
                                  ).then_inc(b_cp, 1)
            for c in range(0, NMIX, 2):
                dve.wait_ge(mix_mm, L * NMIX + c + 1)
                v.tensor_copy(*mixed(c)).then_inc(mix_v, 1)

            def before(g):
                dve.wait_ge(yg_in[g % 2], L * 32 + (g // 2 + 1) * 16)
                if g:
                    dve.wait_ge(yt_mm, L * (G * NY) + g * NY)
                v.tensor_copy(yr[:], yg[:, g % 2, :, :].rearrange("p n (k y) -> p k n y", y=2)).then_inc(yr_cp, 1)

            def front(g):
                for c in range(ND):
                    dve.wait_ge(d_mm, L * (G * ND) + g * ND + c + 1)
                    v.tensor_copy(zx[:, :, 8 * c:8 * c + 8].rearrange("p x (k f) -> p k x f", k=2),
                                  bk(c % 2).rearrange("p (k x f) -> p k x f", k=2, x=S)).then_inc(d_cp, 1)

            dve.wait_ge(conv_in, L + 1)
            norm(M, before, front, lambda g, c: v.tensor_scalar(
                h[:, g, CH * c:CH * (c + 1)], bk(product_bank(g, c)), bias, None, ALU.add))

        with dve.Fori(0, batches) as it:
            norm(it * NORMS, lambda g: None, lambda g: None,
                 lambda g, c: v.tensor_scalar(by_row(g, 4 * c, 4), bk(c % 2).rearrange("p (r q) -> p r q", r=4),
                                              cb[:, 0:1], None, ALU.add), True)
            with dve.Fori(0, LAYERS) as l:
                layer_body(it * LAYERS + l, it * NORMS + l + 1, cb_l[:, 0:1])
            for n in range(NST):
                stat_step(it * NORMS + LAYERS, G - 1, n)
            for g in range(G):
                if g == 1:
                    for k in range(NCH):
                        scale(it * NORMS + LAYERS, G - 1, k)
                for u in range(2):
                    n = g * 2 + u
                    dve.wait_ge(m3_mm, it * (G * 2) + n + 1)
                    if n:
                        dve.wait_ge(tok_out, it * (G * 2 * 32) + n * 32)
                    v.tensor_scalar(tok, bank[3][:, :, :], b3[:, 0:1], None, ALU.add).then_inc(m3_cp, 1)
            dve.wait_ge(tok_out, it * (G * 2 * 32) + G * 2 * 32)

    @block.scalar
    def _(act):
        s = nc.scalar
        act.wait_ge(setup_in, NSET * 16)
        s.activation(epst[:], ident[:, 0:1], ACT.Copy, bias=EPS, scale=0.0).then_inc(eps_set, 1)
        act.wait_ge(eps_set, 1)
        act.wait_ge(setup_v, 7)

        def copy(dst, src):
            return s.activation(dst, src, ACT.Copy)

        def estimate(M, g):
            act.wait_ge(var_mm, M * (G * 4) + (g + 1) * 4)
            s.activation(rstd[:], bank[1][:, :, :], ACT.Abs_reciprocal_sqrt, bias=epst[:, 0:1]).then_inc(rs_done, 1)

        def final(M, g, n, func, gamma, beta):
            act.wait_ge(z_done, M * (G * NCH) + g * NCH + 4 * n + 4)
            hh = h[:, g, 2048 * n:2048 * (n + 1)]
            s.activation(hh, hh, func, bias=beta, scale=gamma).then_inc(h_done, 1)

        def norm(M, front, rest, func, gamma, beta, images):
            front(0)
            for g in range(G):
                if g:
                    estimate(M, g - 1)
                rest(g)
                for n in range(4):
                    act.wait_ge(y_cp, M * (G * NCH) + g * NCH + (NCH if images and g == G - 1 else 2 * n + 2))
                    if n >= 2:
                        act.wait_ge(var_mm, M * (G * 4) + g * 4 + n - 1)
                    if images and g < G - 1:
                        s.activation(sq[:, n % 2, :].rearrange("p (r q) -> p r q", r=8), by_row(g, 8 * n, 8), ACT.Square
                                     ).then_inc(sq_done, 1)
                    else:
                        s.activation(sq[:, n % 2, :], h[:, g, 1024 * n:1024 * (n + 1)], ACT.Square).then_inc(sq_done, 1)
                    if n == 3 and g < G - 1:
                        front(g + 1)
                    if g and n >= 2 and not images:
                        final(M, g - 1, n - 2, func, gamma, beta)
                    if g >= 2 and n in (0, 2) and images:
                        final(M, g - 2, n // 2, func, gamma, beta)
            if images:
                act.wait_ge(z_done, M * (G * NCH) + (G - 1) * NCH)
                final(M, G - 2, 0, func, gamma, beta)
                final(M, G - 2, 1, func, gamma, beta)

        def layer_weights(L, l, M):
            act.wait_ge(y_cp, M * (G * NCH))
            copy(conv_l[:], conv[:, l, :] if isinstance(l, int) else
                 conv[:, bass.ds(l, 1), :].rearrange("p a b -> p (a b)"))
            copy(cb_l[:], cb[:, l + 1:l + 2] if isinstance(l, int) else cb[:, bass.ds(l + 1, 1)]).then_inc(conv_in, 1)

        def layer_body(L, l, M, pending, func):
            layer_weights(L, l, M)
            estimate(M - 1, G - 1)
            for g in range(G):
                for c in range(NA):
                    act.wait_ge(a_mm, L * (G * NA) + g * NA + c + 1)
                    copy(ya[:, :, 16 * c:16 * c + 16, :].rearrange("p k x r -> p x k r"),
                         bk(6 + c % 2)[:, 0:384].rearrange("p (x k r) -> p x k r", x=16, k=M2)).then_inc(a_cp, 1)
                for c in range(NT2):
                    act.wait_ge(t2_mm, L * (G * NT2) + g * NT2 + c + 1)
                    copy(xa[:, 4 * c:4 * c + 4, :].rearrange("p a b -> p (a b)"), bk(4 + c % 2)).then_inc(t2_cp, 1)
                if g == 1:
                    final(M - 1, G - 1, 0, *pending)
                    final(M - 1, G - 1, 1, *pending)
                    act.wait_ge(h_done, M * (G * 2))
                    for n, t in enumerate((gam, bet)):
                        m = copy(gb_l[:, n:n + 1], t[:, l + 1:l + 2] if isinstance(l, int) else t[:, bass.ds(l + 1, 1)])
                        m.then_inc(gb_in, 1)
                    act.wait_ge(gb_in, L * 2 + 2)
            for c in range(1, NMIX, 2):
                act.wait_ge(mix_mm, L * NMIX + c + 1)
                copy(*mixed(c)).then_inc(mix_a, 1)

            def front(g):
                for c in range(NY):
                    act.wait_ge(yt_mm, L * (G * NY) + g * NY + c + 1)
                    copy(yt[:, 3 * c:3 * c + 3, :].rearrange("p a b -> p (a b)"), bk(back_bank(g, c))[0:96, 0:384]
                         ).then_inc(yt_cp, 1)

            def rest(g):
                for c in range(NZ):
                    act.wait_ge(zt_mm, L * (G * NZ) + g * NZ + c + 1)
                    copy(zt[:, 4 * c:4 * c + 4, :].rearrange("p a b -> p (a b)"), bk(back_bank(g, c))[0:96, :]
                         ).then_inc(zt_cp, 1)

            norm(M, front, rest, func, gb_l[:, 0:1], gb_l[:, 1:2], False)

        with act.Fori(0, batches) as it:
            def front0(g):
                act.wait_ge(x_in, it * (G * 16) + G * 16)
                copy(xr[:], xin[:, g, :, :].rearrange("p i (o r) -> p o i r", o=4)).then_inc(xr_cp, 1)
                act.wait_ge(xt_mm, it * G + g + 1)
                copy(xt[:].rearrange("p a b -> p (a b)"), bk(6)[0:96, :]).then_inc(xt_cp, 1)

            affine = (ACT.Identity, gam[:, 0:1], bet[:, 0:1])
            gelu = (ACT.Gelu, gb_l[:, 0:1], gb_l[:, 1:2])
            norm(it * NORMS, front0, lambda g: None, *affine, True)
            layer_body(it * LAYERS, 0, it * NORMS + 1, affine, ACT.Gelu)
            with act.Fori(1, LAYERS - 1) as l:
                layer_body(it * LAYERS + l, l, it * NORMS + l + 1, gelu, ACT.Gelu)
            layer_body(it * LAYERS + LAYERS - 1, LAYERS - 1, it * NORMS + LAYERS, gelu, ACT.Identity)
            estimate(it * NORMS + LAYERS, G - 1)
            for g in range(G):
                if g == 1:
                    for n in range(2):
                        final(it * NORMS + LAYERS, G - 1, n, ACT.Identity, gb_l[:, 0:1], gb_l[:, 1:2])
                for n in range(NM + 1):
                    if n < NM:
                        act.wait_ge(m1_mm, it * (G * NM) + g * NM + n + 1)
                        s.activation(g1[:, n % 2, :], bank[n % 2][:, :, :], ACT.Gelu, bias=b1[:, 0:1]
                                     ).then_inc(m1_done, 1)
                    if n:
                        act.wait_ge(m2_mm, it * (G * NM) + g * NM + n)
                        s.activation(g2[:, (n - 1) % 2, :], bk(4 + (n - 1) % 2), ACT.Gelu, bias=b2[:, 0:1]
                                     ).then_inc(m2_done, 1)


D = 64
HEADS, HD, HP = 4, 16, 32
MAX_REL = 30
TL = 8
ROUNDS = NIMG // (2 * TL)
RT = TL * P
FH = 4 * D
KEPT = S // 2 - 1


def attention_constants():
    f4 = np.float32
    pos = np.arange(2 * MAX_REL + 1, dtype=f4)[:, None]
    div = np.exp(np.arange(0, D, 2, dtype=f4) * f4(-np.log(10000.0) / D)).astype(f4)
    ang = (pos * div).astype(f4)
    enc = np.stack([np.sin(ang), np.cos(ang)], -1).reshape(-1, D)
    near = np.clip(np.arange(2 * S - 1) - (S - 1), -MAX_REL, MAX_REL) + MAX_REL
    enc_t = np.concatenate([enc[near].T, np.ones((1, 2 * S - 1))])
    t = np.arange(P) % S
    before = (np.arange(S)[None, :] < t[:, None])
    out = dict(k_enc=enc_t, k_before=before)
    return {k: np.ascontiguousarray(v, np.float32) for k, v in out.items()}


def attention_layouts(a):
    w_p = np.zeros((HEADS, HP, 5, D + 1), np.float32)
    for n, (wn, bn) in enumerate((("Wq", "bq"), ("Wq", "bq"), ("Wk", "bk"), ("Wv", "bv"), ("Wpos", "bpos"))):
        w_p[:, :HD, n, :D] = a["L0_attn_" + wn].reshape(HEADS, HD, D)
        w_p[:, :HD, n, D] = a["L0_attn_" + bn].reshape(HEADS, HD)
    uv = np.zeros((HEADS, HP, 2), np.float32)
    for n, un in enumerate(("u_bias", "v_bias")):
        uv[:, :HD, n] = a["L0_attn_" + un].reshape(HEADS, HD)
    wo = np.zeros((D, HEADS, HP), np.float32)
    wo[:, :, :HD] = a["L0_attn_Wo"].reshape(D, HEADS, HD)
    rows = np.stack([a["L0_attn_ln_gamma"], a["L0_attn_ln_beta"], a["L0_attn_bo"], a["L0_ffn_wr"][:, 0],
                     a["L0_ffn_b2"]])
    return dict(l_wp=w_p.reshape(P, 5, D + 1), l_uv=uv.reshape(P, 2), l_wo=wo, l_rows=rows.reshape(1, 5 * D))


def attention_and_ffn(nc, ctx, a, tokens, out):
    def sb(name, shape, dt=F32):
        return ctx.enter_context(nc.sbuf_tensor(name, shape, dt))

    def sem(name):
        return ctx.enter_context(nc.semaphore(name))

    bank = [ctx.enter_context(nc.psum_tensor(f"pbank{i}", [P, 2, CH], F32)) for i in range(4)]

    def bk(n):
        return bank[n // 2][:, n % 2, :]

    ident, blk, before = sb("ident2", [P, P]), sb("blk2", [P, IG]), sb("before", [P, S])
    enc_t = sb("enc_t", [D + 1, 2 * S - 1])
    w_p, bias_uv = sb("w_p", [P, 5, D + 1]), sb("bias_uv", [P, 2])
    w_t = sb("w_t", [D + 1, 5, P])
    wo_p, wo_t = sb("wo_p", [D, HEADS, HP]), sb("wo_t", [P, D])
    pos_t, pos_bd = sb("pos_t", [P, 2 * S - 1]), sb("pos_bd", [P, HEADS, 2 * S - 1])
    rows = sb("rows", [P, 5, D])
    br = sb("br", [P, 1])
    w1, w2, fb1 = sb("w1s", [D, FH]), sb("w2s", [P, 2, D]), sb("fb1", [P, 2])

    ht, xa, tmp = sb("ht", [P, TL, D]), sb("xa2", [P, TL, D]), sb("tmp", [P, TL, D])
    ln_s = sb("ln_s", [P, 4, TL])
    xn_t = sb("xn_t", [D, NIMG * S])
    x_t = sb("x_t", [D + 1, RT])
    x5_t = sb("x5_t", [D, RT])
    qv = sb("qv", [P, NIMG, S])
    pos_s = sb("pos_s", [P, 2, TL, HEADS * S])
    pos_in = sb("pos_in", [P, TL, HEADS * S])
    q, k = sb("q", [P, RT]), sb("kk", [P, RT])
    val = sb("val", [S, 2 * TL, P])
    att = sb("att", [P, HEADS, TL, S])
    stat = sb("stat", [P, 2, HEADS, TL])
    att_t = sb("att_t", [S, TL, HEADS, P])
    ctx_t = sb("ctx_t", [P, RT])
    h4, x5 = sb("h4", [P, TL, D]), sb("x5", [P, TL, D])
    w, coef = sb("wgt", [P, TL]), sb("coef", [P, TL])
    above, same = sb("above", [P, TL, S]), sb("same", [P, TL, S])
    hid = sb("hid", [P, 2, 2, CH])

    scr_p = a["scr_p"]
    tok_v = tokens.rearrange("i (t d) -> (i t) d", d=D).rearrange("(n p) d -> p n d", p=P)
    out_v = out.rearrange("i t d -> (i t) d").rearrange("(n p) d -> p n d", p=P)
    pos_v = scr_p.rearrange("i t m -> (i t) m").rearrange("(n p) m -> p n m", p=P)

    s2_in, ones_set, s2_v, s2_mm = sem("s2_in"), sem("ones_set"), sem("s2_v"), sem("s2_mm")
    a_x, a_xt, a_xtc, a_q, a_qc, a_var, a_rs = (sem("a_x"), sem("a_xt"), sem("a_xtc"), sem("a_q"),
                                                      sem("a_qc"), sem("a_var"), sem("a_rs"))
    a_in = [sem("a_in0"), sem("a_in1")]
    pe_passed, sp_passed = sem("pe_passed"), sem("sp_passed")
    buffers = ((ht, xa), (h4, x5))
    p_mm, p_v, p_a, p_out = sem("p_mm"), sem("p_v"), sem("p_a"), [sem("p_out0"), sem("p_out1")]
    names = ("tok_in pos_ld xt_c qk_mm q_c k_c val_mm val_c score_mm shifted exp_c att_n at_mm0 at_mm1 "
             "at_c0 at_c1 ctx_mm ctx_c wo_mm x5_ready x5t_mm x5t_c w_ready wt_mm hid_mm hid_c y2_mm res "
             "out_st seq_a seq_t seq_f b_var b_rs h4_ready wo_read wt_read").split()
    s = {n: sem("b_" + n) for n in names}
    block = ctx.enter_context(nc.Block())
    NSET = 4 + 3 + 1 + 4

    @block.sync
    def _(sp):
        for t, n in ((ident, "k_ident"), (blk, "k_blk"), (before, "k_before"), (enc_t, "k_enc"), (w_p, "l_wp"),
                     (bias_uv, "l_uv"), (wo_p, "l_wo")):
            sp.dma_start(t[:], a[n]).then_inc(s2_in, 16)
        sp.dma_start(rows[:].rearrange("p a d -> p (a d)"), a["l_rows"].broadcast_to([P, 5 * D])).then_inc(s2_in, 16)
        with nc.allow_non_contiguous_dma(reason="a few small weights"):
            sp.dma_start(br[:], a["L0_ffn_br"].rearrange("(a b) -> a b", a=1).broadcast_to([P, 1])).then_inc(s2_in, 16)
            sp.dma_start(w1[:], a["L0_ffn_w1"]).then_inc(s2_in, 16)
            sp.dma_start(w2[:], a["L0_ffn_w2"].rearrange("(n p) d -> p n d", p=P)).then_inc(s2_in, 16)
            sp.dma_start(fb1[:], a["L0_ffn_b1"].rearrange("(n p) -> p n", p=P)).then_inc(s2_in, 16)
        for u in range(2):
            sp.dma_start(buffers[u][0][:], tok_v[:, u * TL:(u + 1) * TL, :]).then_inc(a_in[u], 16)
        with sp.Fori(1, ROUNDS // 2) as oo:
            for u in range(2):
                wait_alone(sp, a_x, oo * 2 + u - 1, sp_passed)
                sp.dma_start(buffers[u][0][:], tok_v[:, bass.ds(oo * (2 * TL) + u * TL, TL), :]).then_inc(a_in[u], 16)
        for n in range(S // TL):
            sp.wait_ge(p_v, 2 * (n + 1))
            sp.wait_ge(p_a, 2 * (n + 1))
            sp.dma_start(scr_p[:, TL * n:TL * (n + 1), :], pos_s[:, n % 2, :, :]).then_inc(p_out[n % 2], 16)
        for n in range(2):
            sp.wait_ge(p_out[n], 16 * (S // TL // 2))
        sp.dma_start(ht[:], tok_v[:, 0:TL, :]).then_inc(s["tok_in"], 16)
        sp.dma_start(pos_in[:], pos_v[:, 0:TL, :]).then_inc(s["pos_ld"], 16)
        def step(o, last):
            wait_alone(sp, s["h4_ready"], o, sp_passed)
            sp.dma_start(ht[:], tok_v[:, bass.ds(o * TL, TL), :]).then_inc(s["tok_in"], 16)
            if not last:
                wait_alone(sp, s["shifted"], o + 1, sp_passed)
                sp.dma_start(pos_in[:], pos_v[:, bass.ds(o * TL + TL, TL), :]).then_inc(s["pos_ld"], 16)
            wait_alone(sp, s["res"], o, sp_passed)
            sp.dma_start(out_v[:, bass.ds(o * TL - TL, TL), :], xa[:]).then_inc(s["out_st"], 16)

        sp.wait_ge(s["shifted"], 1)
        sp.dma_start(pos_in[:], pos_v[:, TL:2 * TL, :]).then_inc(s["pos_ld"], 16)
        with sp.Fori(1, ROUNDS - 1) as o:
            step(o, False)
        step(ROUNDS - 1, True)
        sp.wait_ge(s["res"], ROUNDS)
        sp.dma_start(out_v[:, NIMG * S // P - TL:, :], xa[:]).then_inc(s["out_st"], 16)
        sp.wait_ge(s["out_st"], ROUNDS * 16 + 1)

    @block.tensor
    def _(pe):
        mm = nc.tensor.matmul
        pe.wait_ge(s2_in, NSET * 16)
        pe.wait_ge(s2_v, 1)
        for n in range(5):
            pe.transpose(bk(n // 4)[0:D + 1, P * (n % 4):P * (n % 4 + 1)], w_p[:, n, :], ident[:])
        pe.transpose(bk(2)[:, 0:D], wo_p[:].rearrange("p a b -> p (a b)"), ident[0:D, 0:D]).then_inc(s2_mm, 1)
        pe.wait_ge(s2_v, 3)
        mm(bk(3)[:, 0:2 * S - 1], w_t[:, 4, :], enc_t[:], start=True, stop=True).then_inc(s2_mm, 1)
        pe.wait_ge(s2_v, 5)

        def transposes(src, done):
            for n in range(TL):
                m = pe.transpose(bk(n // 4)[0:D, P * (n % 4):P * (n % 4 + 1)], src[:, n, :], ident[:])
            m.then_inc(done, 1)

        def inputs(o, u, first):
            wait_alone(pe, a_x, o + 1, pe_passed)
            transposes(buffers[u][1], a_xt)
            pe.wait_ge(a_xtc, o + 1)
            if not first:
                pe.wait_ge(a_qc, o)
            for n in range(2):
                m = mm(bk(2 + n), w_t[:, 1, :], x_t[:, CH * n:CH * (n + 1)], start=True, stop=True)
            m.then_inc(a_q, 1)

        pe.sem_inc(a_xt, 2)
        inputs(0, 0, True)
        inputs(1, 1, False)
        with pe.Fori(1, ROUNDS // 2) as oo:
            for u in range(2):
                inputs(oo * 2 + u, u, False)
        pe.wait_ge(a_qc, ROUNDS)
        for t in range(S):
            c = t // 2
            if c >= 8 and t % 2 == 0:
                pe.wait_ge(p_v if c % 2 == 0 else p_a, (c - 8) // 2 + 1)
            m = mm(bk(c % 8)[:, 256 * (t % 2):256 * (t % 2) + 256], qv[:, :, t], pos_bd[:, :, S - 1 - t:2 * S - 1 - t],
                   start=True, stop=True)
            if t % 2:
                m.then_inc(p_mm, 1)
        pe.wait_ge(p_v, S // 4)
        pe.wait_ge(p_a, S // 4)
        def rounds(t, f):
            if t is not None:
                wait_alone(pe, s["att_n"], t + 1, pe_passed)
                wait_alone(pe, s["val_c"], t + 1, pe_passed)
                wait_alone(pe, s["h4_ready"], t + 1, pe_passed)
                for n in range(TL):
                    for hd in range(HEADS):
                        b = (6, 7, 0, 1, 2, 3, 4, 5)[n]
                        m = pe.transpose(bk(b)[0:S, P * hd:P * (hd + 1)], att[:, hd, n, :], ident[:])
                    if n == 3:
                        m.then_inc(s["at_mm0"], 1)
                m.then_inc(s["at_mm1"], 1)
                wait_alone(pe, s["at_c0"], t + 1, pe_passed)
                wait_alone(pe, s["at_c1"], t + 1, pe_passed)
                for n in range(2 * TL):
                    for hd in range(HEADS):
                        m = mm(bk(n // 8)[HP * hd:HP * (hd + 1), S * (n % 8):S * (n % 8) + S],
                               val[:, n, HP * hd:HP * (hd + 1)],
                               att_t[:, n // 2, hd, S * (n % 2):S * (n % 2) + S], start=True, stop=True)
                m.then_inc(s["ctx_mm"], 1)
                pe.wait_ge(s["ctx_c"], t + 1)
                for n in range(TL):
                    m = mm(bk(6)[:, D * n:D * (n + 1)], ctx_t[:, P * n:P * (n + 1)], wo_t[:], start=True, stop=True)
                m.then_inc(s["wo_mm"], 1)
            if f is not None:
                wait_alone(pe, s["xt_c"], f + 1, pe_passed)
                for n in range(2):
                    mm(bk(2 + n), w_t[:, 0, :], x_t[:, CH * n:CH * (n + 1)], start=True, stop=True)
                    m = mm(bk(4 + n), w_t[:, 2, :], x_t[:, CH * n:CH * (n + 1)], start=True, stop=True)
                m.then_inc(s["qk_mm"], 1)
                if t is not None:
                    pe.wait_ge(s["wo_read"], t + 1)
                for n in range(2 * TL):
                    b = (6, 7, 0, 1)[n // 4]
                    m = mm(bk(b)[0:S, P * (n % 4):P * (n % 4 + 1)], x_t[:, S * n:S * (n + 1)], w_t[:, 3, :],
                           start=True, stop=True)
                m.then_inc(s["val_mm"], 1)
            if t is not None:
                wait_alone(pe, s["x5_ready"], t + 1, pe_passed)
                if f is not None:
                    wait_alone(pe, s["val_c"], f + 1, pe_passed)
                else:
                    pe.wait_ge(s["wo_read"], t + 1)
                transposes(x5, s["x5t_mm"])
                pe.wait_ge(s["w_ready"], t + 1)
                for n in range(TL):
                    m = pe.transpose(bk(6 + n // 4)[:, P * (n % 4):P * (n % 4 + 1)], w[:, n:n + 1].broadcast_to([P, P]),
                                     ident[:])
                m.then_inc(s["wt_mm"], 1)
            if f is not None:
                pe.wait_ge(s["q_c"], f + 1)
                pe.wait_ge(s["k_c"], f + 1)
                for n in range(2 * TL):
                    for hd in range(HEADS):
                        r = slice(HP * hd, HP * (hd + 1))
                        m = mm(bk(2 + hd)[S * (n % 2):S * (n % 2) + S, S * (n // 2):S * (n // 2) + S],
                               q[r, S * n:S * (n + 1)], k[r, S * n:S * (n + 1)], start=True, stop=True)
                m.then_inc(s["score_mm"], 1)
            if t is not None:
                pe.wait_ge(s["x5t_c"], t + 1)
                for c in range(2):
                    if c:
                        pe.wait_ge(s["wt_read"], t + 1)
                    for n in range(2):
                        m = mm(bk(6 * c + n), w1[:, P * n:P * (n + 1)], x5_t[:, CH * c:CH * (c + 1)],
                               start=True, stop=True)
                    m.then_inc(s["hid_mm"], 1)
                pe.wait_ge(s["hid_c"], t * 2 + 2)
                for n in range(TL):
                    for c in range(2):
                        m = mm(bk(7)[:, D * n:D * (n + 1)], hid[:, n // 4, c, P * (n % 4):P * (n % 4 + 1)], w2[:, c, :],
                               start=(c == 0), stop=(c == 1))
                m.then_inc(s["y2_mm"], 1)

        rounds(None, 0)
        with pe.Fori(1, ROUNDS) as o:
            rounds(o - 1, o)
        rounds(ROUNDS - 1, None)

    def per_token(v, width=D):
        return v.rearrange("p (n a) -> p n a", a=1).broadcast_to([P, TL, width])

    def per_feature(v):
        return v.rearrange("p (a d) -> p a d", a=1).broadcast_to([P, TL, v.shape[-1]])

    @block.vector
    def _(dve):
        v = nc.vector
        v.memset(x_t[D:D + 1, :], 1.0).then_inc(ones_set, 1)
        dve.wait_ge(s2_in, NSET * 16)
        v.tensor_tensor(w_p[:, 0:2, D], w_p[:, 0:2, D], bias_uv[:], ALU.add).then_inc(s2_v, 1)
        dve.wait_ge(s2_mm, 1)
        v.tensor_copy(w_t[:, 0:4, :].rearrange("p a b -> p (a b)"), bk(0)[0:D + 1, :])
        v.tensor_copy(w_t[:, 4, :], bk(1)[0:D + 1, 0:P]).then_inc(s2_v, 1)
        v.tensor_copy(wo_t[:], bk(2)[:, 0:D]).then_inc(s2_v, 1)
        dve.wait_ge(s2_mm, 2)
        v.tensor_copy(pos_t[:], bk(3)[:, 0:2 * S - 1]).then_inc(s2_v, 1)
        dve.wait_ge(s2_v, 4)
        v.tensor_tensor(pos_bd[:], pos_t[:].rearrange("p (a d) -> p a d", a=1).broadcast_to([P, HEADS, 2 * S - 1]),
                        blk[:].rearrange("p (a d) -> p a d", d=1).broadcast_to([P, HEADS, 2 * S - 1]), ALU.mult
                        ).then_inc(s2_v, 1)
        dve.wait_ge(s2_v, 5)

        class Chain:
            def __init__(self, semaphore, base, steps):
                self.semaphore, self.base, self.n = semaphore, base * steps, 0

            def __call__(self, ins):
                self.n += 1
                ins.then_inc(self.semaphore, 1)
                dve.wait_ge(self.semaphore, self.base + self.n)

        def normalise(link, dst, src, var_ready, rs_ready, nth):
            total, var, est, u = (ln_s[:, n, :] for n in range(4))
            link(v.reduce_sum(total, src, AX_X))
            link(v.scalar_tensor_tensor(out=dst, in0=per_token(total), scalar=-1.0 / D, in1=src, op0=ALU.mult,
                                        op1=ALU.add))
            link(v.tensor_tensor(tmp[:], dst, dst, ALU.mult))
            link(v.reduce_sum(total, tmp[:], AX_X))
            v.tensor_scalar(var, total, 1.0 / D, EPS, ALU.mult, ALU.add).then_inc(var_ready, 1)
            dve.wait_ge(rs_ready, nth)
            link(v.tensor_tensor(u, var, est, ALU.mult))
            link(v.scalar_tensor_tensor(out=u, in0=u, scalar=-0.5, in1=est, op0=ALU.mult, op1=ALU.mult))
            link(v.scalar_tensor_tensor(out=est, in0=u, scalar=1.5, in1=est, op0=ALU.add, op1=ALU.mult))
            return v.tensor_tensor(dst, dst, per_token(est), ALU.mult)

        def inputs(link, o, raw, x):
            link(normalise(link, x[:], raw[:], a_var, a_rs, o * 2 + 1))
            link(normalise(link, x[:], x[:], a_var, a_rs, o * 2 + 2))
            link(v.tensor_tensor(x[:], x[:], per_feature(rows[:, 0, :]), ALU.mult))
            v.tensor_tensor(x[:], x[:], per_feature(rows[:, 1, :]), ALU.add).then_inc(a_x, 1)

        STEPS_A = 17
        with dve.Fori(0, ROUNDS // 2) as oo:
            for u in range(2):
                o = oo * 2 + u
                link = Chain(s["seq_a"], o, STEPS_A)
                dve.wait_ge(a_in[u], oo * 16 + 16)
                dve.wait_ge(a_xt, o + 1)
                inputs(link, o, *buffers[u])
                assert link.n == STEPS_A
        dve.wait_ge(a_x, ROUNDS)
        for c in range(0, S // 2, 2):
            n = c // 4
            if n >= 2 and c % 4 == 0:
                dve.wait_ge(p_out[n % 2], 16 * (n // 2))
            dve.wait_ge(p_mm, c + 1)
            v.tensor_copy(pos_s[:, n % 2, 2 * (c % 4):2 * (c % 4) + 2, :].rearrange("p a b -> p (a b)"), bk(c % 8)
                          ).then_inc(p_v, 1)
        dve.sem_inc(s["out_st"], 1)
        att_v = att[:].rearrange("p h n t -> p (h n) t")
        top = stat[:, 0, :, :].rearrange("p h n -> p (h n)")
        total = stat[:, 1, :, :].rearrange("p h n -> p (h n)")

        def per_row(x):
            return x.rearrange("p (n a) -> p n a", a=1).broadcast_to([P, HEADS * TL, S])

        STEPS_T, STEPS_F = 19, 7

        def rounds(t, f):
            tail = Chain(s["seq_t"], t, STEPS_T) if t is not None else None
            link = Chain(s["seq_f"], f, STEPS_F) if f is not None else None
            if tail:
                dve.wait_ge(s["tok_in"], t * 16 + 16)
                v.tensor_tensor(h4[:], ht[:], per_feature(rows[:, 2, :]), ALU.add).then_inc(s["h4_ready"], 1)
                dve.wait_ge(s["at_mm1"], t + 1)
                v.tensor_copy(att_t[:, 4:6, :, :].rearrange("p a h t -> p (a h t)").rearrange("p (a b) -> p a b", a=2),
                              bank[1][0:S, :, :])
                v.tensor_copy(att_t[:, 6:8, :, :].rearrange("p a h t -> p (a h t)").rearrange("p (a b) -> p a b", a=2),
                              bank[2][0:S, :, :]).then_inc(s["at_c1"], 1)
                dve.wait_ge(s["h4_ready"], t + 1)
                dve.wait_ge(s["wo_mm"], t + 1)
                v.tensor_tensor(h4[:].rearrange("p n d -> p (n d)"), bk(6), h4[:].rearrange("p n d -> p (n d)"), ALU.add
                                ).then_inc(s["wo_read"], 1)
                dve.wait_ge(s["wo_read"], t + 1)
                normalise(tail, x5[:], h4[:], s["b_var"], s["b_rs"], t + 1).then_inc(s["x5_ready"], 1)
                dve.wait_ge(s["x5_ready"], t + 1)
                tail(v.tensor_tensor(tmp[:], x5[:], per_feature(rows[:, 3, :]), ALU.mult))
                tail(v.reduce_sum(w[:], tmp[:], AX_X))
                v.tensor_scalar(w[:], w[:], br[:, 0:1], None, ALU.add).then_inc(s["w_ready"], 1)
            if link:
                dve.wait_ge(s["qk_mm"], f + 1)
                v.tensor_copy(k[:].rearrange("p (a b) -> p a b", a=2), bank[2][:, :, :]).then_inc(s["k_c"], 1)
            if tail:
                tail(v.tensor_tensor(h4[:], h4[:], x5[:], ALU.add))
                dve.wait_ge(s["w_ready"], t + 1)
                dve.wait_ge(s["wt_mm"], t + 1)
                for i in range(2):
                    r = slice(S * i, S * (i + 1))
                    others = bank[3][r, :, :].rearrange("p a b -> p (a b)").rearrange("p (n c j) -> p n c j", c=2, j=S)[:, :, i, :]
                    own = w[r, :].rearrange("p (n a) -> p n a", a=1).broadcast_to([S, TL, S])
                    tail(v.tensor_tensor(above[r, :, :], others, own, ALU.is_gt))
                    m = v.tensor_tensor(same[r, :, :], others, own, ALU.is_equal)
                    if i == 0:
                        tail(m)
                m.then_inc(s["wt_read"], 1)
                dve.wait_ge(s["wt_read"], t + 1)
            if link:
                dve.wait_ge(s["score_mm"], f + 1)
                dve.wait_ge(s["pos_ld"], f * 16 + 16)
                for hd in range(HEADS):
                    link(v.tensor_tensor(att[:, hd, :, :], bk(2 + hd).rearrange("p (n t) -> p n t", t=S),
                                         pos_in[:, :, S * hd:S * (hd + 1)], ALU.add))
                link(v.tensor_reduce(top, att_v, AX_X, ALU.max))
                v.tensor_tensor(att_v, att_v, per_row(top), ALU.subtract).then_inc(s["shifted"], 1)
            if tail:
                tail(v.tensor_tensor(same[:], same[:], per_feature(before[:]), ALU.mult))
                tail(v.tensor_tensor(above[:], above[:], same[:], ALU.add))
                tail(v.reduce_sum(coef[:], above[:], AX_X))
                tail(v.scalar_tensor_tensor(out=coef[:], in0=coef[:], scalar=KEPT - 0.5, in1=w[:], op0=ALU.is_lt,
                                            op1=ALU.mult))
            if link:
                dve.wait_ge(s["exp_c"], f + 1)
                link(v.reduce_sum(total, att_v, AX_X))
                link(v.reciprocal(top, total))
                v.tensor_tensor(att_v, att_v, per_row(top), ALU.mult).then_inc(s["att_n"], 1)
                assert link.n == STEPS_F
            if tail:
                dve.wait_ge(s["y2_mm"], t + 1)
                tail(v.tensor_tensor(tmp[:], bk(7).rearrange("p (n d) -> p n d", d=D), per_feature(rows[:, 4, :]), ALU.add))
                tail(v.tensor_tensor(tmp[:], tmp[:], per_token(coef[:]), ALU.mult))
                dve.wait_ge(s["out_st"], t * 16 + 1)
                v.tensor_tensor(xa[:], tmp[:], h4[:], ALU.add).then_inc(s["res"], 1)
                dve.wait_ge(s["res"], t + 1)
                assert tail.n == STEPS_T, tail.n

        rounds(None, 0)
        with dve.Fori(1, ROUNDS) as o:
            rounds(o - 1, o)
        rounds(ROUNDS - 1, None)

    @block.scalar
    def _(act):
        f = nc.scalar
        act.wait_ge(s2_v, 5)

        def copy(dst, src):
            return f.activation(dst, src, ACT.Copy)

        def estimate(var_ready, rs_ready, nth):
            act.wait_ge(var_ready, nth)
            f.activation(ln_s[:, 2, :], ln_s[:, 1, :], ACT.Abs_reciprocal_sqrt).then_inc(rs_ready, 1)

        def turned(o):
            act.wait_ge(a_xt, o + 3)
            copy(x_t[0:D, :].rearrange("p (a b) -> p a b", a=2), bank[0][0:D, :, :])
            copy(xn_t[:, bass.ds(o * RT, RT)].rearrange("p (a b) -> p a b", a=2), bank[0][0:D, :, :]).then_inc(a_xtc, 1)

        def queries(o):
            act.wait_ge(a_q, o + 1)
            copy(qv[:, bass.ds(o * 2 * TL, 2 * TL), :].rearrange("p i t -> p (i t)").rearrange("p (a b) -> p a b", a=2),
                 bank[1][:, :, :]).then_inc(a_qc, 1)

        estimate(a_var, a_rs, 1)
        estimate(a_var, a_rs, 2)
        with act.Fori(1, ROUNDS) as o:
            estimate(a_var, a_rs, o * 2 + 1)
            turned(o - 1)
            estimate(a_var, a_rs, o * 2 + 2)
            queries(o - 1)
        turned(ROUNDS - 1)
        queries(ROUNDS - 1)
        for c in range(1, S // 2, 2):
            n = c // 4
            if n >= 2 and c % 4 == 1:
                act.wait_ge(p_out[n % 2], 16 * (n // 2))
            act.wait_ge(p_mm, c + 1)
            copy(pos_s[:, n % 2, 2 * (c % 4):2 * (c % 4) + 2, :].rearrange("p a b -> p (a b)"), bk(c % 8)
                 ).then_inc(p_a, 1)
        act.wait_ge(a_xtc, ROUNDS)
        def rounds(t, f):
            if f is not None:
                copy(x_t[0:D, :], xn_t[:, bass.ds(f * RT, RT)]).then_inc(s["xt_c"], 1)
            if t is not None:
                act.wait_ge(s["at_mm0"], t + 1)
                copy(att_t[:, 0:2, :, :].rearrange("p a h t -> p (a h t)").rearrange("p (a b) -> p a b", a=2),
                     bank[3][0:S, :, :])
                copy(att_t[:, 2:4, :, :].rearrange("p a h t -> p (a h t)").rearrange("p (a b) -> p a b", a=2),
                     bank[0][0:S, :, :]).then_inc(s["at_c0"], 1)
                act.wait_ge(s["ctx_mm"], t + 1)
                copy(ctx_t[:].rearrange("p (a b) -> p a b", a=2), bank[0][:, :, :]).then_inc(s["ctx_c"], 1)
                estimate(s["b_var"], s["b_rs"], t + 1)
            if f is not None:
                act.wait_ge(s["qk_mm"], f + 1)
                copy(q[:].rearrange("p (a b) -> p a b", a=2), bank[1][:, :, :]).then_inc(s["q_c"], 1)
                act.wait_ge(s["val_mm"], f + 1)
                copy(val[:, 0:8, :].rearrange("p a b -> p (a b)").rearrange("p (a b) -> p a b", a=2), bank[3][0:S, :, :])
                copy(val[:, 8:16, :].rearrange("p a b -> p (a b)").rearrange("p (a b) -> p a b", a=2), bank[0][0:S, :, :]
                     ).then_inc(s["val_c"], 1)
            if t is not None:
                act.wait_ge(s["x5t_mm"], t + 1)
                copy(x5_t[:].rearrange("p (a b) -> p a b", a=2), bank[0][0:D, :, :]).then_inc(s["x5t_c"], 1)
                for c in range(2):
                    act.wait_ge(s["hid_mm"], t * 2 + c + 1)
                    for n in range(2):
                        m = nc.scalar.activation(hid[:, c, n, :], bk(6 * c + n), ACT.Gelu_apprx_tanh, bias=fb1[:, n:n + 1])
                    m.then_inc(s["hid_c"], 1)
            if f is not None:
                act.wait_ge(s["shifted"], f + 1)
                av = att[:].rearrange("p h n t -> p (h n t)")
                nc.scalar.activation(av, av, ACT.Exp, scale=float(HD) ** -0.5).then_inc(s["exp_c"], 1)

        rounds(None, 0)
        with act.Fori(1, ROUNDS) as o:
            rounds(o - 1, o)
        rounds(ROUNDS - 1, None)


def vision_tower(nc, a, out):
    tokens = nc.dram_tensor("tokens", (NIMG, PIX), F32, kind="Internal").ap()
    a["scr_x"] = nc.dram_tensor("scr_x", (BI, C, XM), F32, kind="Internal").ap()
    a["scr_y"] = nc.dram_tensor("scr_y", (2 * Q, 2, BI, C, MODES // Q), F32, kind="Internal").ap()
    a["scr_w"] = nc.dram_tensor("scr_w", (2, LAYERS, C, C, MODES), F32, kind="Internal").ap()
    a["scr_p"] = nc.dram_tensor("scr_p", (NIMG, S, HEADS * S), F32, kind="Internal").ap()
    with ExitStack() as ctx:
        tokenizer(nc, ctx, a, tokens, NIMG // BI)
    with ExitStack() as ctx:
        attention_and_ffn(nc, ctx, a, tokens, out)


def kernel(**inputs):
    import concourse.bacc as bacc
    from concourse.bass_utils import run_bass_kernel_spmd

    nc = bacc.Bacc("TRN2", target_bir_lowering=False, num_devices=1, dynamic_dma_scratch_size=256)
    arrays, aps = {}, {}
    given = {n: np.ascontiguousarray(v) for n, v in inputs.items()}
    for name, array in {**given, **layouts(given), **constants(), **attention_layouts(given), **attention_constants()}.items():
        arrays[f"in_{name}"] = array
        aps[name] = nc.dram_tensor(f"in_{name}", array.shape, mybir.dt.from_np(array.dtype), kind="ExternalInput").ap()
    out = nc.dram_tensor("out_0", (NIMG, S, S), F32, kind="ExternalOutput").ap()
    vision_tower(nc, aps, out)
    r = run_bass_kernel_spmd(nc, [arrays], core_ids=[0])
    return r.results[0]["out_0"]
```
